# Optimizing a Trainium2 kernel written in Bass

```python
import numpy as np
import jax
import jax.numpy as jnp

def _softmax(x, axis=-1):
    return jax.nn.softmax(x, axis=axis)

def _gelu(x):
    return jax.nn.gelu(x, approximate=True)

def _silu(x):
    return jax.nn.silu(x)

def _sigmoid(x):
    return jax.nn.sigmoid(x)

def _layernorm(x, axis=-1, eps=1e-05):
    m = jnp.mean(x, axis=axis, keepdims=True)
    v = jnp.var(x, axis=axis, keepdims=True)
    return (x - m) / jnp.sqrt(v + eps)

def _scatter_add(tgt, idx, src, axis=0):
    return tgt.at[idx].add(src)

def _segment_sum(src, seg, n):
    return jax.ops.segment_sum(src, seg, n)
kernel_name = 'mk_gnn_ffn_d1_gnn_r32_de2da1'

def setup_inputs(seed: int=0):
    np.random.seed(seed)
    _w = jnp.asarray

    def _rec_inputs():
        import jax
        import jax.numpy as jnp
        _gk = jax.random.key(seed)
        x = -0.0003713 + 1 * jax.random.normal(jax.random.fold_in(_gk, 1), (3125, 256), jnp.float32)
        _s = jax.random.randint(jax.random.fold_in(_gk, 2), (25000,), 0, 3125, jnp.int32)
        _d = jax.random.randint(jax.random.fold_in(_gk, 3), (25000,), 0, 3125, jnp.int32)
        _loop = jnp.arange(3125, dtype=jnp.int32)
        src = jnp.concatenate([_s, _d, _loop])
        dst = jnp.concatenate([_d, _s, _loop])
        _o = jnp.argsort(dst, stable=True)
        src = src[_o]
        dst = dst[_o]
        return (x, src, dst)
    x, src, dst = _rec_inputs()

    def _L0_gnn_setup():
        import jax, jax.numpy as jnp
        import numpy as np
        N_NODES = 50000
        N_EDGES = 25000
        D_IN = 256
        D_HID = 256
        D_OUT = 256
        EPS = 1e-12

        def _sage_conv(x, src, dst, W_proj, b_proj, W_l, b_l, W_r):
            n = x.shape[0]
            xp = jax.nn.relu(x @ W_proj + b_proj)
            msg_sum = jax.ops.segment_sum(xp[src], dst, num_segments=n)
            cnt = jax.ops.segment_sum(jnp.ones_like(dst, dtype=x.dtype), dst, num_segments=n)
            aggr = msg_sum / jnp.maximum(cnt, 1.0)[:, None]
            out = aggr @ W_l + b_l + x @ W_r
            norm = jnp.linalg.norm(out, axis=-1, keepdims=True)
            return out / jnp.maximum(norm, EPS)
        key = jax.random.key(seed)
        ks = jax.random.split(key, 12)
        s = 1.0 / np.sqrt(D_IN)
        sh = 1.0 / np.sqrt(D_HID)
        inp = {'node_emb': jax.random.normal(ks[0], (N_NODES, D_IN), dtype=jnp.float32), 'edge_index': jax.random.randint(ks[1], (2, N_EDGES), 0, N_NODES, dtype=jnp.int64), 'W_proj1': jax.random.uniform(ks[2], (D_IN, D_IN), jnp.float32, -s, s), 'b_proj1': jax.random.uniform(ks[3], (D_IN,), jnp.float32, -s, s), 'W_l1': jax.random.uniform(ks[4], (D_IN, D_HID), jnp.float32, -s, s), 'b_l1': jax.random.uniform(ks[5], (D_HID,), jnp.float32, -s, s), 'W_r1': jax.random.uniform(ks[6], (D_IN, D_HID), jnp.float32, -s, s), 'W_proj2': jax.random.uniform(ks[7], (D_HID, D_HID), jnp.float32, -sh, sh), 'b_proj2': jax.random.uniform(ks[8], (D_HID,), jnp.float32, -sh, sh), 'W_l2': jax.random.uniform(ks[9], (D_HID, D_OUT), jnp.float32, -sh, sh), 'b_l2': jax.random.uniform(ks[10], (D_OUT,), jnp.float32, -sh, sh), 'W_r2': jax.random.uniform(ks[11], (D_HID, D_OUT), jnp.float32, -sh, sh)}
        return inp
    _L0_gnn_all = _L0_gnn_setup()
    _L0_gnn_in = {k: v for k, v in _L0_gnn_all.items() if k in ('W_proj1', 'b_proj1', 'W_l1', 'b_l1', 'W_r1', 'W_proj2', 'b_proj2', 'W_l2', 'b_l2', 'W_r2')}
    del _L0_gnn_all

    def _L0_ffn_setup():
        import jax, jax.numpy as jnp
        import numpy as np
        DIM = 256
        H = 8
        D = 64
        G = 64
        INNER = H * D
        SCALE = D ** (-0.5)
        key = jax.random.key(seed)
        ks = jax.random.split(key, 12)
        B, N = (4, 512)
        x = jax.random.normal(ks[0], (B, N, DIM), dtype=jnp.float32)
        s = lambda fan_in: 1.0 / np.sqrt(fan_in)
        W_fx = jax.random.normal(ks[1], (DIM, INNER), dtype=jnp.float32) * s(DIM)
        b_fx = jnp.zeros((INNER,), dtype=jnp.float32)
        W_x = jax.random.normal(ks[2], (DIM, INNER), dtype=jnp.float32) * s(DIM)
        b_x = jnp.zeros((INNER,), dtype=jnp.float32)
        A = jax.random.normal(ks[3], (G, D), dtype=jnp.float32)
        Q, _ = jnp.linalg.qr(A.T)
        W_slice = Q[:, :G].astype(jnp.float32)
        b_slice = jnp.zeros((G,), dtype=jnp.float32)
        W_q = jax.random.normal(ks[4], (D, D), dtype=jnp.float32) * s(D)
        W_k = jax.random.normal(ks[5], (D, D), dtype=jnp.float32) * s(D)
        W_v = jax.random.normal(ks[6], (D, D), dtype=jnp.float32) * s(D)
        W_out = jax.random.normal(ks[7], (INNER, DIM), dtype=jnp.float32) * s(INNER)
        b_out = jnp.zeros((DIM,), dtype=jnp.float32)
        temperature = jnp.ones((1, H, 1, 1), dtype=jnp.float32) * 0.5
        return {'x': x, 'W_fx': W_fx, 'b_fx': b_fx, 'W_x': W_x, 'b_x': b_x, 'W_slice': W_slice, 'b_slice': b_slice, 'W_q': W_q, 'W_k': W_k, 'W_v': W_v, 'W_out': W_out, 'b_out': b_out, 'temperature': temperature}
    _L0_ffn_all = _L0_ffn_setup()
    _L0_ffn_in = {k: v for k, v in _L0_ffn_all.items() if k in ('W_fx', 'b_fx', 'W_x', 'b_x', 'W_slice', 'b_slice', 'W_q', 'W_k', 'W_v', 'W_out', 'b_out', 'temperature')}
    del _L0_ffn_all
    return {'x': x, 'src': src, 'dst': dst, 'L0_gnn_W_proj1': _L0_gnn_in['W_proj1'], 'L0_gnn_b_proj1': _L0_gnn_in['b_proj1'], 'L0_gnn_W_l1': _L0_gnn_in['W_l1'], 'L0_gnn_b_l1': _L0_gnn_in['b_l1'], 'L0_gnn_W_r1': _L0_gnn_in['W_r1'], 'L0_gnn_W_proj2': _L0_gnn_in['W_proj2'], 'L0_gnn_b_proj2': _L0_gnn_in['b_proj2'], 'L0_gnn_W_l2': _L0_gnn_in['W_l2'], 'L0_gnn_b_l2': _L0_gnn_in['b_l2'], 'L0_gnn_W_r2': _L0_gnn_in['W_r2'], 'L0_ffn_W_fx': _L0_ffn_in['W_fx'], 'L0_ffn_b_fx': _L0_ffn_in['b_fx'], 'L0_ffn_W_x': _L0_ffn_in['W_x'], 'L0_ffn_b_x': _L0_ffn_in['b_x'], 'L0_ffn_W_slice': _L0_ffn_in['W_slice'], 'L0_ffn_b_slice': _L0_ffn_in['b_slice'], 'L0_ffn_W_q': _L0_ffn_in['W_q'], 'L0_ffn_W_k': _L0_ffn_in['W_k'], 'L0_ffn_W_v': _L0_ffn_in['W_v'], 'L0_ffn_W_out': _L0_ffn_in['W_out'], 'L0_ffn_b_out': _L0_ffn_in['b_out'], 'L0_ffn_temperature': _L0_ffn_in['temperature']}

def reference(x, src, dst, L0_gnn_W_proj1, L0_gnn_b_proj1, L0_gnn_W_l1, L0_gnn_b_l1, L0_gnn_W_r1, L0_gnn_W_proj2, L0_gnn_b_proj2, L0_gnn_W_l2, L0_gnn_b_l2, L0_gnn_W_r2, L0_ffn_W_fx, L0_ffn_b_fx, L0_ffn_W_x, L0_ffn_b_x, L0_ffn_W_slice, L0_ffn_b_slice, L0_ffn_W_q, L0_ffn_W_k, L0_ffn_W_v, L0_ffn_W_out, L0_ffn_b_out, L0_ffn_temperature):
    import jax
    import jax.numpy as jnp

    def _L0_gnn_ref(node_emb, edge_index, W_proj1, b_proj1, W_l1, b_l1, W_r1, W_proj2, b_proj2, W_l2, b_l2, W_r2):
        import jax, jax.numpy as jnp
        import numpy as np
        N_NODES = 50000
        N_EDGES = 25000
        D_IN = 256
        D_HID = 256
        D_OUT = 256
        EPS = 1e-12

        def _sage_conv(x, src, dst, W_proj, b_proj, W_l, b_l, W_r):
            n = x.shape[0]
            xp = jax.nn.relu(x @ W_proj + b_proj)
            msg_sum = jax.ops.segment_sum(xp[src], dst, num_segments=n)
            cnt = jax.ops.segment_sum(jnp.ones_like(dst, dtype=x.dtype), dst, num_segments=n)
            aggr = msg_sum / jnp.maximum(cnt, 1.0)[:, None]
            out = aggr @ W_l + b_l + x @ W_r
            norm = jnp.linalg.norm(out, axis=-1, keepdims=True)
            return out / jnp.maximum(norm, EPS)
        src, dst = (edge_index[0], edge_index[1])
        h = _sage_conv(node_emb, src, dst, W_proj1, b_proj1, W_l1, b_l1, W_r1)
        h = jax.nn.relu(h)
        out = _sage_conv(h, src, dst, W_proj2, b_proj2, W_l2, b_l2, W_r2)
        return out

    def _L0_ffn_ref(x, W_fx, b_fx, W_x, b_x, W_slice, b_slice, W_q, W_k, W_v, W_out, b_out, temperature):
        import jax, jax.numpy as jnp
        import numpy as np
        DIM = 256
        H = 8
        D = 64
        G = 64
        INNER = H * D
        SCALE = D ** (-0.5)
        B, N, _ = x.shape
        fx_mid = (x @ W_fx + b_fx).reshape(B, N, H, D).transpose(0, 2, 1, 3)
        x_mid = (x @ W_x + b_x).reshape(B, N, H, D).transpose(0, 2, 1, 3)
        temp = jnp.clip(temperature, 0.1, 5.0)
        slice_weights = jax.nn.softmax((x_mid @ W_slice + b_slice) / temp, axis=-1)
        slice_norm = slice_weights.sum(axis=2)
        slice_token = jnp.einsum('bhnc,bhng->bhgc', fx_mid, slice_weights)
        slice_token = slice_token / (slice_norm[..., None] + 1e-05)
        q = slice_token @ W_q
        k = slice_token @ W_k
        v = slice_token @ W_v
        attn = jax.nn.softmax(jnp.einsum('bhgc,bhkc->bhgk', q, k) * SCALE, axis=-1)
        out_slice = jnp.einsum('bhgk,bhkc->bhgc', attn, v)
        out_x = jnp.einsum('bhgc,bhng->bhnc', out_slice, slice_weights)
        out_x = out_x.transpose(0, 2, 1, 3).reshape(B, N, INNER)
        return out_x @ W_out + b_out
    edge_index = jnp.stack([src, dst])
    x = x + _L0_gnn_ref(_layernorm(x, axis=-1), edge_index, L0_gnn_W_proj1, L0_gnn_b_proj1, L0_gnn_W_l1, L0_gnn_b_l1, L0_gnn_W_r1, L0_gnn_W_proj2, L0_gnn_b_proj2, L0_gnn_W_l2, L0_gnn_b_l2, L0_gnn_W_r2)
    x = x + _L0_ffn_ref(_layernorm(x, axis=-1)[None], L0_ffn_W_fx, L0_ffn_b_fx, L0_ffn_W_x, L0_ffn_b_x, L0_ffn_W_slice, L0_ffn_b_slice, L0_ffn_W_q, L0_ffn_W_k, L0_ffn_W_v, L0_ffn_W_out, L0_ffn_b_out, L0_ffn_temperature)[0]
    return x

_drawn_inputs = setup_inputs


def setup_inputs(seed=0):
    import zlib

    import numpy as np

    out = dict(_drawn_inputs(seed))
    spreads = {'L0_ffn_b_fx': (0.0, 0.1),
     'L0_ffn_b_x': (0.0, 0.8),
     'L0_ffn_b_slice': (0.0, 0.8),
     'L0_ffn_b_out': (0.0, 0.1),
     'L0_ffn_temperature': (0.5, 0.6)}
    factors = {'L0_gnn_W_proj1': 8.0,
     'L0_gnn_b_proj1': 30.955,
     'L0_gnn_W_l1': 5.762,
     'L0_gnn_b_l1': 59.761,
     'L0_gnn_W_proj2': 5.268,
     'L0_ffn_W_x': 8.0,
     'L0_ffn_W_slice': 8.0,
     'L0_ffn_W_q': 8.0,
     'L0_ffn_W_k': 8.0,
     'L0_gnn_W_r1': 7.456}
    for name, (base, spread) in spreads.items():
        noise = np.random.default_rng([zlib.crc32(name.encode()), seed]).standard_normal(out[name].shape)
        drawn = base * np.exp(spread * noise) if base else spread * noise
        out[name] = jnp.asarray(drawn.astype(out[name].dtype))
    for name, factor in factors.items():
        out[name] = (out[name] * factor).astype(out[name].dtype)
    return out
```

```python
from contextlib import ExitStack

import concourse.bass as bass
from concourse import mybir

ALU = mybir.AluOpType
ACT = mybir.ActivationFunctionType
AX_X = mybir.AxisListType.X
F32 = mybir.dt.float32
F16 = mybir.dt.float16
I32 = mybir.dt.int32
U32 = mybir.dt.uint32

P = 128
C = 256
KC = C // P


class Chain:

    def __init__(self, eng, sem):
        self.eng, self.sem, self.n, self.done = eng, sem, 0, 0

    def link(self, ins):
        ins.then_inc(self.sem, 1)
        self.n += 1
        self.eng.wait_ge(self.sem, self.done + self.n)

    def loop(self, passes, per):
        self.done = passes * per
        self.start, self.per = self.n, per

    def end(self, passes):
        assert self.n == self.start + self.per, (self.n - self.start, self.per)
        self.n, self.done = self.start + passes * self.per, 0


def bass_gnn_ffn_kernel(nc, x, src, dst, Wp1, bp1, Wl1, bl1, Wr1, Wp2, bp2, Wl2, bl2, Wr2,
                        W_fx, b_fx, W_xT, b_xT, W_slice, b_slice, W_q, W_k, W_v, W_out, b_out,
                        temperature, out):
    N = x.shape[0]
    E = src.shape[0]
    TN = 125
    T = N // TN
    D5 = 5
    Q = N // D5
    WIN = P
    COARSE = 512
    ROW = E // TN
    KEYS = T * D5
    CT = 4
    CN = CT * TN
    CH = T // CT
    H, G = temperature.shape[1], W_slice.shape[1]
    D = W_slice.shape[0]
    INNER = H * D
    EPS_LN, EPS_NORM, EPS_SLICE = 1e-5, 1e-12, 1e-5
    SCALE = D ** -0.5
    assert T * TN == N and Q * D5 == N and ROW * TN == E and CH * CT + 1 == T and TN == 5 * T
    assert C == 2 * P and H * G == 4 * P and D == 64 and G == 64

    SUB, PASS = 8, 3
    PASSES = Q // (SUB * PASS)
    HALF = SUB // 2
    BANKS = PASSES * PASS * 2 + 1
    assert PASSES == T + 1 and PASSES * PASS * SUB + 1 == Q
    HG = H * G
    PAIRS = HG // P
    R = 4
    RG = 5
    ROUNDS = ROW // RG
    assert ROUNDS * RG == ROW and E % N == 0
    g_xp_dram = nc.dram_tensor("g_xp_scratch", (N, 2 * C), F16, kind="Internal").ap()
    wxs_dram = nc.dram_tensor("wxs_scratch", (P, KC, HG), F32, kind="Internal").ap()
    bxs_dram = nc.dram_tensor("bxs_scratch", (1, HG), F32, kind="Internal").ap()
    xr_dram = nc.dram_tensor("xr_scratch", (T, TN, C), F32, kind="Internal").ap()
    xp_dram = nc.dram_tensor("xp_scratch", (N, 2 * C), F16, kind="Internal").ap()
    x1_dram = nc.dram_tensor("x1_scratch", (T, TN, C), F32, kind="Internal").ap()
    cnt_dram = nc.dram_tensor("cnt_scratch", (N,), F32, kind="Internal").ap()
    x_t = x.rearrange("(t p) c -> t p c", p=TN)
    out_t = out.rearrange("(t p) c -> t p c", p=TN)
    xp_t = xp_dram.rearrange("(t p) c -> t p c", p=TN)

    with ExitStack() as ctx:
        def sb(name, shape, dt=F32):
            return ctx.enter_context(nc.sbuf_tensor(name, shape, dt))

        def sem(name):
            return ctx.enter_context(nc.semaphore(name))

        adj = sb("adj", [P, T, N + 1], F16)
        adj_words = T * (N + 1) // 2
        xp = sb("xp", [P, T, 2 * C], F16)
        ps = ctx.enter_context(nc.psum_tensor("ps", [P, 8, 512], F32))
        ident = sb("ident", [P, P])
        ones = sb("ones", [P, P])
        wp = sb("wp", [P, KC, C])
        wr = sb("wr", [P, KC, C])
        wl = sb("wl", [P, KC, C])
        bias_p = sb("bias_p", [1, C])
        bias_r = sb("bias_r", [1, C])
        rcnt = sb("rcnt", [P, T])
        covered = sb("covered", [1, 2], I32)
        stats2 = sb("stats2", [P, T, 6])
        key_t = sb("key_t", [P, Q + 1], F16)
        low_t = sb("low_t", [P, Q + 1], F16)
        work_words = 4586
        work = sb("work", [P, work_words])

        class Region:

            def __init__(self, base, limit):
                self.base, self.at, self.limit = base, 0, limit

            def take(self, shape, dt=F32):
                n = 1
                for s in shape[1:]:
                    n *= s
                words = n if dt in (F32, I32) else (n + 1) // 2
                words = (words + 1) // 2 * 2
                assert self.at + words <= self.limit, (self.at + words, self.limit)
                v = self.base[:, self.at:self.at + words]
                self.at += words
                if dt != F32:
                    v = v.bitcast(dt)
                v = v[0:shape[0], 0:n]
                names = "abcd"[:len(shape) - 1]
                sizes = dict(zip(names[1:], shape[2:]))
                return v.rearrange(f"p ({' '.join(names)}) -> p {' '.join(names)}", **sizes) if len(shape) > 2 else v

        def over_adj():
            return Region(adj[:, :, :].rearrange("p a b -> p (a b)")[:, 0:2 * adj_words].bitcast(F32), adj_words)

        def over_work():
            return Region(work[:, :], work_words)

        r = over_adj()
        rows = r.take([TN, ROW], I32)
        thr = r.take([TN, TN])
        base5 = r.take([TN, 5])
        own = r.take([TN, T])
        rowmax = r.take([TN, 1])
        step = r.take([TN, TN])
        r0 = r.take([TN, 1])
        r0_i = r.take([TN, 1], I32)
        picked = r.take([TN, ROW], I32)
        picked_f = r.take([TN, ROW])
        junk = r.take([TN, COARSE])
        below = r.take([TN, 1])
        start = r.take([TN, 1])
        start_c = r.take([TN, 1])
        start_i = r.take([TN, 1], I32)
        coarse = r.take([TN, COARSE], I32)
        coarse_f = r.take([TN, COARSE])
        below5 = r.take([TN, 5])
        start5 = r.take([TN, 5])
        start5_i = r.take([TN, 5, 8], I32)
        win_d = r.take([TN, 5, WIN], I32)
        win_s = r.take([TN, 5, WIN], I32)
        hi_i = r.take([TN, 5, WIN], I32)
        low_f = r.take([TN, 5, WIN])
        win_f = r.take([TN, 5, WIN])
        dl = r.take([TN, 5, WIN])
        ge0 = r.take([TN, 5, WIN])
        valid = r.take([TN, 5, WIN])
        pair_f = r.take([TN, 5, WIN])
        key_f = r.take([TN, 5, WIN])
        junk2 = r.take([TN, WIN])
        cnt = r.take([TN, T])
        cnt_row = r.take([TN, 1])
        wxT = r.take([D, H, C])
        wsl = r.take([D, G])
        bxT = r.take([D, H])
        bsl = r.take([1, G])
        temp = r.take([1, H])
        rtemp = r.take([1, H])
        rtemp_row = r.take([1, H, G])
        rtemp_all = r.take([P, HG])
        wxs_o = r.take([P, KC, HG])
        bxs_t = r.take([1, H, G])
        bxs_o = r.take([1, H, G])

        r = over_work()
        iota_low = r.take([P, P, 2], F16)
        iota_key = r.take([P, KEYS, 2], F16)
        oh_low = r.take([P, PASS * HALF, P, 2], F16)
        oh_key = r.take([P, PASS * HALF, KEYS, 2], F16)
        x_in = r.take([TN, 2, C])
        xn = r.take([TN, C])
        xnT = r.take([P, KC, TN])
        xr_o = r.take([TN, C])
        st6 = r.take([TN, 6])
        mv = r.take([TN, 2])
        var = r.take([TN, 1])
        std = r.take([TN, 1])
        rstd = r.take([TN, 1])

        r = over_work()
        msgT = r.take([P, KC, CN])
        o_t = r.take([TN, CT, C])
        xr_in = r.take([TN, CT, C])
        ss = r.take([TN, CT])
        nrm = r.take([TN, CT])
        inv = r.take([TN, CT])
        mark = r.at
        hT = r.take([P, 2, KC, TN])
        xr_o2 = r.take([TN, 2, C])
        xp_o = r.take([TN, 2, 2 * C], F16)
        r.at = mark
        x_res = r.take([TN, CT, C])

        r = over_adj()
        g_src = r.take([TN, ROW + 1], I32)
        g_dst_i = r.take([TN, ROW], I32)
        g_dst = r.take([TN, ROW])
        g_rel = r.take([TN, ROW])
        g_iota = r.take([TN, CN], F16)
        g_idx = r.take([TN, RG, 2], I32)
        g_rows = r.take([TN, RG, 2 * C], F16)
        g_oh = r.take([TN, RG, CN], F16)
        g_all_i = r.take([TN, N], I32)
        g_all = r.take([TN, N])
        g_eq = r.take([TN, N])
        g_node = r.take([TN, T])
        g_part = r.take([TN, T])
        g_cnt = r.take([TN, T])

        r = over_adj()
        w_tr = r.take([P, PAIRS, N])
        f_in = r.take([TN, R, C])
        f_xn = r.take([TN, R, C + 8])
        f_xT = r.take([P, R, KC, TN])
        f_e = r.take([TN, R, HG])
        f_w = r.take([TN, R, HG])
        f_mx = r.take([TN, R, H])
        f_sm = r.take([TN, R, H])
        f_rs = r.take([TN, R, H])
        var2 = r.take([TN, T])
        mean2 = r.take([TN, T])
        half2 = r.take([TN, T])
        std2 = r.take([TN, T])
        rstd2 = r.take([TN, T])
        wxs = r.take([P, KC, HG])
        bxs = r.take([1, HG])
        wfx = r.take([P, KC, INNER])
        bfx = r.take([1, INNER])
        wq = r.take([D, D])
        wk = r.take([D, D])
        wv = r.take([D, D])
        wo = r.take([D, H, C])
        bo = r.take([1, C])
        sn_e = r.take([P, PAIRS])
        sn_inv = r.take([P, PAIRS])
        s_sb = r.take([P, PAIRS, C + 8])
        sT = r.take([P, KC, HG])
        nr = r.take([1, HG])
        tokT = r.take([D, HG])
        qT = r.take([D, HG])
        kT = r.take([D, HG])
        v_sb = r.take([G, HG])
        am = r.take([G, H])
        a_e = r.take([G, H, G])
        a_s = r.take([G, H])
        a_r = r.take([G, H])
        a_w = r.take([G, H, G])
        aT = r.take([G, HG])
        osT = r.take([D, HG])
        t_sb = r.take([P, PAIRS, C])
        w_st = r.take([P, 2, PAIRS, TN])
        y_in = r.take([TN, 2, C])
        y_o = r.take([TN, 2, C])
        assert PAIRS == 4

        consts, dve_consts = sem("consts"), sem("dve_consts")
        rows_in, weights_in, fold_in = sem("rows_in"), sem("weights_in"), sem("fold_in")
        step_ready, r0_done, r0_ready, row_in = sem("step_ready"), sem("r0_done"), sem("r0_ready"), sem("row_in")
        start_ready, coarse_in, fine_ready = sem("start_ready"), sem("coarse_in"), sem("fine_ready")
        win_in = [sem(f"win_in{i}") for i in range(5)]
        keys_ready, turned, tables_ready = sem("keys_ready"), sem("turned"), sem("tables_ready")
        rt_row, rt_done, rt_ready, fold_done, fold_ready, fold_stored = (sem(n) for n in (
            "rt_row", "rt_done", "rt_ready", "fold_done", "fold_ready", "fold_stored"))
        cnt_out, cnt_in = sem("cnt_out"), sem("cnt_in")
        cnt_rows_ready, total_done, covered_ready = sem("cnt_rows_ready"), sem("total_done"), sem("covered_ready")
        g_tables_in, g_xp_out, g_iota_ready, g_node_ready = (sem(n) for n in ("g_tables_in", "g_xp_out", "g_iota_ready", "g_node_ready"))
        g_dst_ready, g_all_in, g_all_used, g_steps = (sem(n) for n in ("g_dst_ready", "g_all_in", "g_all_used", "g_steps"))
        g_free, g_idx_ready, g_oh_ready, g_rel_ready = (sem(n) for n in ("g_free", "g_idx_ready", "g_oh_ready", "g_rel_ready"))
        g_in = [sem(f"g_in{j}") for j in range(RG)]
        oh_ready, built, stored = sem("oh_ready"), sem("built"), sem("adj_stored")
        x_loaded = [sem(f"x_loaded{i}") for i in range(2)]
        var_ready, std_ready, xn_ready, xt_done, xT_ready = (sem(n) for n in (
            "var_ready", "std_ready", "xn_ready", "xt_done", "xT_ready"))
        proj_done, hi_ready, lo_ready, xr_ready, xr_stored = (sem(n) for n in (
            "proj_done", "hi_ready", "lo_ready", "xr_ready", "xr_stored"))
        dve_steps, act_steps, pool_steps = sem("dve_steps"), sem("act_steps"), sem("pool_steps")
        agg_done = [[sem(f"agg_done{k}_{c}") for c in range(2)] for k in range(2)]
        msg_ready = [[sem(f"msg_ready{k}_{c}") for c in range(2)] for k in range(2)]
        wl_done, o_ready, sq_done, nrm_ready = ([sem(f"{n}{k}") for k in range(2)] for n in (
            "wl_done", "o_ready", "sq_done", "nrm_ready"))
        xr_loaded = [[sem(f"xr_loaded{k}_{j}") for j in range(CT)] for k in range(2)]
        res_loaded = [sem(f"res_loaded{j}") for j in range(CT)]
        h_ready, ht_done, hT_ready, proj2_done, hi2_ready, lo2_ready, xr2_ready = (sem(n) for n in (
            "h_ready", "ht_done", "hT_ready", "proj2_done", "hi2_ready", "lo2_ready", "xr2_ready"))
        xp_stored = [sem(f"xp_stored{j}") for j in range(2)]
        xr2_stored = [sem(f"xr2_stored{j}") for j in range(2)]
        w2_in, wl2_in = sem("w2_in"), sem("wl2_in")
        xp_in = [sem(f"xp_in{j}") for j in range(2)]
        x1_ready, stats2_ready = sem("x1_ready"), sem("stats2_ready")
        x1_stored = [sem(f"x1_stored{j}") for j in range(CT)]
        var2_ready, std2_ready, slice_w_in, mid_w_in, f_ones = (sem(n) for n in (
            "var2_ready", "std2_ready", "slice_w_in", "mid_w_in", "f_ones"))
        f_loaded = [sem(f"f_loaded{j}") for j in range(R)]
        f_xn_ready, f_xt_done, f_xT_ready, lg_done, sub_ready, exp_ready, rs_ready, fw_ready, s_done, wT_done, wT_ready = (
            sem(n) for n in ("f_xn_ready", "f_xt_done", "f_xT_ready", "lg_done", "sub_ready", "exp_ready", "rs_ready",
                             "fw_ready", "s_done", "wT_done", "wT_ready"))
        mid_pe, mid_dve, mid_act = sem("mid_pe"), sem("mid_dve"), sem("mid_act")
        y_loaded = [sem(f"y_loaded{j}") for j in range(2)]
        y_stored = [sem(f"y_stored{j}") for j in range(2)]
        w_st_ready, y_done, y_ready = sem("w_st_ready"), sem("y_done"), sem("y_ready")

        block = ctx.enter_context(nc.Block())
        LAST = T - 1

        @block.sync
        def _(sp):
            sp.dma_start(rows, dst.rearrange("(p k) -> p k", k=ROW)).then_inc(rows_in, 16)
            for w, d in ((wp, Wp1), (wr, Wr1), (wl, Wl1)):
                sp.dma_start(w[:, :, :], d.rearrange("(k p) c -> p k c", p=P)).then_inc(weights_in, 16)
            sp.dma_start(bias_p[:, :], bp1.rearrange("(a c) -> a c", a=1)).then_inc(weights_in, 16)
            sp.dma_start(bias_r[:, :], bl1.rearrange("(a c) -> a c", a=1)).then_inc(weights_in, 16)
            sp.dma_start(temp, temperature.rearrange("a h b c -> a (h b c)")).then_inc(fold_in, 16)
            sp.dma_start(wxT, W_xT).then_inc(fold_in, 16)
            sp.dma_start(wsl, W_slice).then_inc(fold_in, 16)
            sp.dma_start(bxT, b_xT).then_inc(fold_in, 16)
            sp.dma_start(bsl, b_slice.rearrange("(a g) -> a g", a=1)).then_inc(fold_in, 16)
            sp.wait_ge(fold_ready, 2)
            sp.dma_start(wxs_dram, wxs_o).then_inc(fold_stored, 16)
            sp.dma_start(bxs_dram, bxs_o.rearrange("a h g -> a (h g)")).then_inc(fold_stored, 16)
            sp.wait_ge(cnt_rows_ready, 1)
            sp.dma_start(cnt_dram.rearrange("(p c) -> p c", c=T), cnt).then_inc(cnt_out, 16)
            sp.wait_ge(cnt_out, 16)
            sp.dma_start(rcnt[0:TN, :], cnt_dram.rearrange("(t p) -> p t", p=TN), allow_slow_non_contiguous=True).then_inc(cnt_in, 16)

            def load_x(t, par):
                sp.dma_start(x_in[:, par, :], x_t[bass.ds(t, 1)].rearrange("a p c -> p (a c)")).then_inc(x_loaded[par], 16)

            load_x(0, 0)
            load_x(1, 1)
            sp.wait_ge(xn_ready, 1)
            load_x(2, 0)
            with sp.Fori(0, (T - 3) // 2) as i:
                for par in (1, 0):
                    t = 2 * i + 3 + (1 - par)
                    sp.wait_ge(xn_ready, 2 * i + 2 + (1 - par))
                    load_x(t, par)

            def load_xr(k, n, j, first):
                if not first:
                    sp.wait_ge(o_ready[k], n - CT + 1)
                sp.dma_start(xr_in[:, j, :], xr_dram[bass.ds(n, 1)].rearrange("a p c -> p (a c)")).then_inc(xr_loaded[k][j], 16)

            sp.wait_ge(xr_stored, 16 * T)
            sp.wait_ge(stored, BANKS)
            for j in range(CT):
                load_xr(0, j, j, True)
            sp.wait_ge(proj_done, T)
            for w, d in ((wp, Wp2), (wr, Wr2)):
                sp.dma_start(w[:, :, :], d.rearrange("(k p) c -> p k c", p=P)).then_inc(w2_in, 16)
            sp.dma_start(bias_p[:, :], bp2.rearrange("(a c) -> a c", a=1)).then_inc(w2_in, 16)
            sp.dma_start(bias_r[:, :], bl2.rearrange("(a c) -> a c", a=1)).then_inc(w2_in, 16)
            with sp.Fori(1, CH) as ch:
                for j in range(CT):
                    load_xr(0, CT * ch + j, j, False)
            load_xr(0, LAST, 0, False)
            sp.wait_ge(wl_done[0], T)
            sp.dma_start(wl[:, :, :], Wl2.rearrange("(k p) c -> p k c", p=P)).then_inc(wl2_in, 16)

            CUT = 20
            sp.wait_ge(agg_done[0][1], CH + 1)
            xp_all = xp_dram.rearrange("(t p) c -> p t c", p=TN)
            for j in range(2):
                sp.wait_ge(xp_stored[j], 16 * CUT // 2)
            sp.dma_start(xp[0:TN, 0:CUT, :], xp_all[:, 0:CUT, :]).then_inc(xp_in[0], 16)
            sp.wait_ge(xp_stored[0], 16 * (T // 2 + 1))
            sp.wait_ge(xp_stored[1], 16 * (T // 2))
            sp.dma_start(xp[0:TN, CUT:T, :], xp_all[:, CUT:T, :]).then_inc(xp_in[1], 16)
            sp.wait_ge(xr2_stored[0], 16 * (T // 2 + 1))
            sp.wait_ge(xr2_stored[1], 16 * (T // 2))
            sp.wait_ge(o_ready[0], T)

            def load_res(n, j, first):
                if not first:
                    sp.wait_ge(x1_ready, n - CT + 1)
                sp.dma_start(x_res[:, j, :], x_t[bass.ds(n, 1)].rearrange("a p c -> p (a c)")).then_inc(res_loaded[j], 16)

            for j in range(CT):
                load_xr(1, j, j, True)
                load_res(j, j, True)
            with sp.Fori(1, CH) as ch:
                for j in range(CT):
                    load_xr(1, CT * ch + j, j, False)
                    load_res(CT * ch + j, j, False)
            load_xr(1, LAST, 0, False)
            load_res(LAST, 0, False)

            sp.wait_ge(agg_done[1][1], CH + 1)
            sp.wait_ge(fold_stored, 32)
            sp.dma_start(wxs, wxs_dram).then_inc(slice_w_in, 16)
            sp.dma_start(bxs, bxs_dram).then_inc(slice_w_in, 16)

            def load_f(t, j, first):
                if not first:
                    sp.wait_ge(f_xn_ready, t - R + 1)
                sp.dma_start(f_in[:, j, :], x1_dram[bass.ds(t, 1)].rearrange("a p c -> p (a c)")).then_inc(f_loaded[j], 16)

            for j in range(CT):
                sp.wait_ge(x1_stored[j], 16 * CH)
                load_f(j, j, True)
            sp.dma_start(wfx, W_fx.rearrange("(k p) c -> p k c", p=P)).then_inc(mid_w_in, 16)
            sp.dma_start(bfx, b_fx.rearrange("(a c) -> a c", a=1)).then_inc(mid_w_in, 16)
            for w, d in ((wq, W_q), (wk, W_k), (wv, W_v)):
                sp.dma_start(w, d).then_inc(mid_w_in, 16)
            sp.dma_start(wo, W_out.rearrange("(h d) c -> d h c", d=D)).then_inc(mid_w_in, 16)
            sp.dma_start(bo, b_out.rearrange("(a c) -> a c", a=1)).then_inc(mid_w_in, 16)
            with sp.Fori(1, CH) as ch:
                for j in range(R):
                    load_f(R * ch + j, j, False)
            sp.wait_ge(x1_stored[0], 16 * (CH + 1))
            load_f(LAST, 0, False)

            def load_y(t, par, first):
                if not first:
                    sp.wait_ge(y_ready, t - 1)
                sp.dma_start(y_in[:, par, :], x1_dram[bass.ds(t, 1)].rearrange("a p c -> p (a c)")).then_inc(y_loaded[par], 16)

            load_y(0, 0, True)
            load_y(1, 1, True)
            load_y(2, 0, False)
            with sp.Fori(0, (T - 3) // 2) as i:
                load_y(2 * i + 3, 1, False)
                load_y(2 * i + 4, 0, False)

        @block.gpsimd
        def _(pool):
            ch_ = Chain(pool, pool_steps)
            small = dict(allow_small_or_imprecise_dtypes=True)
            ch_.link(pool.memset(ones[:, :], 1.0))
            pool.iota(thr, [[T, TN]], base=0, channel_multiplier=0, **small).then_inc(consts, 1)
            pool.iota(base5, [[D5, 5]], base=0, channel_multiplier=T, **small)
            pool.iota(own, [[1, T]], base=0, channel_multiplier=T, **small).then_inc(consts, 1)
            pool.affine_select(out=ident[:, :], in_=ones[:, :], compare_op=ALU.is_equal, fill=0.0, base=0,
                               pattern=[[-1, P]], channel_multiplier=1).then_inc(consts, 1)
            pool.iota(iota_low, [[1, P], [0, 2]], base=0, channel_multiplier=0, **small)
            pool.iota(iota_key, [[1, KEYS], [0, 2]], base=1, channel_multiplier=0, **small)
            pool.memset(key_t[:, Q:Q + 1], 0.0)
            pool.memset(low_t[:, Q:Q + 1], 0.0).then_inc(consts, 1)

            pool.wait_ge(r0_ready, 1)
            pool.indirect_dma_start(picked, None, dst.rearrange("(p k) -> p k", k=ROW),
                                    bass.IndirectOffsetOnAxis(ap=r0_i.bitcast(U32), axis=0)).then_inc(row_in, 16)
            dst_1, src_1 = dst.rearrange("(e a) -> e a", a=1), src.rearrange("(e a) -> e a", a=1)
            pool.wait_ge(start_ready, 1)
            pool.indirect_dma_start(coarse, None, dst_1,
                                    bass.IndirectOffsetOnAxis(ap=start_i.bitcast(U32), axis=0)).then_inc(coarse_in, 16)
            pool.wait_ge(fine_ready, 1)
            for i in range(5):
                at = bass.IndirectOffsetOnAxis(ap=start5_i[:, i, 0:1].bitcast(U32), axis=0)
                pool.indirect_dma_start(win_d[:, i, :], None, dst_1, at).then_inc(win_in[i], 16)
                pool.indirect_dma_start(win_s[:, i, :], None, src_1, at).then_inc(win_in[i], 16)

            def store_xr(t):
                pool.wait_ge(xr_ready, t + 1)
                pool.dma_start(xr_dram[bass.ds(t, 1)].rearrange("a p c -> p (a c)"), xr_o).then_inc(xr_stored, 16)

            with pool.Fori(0, T) as t:
                store_xr(t)

            def store_2(n, par):
                pool.wait_ge(lo2_ready, n + 1)
                pool.dma_start(xp_t[bass.ds(n, 1)].rearrange("a p c -> p (a c)"), xp_o[:, par, :]).then_inc(xp_stored[par], 16)
                pool.wait_ge(xr2_ready, n + 1)
                pool.dma_start(xr_dram[bass.ds(n, 1)].rearrange("a p c -> p (a c)"), xr_o2[:, par, :]).then_inc(xr2_stored[par], 16)

            pool.wait_ge(covered_ready, 1)
            is_covered = pool.value_load(covered[0:1, 0:1], min_val=0, max_val=1)
            with pool.If(is_covered == 1):
                pool.nop()
            with pool.Else():
                pool.wait_ge(stored, BANKS)
                pool.wait_ge(lo_ready, T)
                pool.dma_start(g_src[:, 0:ROW], src.rearrange("(p k) -> p k", k=ROW)).then_inc(g_tables_in, 16)
                pool.dma_start(g_dst_i, dst.rearrange("(p k) -> p k", k=ROW)).then_inc(g_tables_in, 16)
                pool.dma_start(g_xp_dram.rearrange("(t p) c -> p t c", p=TN), xp[0:TN, :, :]).then_inc(g_xp_out, 16)
                pool.iota(g_iota, [[1, CN]], base=0, channel_multiplier=0, **small).then_inc(g_iota_ready, 1)
                pool.iota(g_node, [[TN, T]], base=0, channel_multiplier=1, **small).then_inc(g_node_ready, 1)
                pieces = dst.rearrange("(s n) -> s n", n=N)
                with pool.Fori(0, E // N) as s_:
                    pool.wait_ge(g_all_used, s_)
                    pool.dma_start(g_all_i, pieces[bass.ds(s_, 1)].to_broadcast([TN, N])).then_inc(g_all_in, 16)
                pool.wait_ge(g_xp_out, 16)
                pool.wait_ge(g_tables_in, 32)
                pool.tensor_copy(g_src[:, ROW:ROW + 1], g_src[:, 0:1]).then_inc(g_idx_ready, 1)
                pool.tensor_copy(g_idx[:, 0, 0:1], g_src[:, 0:1]).then_inc(g_idx_ready, 1)
            pool.nop()

            def general_gathers(k, ch):
                table = g_xp_dram if k == 0 else xp_dram
                chunk = (CH + 1) * k + ch

                def group(i, slot):
                    u = ROW * chunk + RG * i + slot
                    pool.wait_ge(g_free, u + 2)
                    pool.wait_ge(g_idx_ready, u + 2)
                    pool.tensor_copy(g_idx[:, (slot + 1) % RG, 0:1], g_src[:, bass.ds(RG * i + slot + 1, 1)]
                                     ).then_inc(g_idx_ready, 1)
                    pool.indirect_dma_start(g_rows[:, slot, :], None, table,
                                            bass.IndirectOffsetOnAxis(ap=g_idx[:, slot, 0:1].bitcast(U32), axis=0)
                                            ).then_inc(g_in[slot], 16)

                with pool.If(is_covered == 1):
                    pool.nop()
                with pool.Else():
                    with pool.Fori(0, ROUNDS) as i:
                        for slot in range(RG):
                            group(i, slot)
                pool.nop()

            def stores_2(ch, tiles):
                for j in range(tiles):
                    store_2(CT * ch + j, j % 2)

            general_gathers(0, 0)
            with pool.Fori(1, CH + 1) as ch:
                general_gathers(0, ch)
                stores_2(ch - 1, CT)
            stores_2(CH, 1)
            for j in range(2):
                pool.wait_ge(xp_stored[j], 16 * (T // 2 + 1 - j))

            def store_x1(n, j):
                pool.wait_ge(x1_ready, n + 1)
                pool.dma_start(x1_dram[bass.ds(n, 1)].rearrange("a p c -> p (a c)"), o_t[:, j, :]).then_inc(x1_stored[j], 16)

            general_gathers(1, 0)
            with pool.Fori(1, CH + 1) as ch:
                general_gathers(1, ch)
                for j in range(CT):
                    store_x1(CT * (ch - 1) + j, j)
            store_x1(LAST, 0)

            pool.wait_ge(agg_done[1][1], CH + 1)
            pool.memset(f_xn[:, :, C:C + 1], 1.0).then_inc(f_ones, 1)

            def quotient(t, j, first):
                pool.wait_ge(rs_ready, t + 1)
                if not first:
                    pool.wait_ge(wT_done, t - R + 1)
                pool.tensor_tensor(f_w[:, j, :].rearrange("p (h g) -> p h g", h=H), f_e[:, j, :].rearrange("p (h g) -> p h g", h=H),
                                   f_rs[:, j, :].unsqueeze(2).to_broadcast([TN, H, G]), ALU.mult).then_inc(fw_ready, 1)

            for j in range(R):
                quotient(j, j, True)
            with pool.Fori(1, CH) as ch:
                for j in range(R):
                    quotient(R * ch + j, j, False)
            quotient(LAST, 0, False)

            def store_y(t, par):
                pool.wait_ge(y_ready, t + 1)
                pool.dma_start(out_t[bass.ds(t, 1)].rearrange("a p c -> p (a c)"), y_o[:, par, :]).then_inc(y_stored[par], 16)

            with pool.Fori(0, T // 2) as i:
                store_y(2 * i, 0)
                store_y(2 * i + 1, 1)
            store_y(LAST, 0)
            pool.wait_ge(y_stored[0], 16 * (T // 2 + 1))
            pool.wait_ge(y_stored[1], 16 * (T // 2))

        @block.tensor
        def _(pe):
            pe.wait_ge(step_ready, 1)
            pe.wait_ge(consts, 1)
            pe.matmul(ps[0:TN, 7, 0:1], step, ones[0:TN, 0:1], start=True, stop=True).then_inc(r0_done, 1)
            pe.wait_ge(fold_in, 16 * 5)
            for kc in range(KC):
                for h in range(H):
                    last = pe.matmul(ps[:, 4 + kc, h * G:(h + 1) * G], wxT[:, h, kc * P:(kc + 1) * P], wsl,
                                     start=True, stop=True)
            for h in range(H):
                last = pe.matmul(ps[0:1, 6, h * G:(h + 1) * G], bxT[:, h:h + 1], wsl, start=True, stop=True)
            last.then_inc(fold_done, 1)
            pe.wait_ge(rt_row, 1)
            pe.wait_ge(r0_ready, 1)
            pe.matmul(ps[:, 7, :], ones[0:1, :], rtemp_row.rearrange("a h g -> a (h g)"), start=True, stop=True).then_inc(rt_done, 1)
            pe.wait_ge(consts, 3)
            for i in range(5):
                pe.wait_ge(keys_ready, i + 1)
                if i >= 3:
                    pe.wait_ge(tables_ready, 2 * (i - 2))
                pe.transpose(ps[:, i % 3, 0:TN], key_f[:, i, :], ident[0:TN, 0:TN])
                pe.transpose(ps[:, i % 3, P:P + TN], low_f[:, i, :], ident[0:TN, 0:TN]).then_inc(turned, 1)
            pe.wait_ge(tables_ready, 10)

            def count_group(g, slot, bank0):
                pe.wait_ge(oh_ready, g + 1)
                for half in range(2):
                    bank = (bank0 + half) % 3
                    first_use = isinstance(g, int) and 2 * g + half < 3
                    if not first_use:
                        pe.wait_ge(stored, 2 * g + half - 2)
                    for q in range(HALF):
                        pair, k = slot * HALF + half * 2 + q // 2, q % 2
                        last = pe.matmul(ps[:, bank, q * KEYS:(q + 1) * KEYS], oh_low[:, pair, :, k], oh_key[:, pair, :, k],
                                         start=True, stop=True)
                    last.then_inc(built, 1)

            def turn_x(t):
                pe.wait_ge(xn_ready, t + 1)
                if not (isinstance(t, int) and t == 0):
                    pe.wait_ge(xT_ready, t)
                for kc in range(KC):
                    last = pe.transpose(ps[:, 4, kc * TN:(kc + 1) * TN], xn[:, kc * P:(kc + 1) * P], ident[0:TN, 0:TN])
                last.then_inc(xt_done, 1)

            def project(dst_p, dst_r, xT, done):
                for kc in range(KC):
                    pe.matmul(dst_p, xT[:, kc, :], wp[:, kc, :], start=(kc == 0), stop=False)
                pe.matmul(dst_p, ones[0:1, 0:TN], bias_p[:, :], start=False, stop=True)
                for kc in range(KC):
                    pe.matmul(dst_r, xT[:, kc, :], wr[:, kc, :], start=(kc == 0), stop=False)
                pe.matmul(dst_r, ones[0:1, 0:TN], bias_r[:, :], start=False, stop=True).then_inc(done, 1)

            def project_x(b):
                pe.wait_ge(xT_ready, b + 1)
                if not (isinstance(b, int) and b == 0):
                    pe.wait_ge(lo_ready, b)
                    pe.wait_ge(xr_ready, b)
                project(ps[0:TN, 5, 0:C], ps[0:TN, 6, 0:C], xnT, proj_done)

            def build_pass(it, front, back):
                count_group(3 * it, 0, 0)
                if back:
                    project_x(it - 1)
                count_group(3 * it + 1, 1, 2)
                if front:
                    turn_x(it)
                count_group(3 * it + 2, 2, 1)

            pe.wait_ge(weights_in, 16 * 5)
            pe.wait_ge(rt_ready, 1)
            pe.wait_ge(fold_ready, 2)
            pe.wait_ge(cnt_rows_ready, 1)
            pe.matmul(ps[0:1, 7, 0:1], cnt_row, ones[0:TN, 0:1], start=True, stop=True).then_inc(total_done, 1)
            build_pass(0, True, False)
            with pe.Fori(1, T) as it:
                build_pass(it, True, True)
            build_pass(T, False, True)
            pe.wait_ge(oh_ready, 3 * PASSES + 1)
            pe.wait_ge(stored, BANKS - 3)
            pe.matmul(ps[:, 0, 0:KEYS], oh_low[:, 0, :, 0], oh_key[:, 0, :, 0], start=True, stop=True).then_inc(built, 1)

            def sum_messages(k, ch, n):
                with pe.If(is_covered == 1):
                    for c in range(KC):
                        if not (isinstance(ch, int) and ch == 0):
                            pe.wait_ge(msg_ready[k][c], ch)
                        for t in range(T):
                            for part in range(2):
                                last = pe.matmul(ps[:, c, 0:n], xp[0:TN, t, part * C + c * P:part * C + (c + 1) * P],
                                                 adj[0:TN, t, bass.ds(CN * ch, n)],
                                                 start=(t == 0 and part == 0), stop=(t == T - 1 and part == 1))
                        last.then_inc(agg_done[k][c], 1)
                with pe.Else():
                    general_sum(k, ch, n)
                pe.nop()

            def general_sum(k, ch, n):
                chunk = (CH + 1) * k + ch

                def group(i, slot, first=False, final=False):
                    pe.wait_ge(g_in[slot], 16 * (ROUNDS * chunk + i + 1))
                    pe.wait_ge(g_oh_ready, ROW * chunk + RG * i + slot + 1)
                    for c in range(KC):
                        for part in range(2):
                            last = pe.matmul(ps[:, c, 0:n], g_rows[:, slot, part * C + c * P:part * C + (c + 1) * P],
                                             g_oh[:, slot, 0:n], start=first and part == 0, stop=final and part == 1)
                            if first and c == 0 and part == 0:
                                last.then_inc(g_free, 1)
                        if final:
                            last.then_inc(agg_done[k][c], 1)
                    if not final:
                        last.then_inc(g_free, 1)

                if not (isinstance(ch, int) and ch == 0):
                    for c in range(KC):
                        pe.wait_ge(msg_ready[k][c], ch)
                for slot in range(RG):
                    group(0, slot, first=slot == 0)
                with pe.Fori(1, ROUNDS - 1) as i:
                    for slot in range(RG):
                        group(i, slot)
                for slot in range(RG):
                    group(ROUNDS - 1, slot, final=slot == RG - 1)

            def times_wl(k, ch, tiles):
                for c in range(KC):
                    pe.wait_ge(msg_ready[k][c], ch + 1)
                if not (isinstance(ch, int) and ch == 0):
                    pe.wait_ge(o_ready[k], CT * ch)
                    pe.wait_ge(nrm_ready[k], ch)
                for j in range(tiles):
                    to = ps[0:TN, 2 + j // 2, (j % 2) * C:(j % 2 + 1) * C]
                    for kc in range(KC):
                        last = pe.matmul(to, msgT[:, kc, j * TN:(j + 1) * TN], wl[:, kc, :], start=(kc == 0), stop=(kc == 1))
                    last.then_inc(wl_done[k], 1)

            def turn_h(n, j):
                pe.wait_ge(h_ready, n + 1)
                if not isinstance(n, int) or n >= 2:
                    pe.wait_ge(hT_ready, n - 1)
                for kc in range(KC):
                    last = pe.transpose(ps[:, 4 + j % 2, kc * TN:(kc + 1) * TN], o_t[:, j, kc * P:(kc + 1) * P], ident[0:TN, 0:TN])
                last.then_inc(ht_done, 1)

            def project_h(n, j):
                pe.wait_ge(hT_ready, n + 1)
                if not isinstance(n, int) or n >= 2:
                    pe.wait_ge(lo2_ready, n - 1)
                    pe.wait_ge(xr2_ready, n - 1)
                project(ps[0:TN, 6 + j % 2, 0:C], ps[0:TN, 6 + j % 2, C:2 * C], hT[:, j % 2], proj2_done)

            def next_inputs(ch, tiles):
                for j in range(min(2, tiles)):
                    turn_h(CT * ch + j, j)
                for j in range(tiles):
                    project_h(CT * ch + j, j)
                    if j + 2 < tiles:
                        turn_h(CT * ch + j + 2, j + 2)

            pe.wait_ge(stored, BANKS)
            pe.wait_ge(lo_ready, T)
            pe.wait_ge(xr_ready, T)
            pe.wait_ge(covered_ready, 1)
            is_covered = pe.value_load(covered[0:1, 0:1], min_val=0, max_val=1)
            with pe.If(is_covered == 1):
                pe.nop()
            with pe.Else():
                pe.nop().then_inc(g_free, RG - 1)
            pe.nop()
            sum_messages(0, 0, CN)
            pe.wait_ge(w2_in, 16 * 4)
            times_wl(0, 0, CT)
            sum_messages(0, 1, CN)
            next_inputs(0, CT)
            with pe.Fori(2, CH) as ch:
                times_wl(0, ch - 1, CT)
                sum_messages(0, ch, CN)
                next_inputs(ch - 1, CT)
            times_wl(0, CH - 1, CT)
            sum_messages(0, CH, TN)
            next_inputs(CH - 1, CT)
            times_wl(0, CH, 1)
            next_inputs(CH, 1)

            for j in range(2):
                pe.wait_ge(xp_in[j], 16)
            pe.wait_ge(msg_ready[0][0], CH + 1)
            pe.wait_ge(msg_ready[0][1], CH + 1)
            sum_messages(1, 0, CN)
            pe.wait_ge(wl2_in, 16)
            pe.wait_ge(nrm_ready[0], CH + 1)
            with pe.Fori(1, CH) as ch:
                times_wl(1, ch - 1, CT)
                sum_messages(1, ch, CN)
            times_wl(1, CH - 1, CT)
            sum_messages(1, CH, TN)
            times_wl(1, CH, 1)

            def turn_f(t, j):
                pe.wait_ge(f_xn_ready, t + 1)
                if not (isinstance(t, int) and t == 0):
                    pe.wait_ge(f_xT_ready, t)
                for kc in range(KC):
                    last = pe.transpose(ps[:, 5, kc * TN:(kc + 1) * TN], f_xn[:, j, kc * P:(kc + 1) * P], ident[0:TN, 0:TN])
                last.then_inc(f_xt_done, 1)

            def logits(t, j):
                pe.wait_ge(f_xT_ready, t + 1)
                if not isinstance(t, int) or t >= 2:
                    pe.wait_ge(sub_ready, t - 1)
                to = ps[0:TN, 4 if j % 2 == 0 else 7, :]
                for kc in range(KC):
                    pe.matmul(to, f_xT[:, j, kc, :], wxs[:, kc, :], start=(kc == 0), stop=False)
                pe.matmul(to, ones[0:1, 0:TN], bxs, start=False, stop=True).then_inc(lg_done, 1)

            def gather_slices(t, j, first, last_):
                pe.wait_ge(fw_ready, t + 1)
                for k in range(PAIRS):
                    last = pe.matmul(ps[:, k, 0:C + 1], f_w[:, j, k * P:(k + 1) * P], f_xn[:, j, 0:C + 1], start=first, stop=last_)
                last.then_inc(s_done, 1)
                if not first:
                    pe.wait_ge(wT_ready, t)
                for k in range(PAIRS):
                    last = pe.transpose(ps[:, 6, k * TN:(k + 1) * TN], f_w[:, j, k * P:(k + 1) * P], ident[0:TN, 0:TN])
                last.then_inc(wT_done, 1)

            def slice_pass(p, j, front=True, back=True):
                if front:
                    turn_f(p, j)
                if back:
                    gather_slices(p - 2, (j - 2) % R, isinstance(p, int) and p == 2, isinstance(p, int) and p == T + 1)
                if front:
                    logits(p, j)

            pe.wait_ge(f_ones, 1)
            pe.wait_ge(slice_w_in, 32)
            pe.wait_ge(o_ready[1], T)
            pe.wait_ge(nrm_ready[1], CH + 1)
            slice_pass(0, 0, back=False)
            slice_pass(1, 1, back=False)
            slice_pass(2, 2)
            with pe.Fori(0, (T - 5) // R) as i:
                for j in range(R):
                    slice_pass(R * i + 3 + j, (3 + j) % R)
            for p in range(3 + (T - 5) // R * R, T + 2):
                slice_pass(p, p % R, front=p < T)

            pe.wait_ge(mid_w_in, 16 * 7)
            pe.wait_ge(mid_dve, 1)
            for kc in range(KC):
                for k in range(PAIRS):
                    pe.transpose(ps[:, 4 + kc, k * P:(k + 1) * P], s_sb[:, k, kc * P:(kc + 1) * P], ident[:, :])
            pe.wait_ge(wT_ready, T)
            for k in range(PAIRS):
                last = pe.transpose(ps[0:1, 6, k * P:(k + 1) * P], s_sb[:, k, C:C + 1], ident[:, :])
            last.then_inc(mid_pe, 1)
            pe.wait_ge(mid_dve, 2)
            pe.wait_ge(mid_act, 1)
            for h in range(H):
                hs = slice(h * D, (h + 1) * D)
                for kc in range(KC):
                    pe.matmul(ps[0:D, 7, hs], wfx[:, kc, hs], sT[:, kc, hs], start=(kc == 0), stop=False)
                last = pe.matmul(ps[0:D, 7, hs], bfx[:, hs], nr[:, hs], start=False, stop=True)
            last.then_inc(mid_pe, 1)
            pe.wait_ge(mid_dve, 3)
            pe.matmul(ps[0:D, 4, :], wq, tokT, start=True, stop=True).then_inc(mid_pe, 1)
            pe.matmul(ps[0:D, 5, :], wk, tokT, start=True, stop=True).then_inc(mid_pe, 1)
            for h in range(H):
                hs = slice(h * G, (h + 1) * G)
                last = pe.matmul(ps[0:G, 6, h * D:(h + 1) * D], tokT[:, hs], wv, start=True, stop=True)
            last.then_inc(mid_pe, 1)
            pe.wait_ge(mid_dve, 4)
            pe.wait_ge(mid_act, 2)
            for h in range(H):
                hs = slice(h * G, (h + 1) * G)
                last = pe.matmul(ps[0:G, 7, hs], qT[:, hs], kT[:, hs], start=True, stop=True)
            last.then_inc(mid_pe, 1)
            pe.wait_ge(mid_dve, 6)
            for h in range(H):
                last = pe.transpose(ps[0:G, 4, h * G:(h + 1) * G], a_w[:, h, :], ident[0:G, 0:G])
            last.then_inc(mid_pe, 1)
            pe.wait_ge(mid_act, 3)
            pe.wait_ge(mid_dve, 7)
            for h in range(H):
                last = pe.matmul(ps[0:D, 5, h * G:(h + 1) * G], v_sb[:, h * D:(h + 1) * D], aT[:, h * G:(h + 1) * G],
                                 start=True, stop=True)
            last.then_inc(mid_pe, 1)
            pe.wait_ge(mid_dve, 8)
            for h in range(H):
                k = h // 2
                to = ps[(h % 2) * G:(h % 2 + 1) * G, 6 + k // 2, (k % 2) * C:(k % 2 + 1) * C]
                last = pe.matmul(to, osT[:, h * G:(h + 1) * G], wo[:, h, :], start=True, stop=True)
            last.then_inc(mid_pe, 1)

            def outputs(t, par, first):
                pe.wait_ge(w_st_ready, t + 1)
                if not first:
                    pe.wait_ge(y_ready, t - 1)
                to = ps[0:TN, par, 0:C]
                for k in range(PAIRS):
                    pe.matmul(to, w_st[:, par, k, :], t_sb[:, k, :], start=(k == 0), stop=False)
                pe.matmul(to, ones[0:1, 0:TN], bo, start=False, stop=True).then_inc(y_done, 1)

            pe.wait_ge(mid_dve, 10)
            outputs(0, 0, True)
            outputs(1, 1, True)
            outputs(2, 0, False)
            with pe.Fori(0, (T - 3) // 2) as i:
                outputs(2 * i + 3, 1, False)
                outputs(2 * i + 4, 0, False)

        @block.scalar
        def _(act):
            ch_ = Chain(act, act_steps)
            def table(i, at, to):
                act.wait_ge(turned, i + 1)
                act.activation(to[:, 0:Q].rearrange("e (p i) -> e i p", i=5)[:, i, :], ps[:, i % 3, at:at + TN],
                               ACT.Copy).then_inc(tables_ready, 1)

            for i in range(5):
                table(i, 0, key_t)
                table(i, P, low_t)

            def store_counts(hb, bank):
                act.wait_ge(built, hb + 1)
                d0 = hb * HALF * D5
                act.activation(adj[:, :, bass.ds(d0, HALF * D5)].rearrange("p s (q d) -> p q s d", q=HALF),
                               ps[:, bank, 0:HALF * KEYS].rearrange("p (q s d) -> p q s d", q=HALF, s=T),
                               ACT.Copy).then_inc(stored, 1)

            def build_pass(it, front, back):
                b = it - 1
                store_counts(6 * it, 0)
                store_counts(6 * it + 1, 1)
                if back:
                    act.wait_ge(proj_done, b + 1)
                    act.activation(xp[0:TN, bass.ds(b, 1), 0:C].rearrange("p a c -> p (a c)"), ps[0:TN, 5, 0:C],
                                   ACT.Relu).then_inc(hi_ready, 1)
                    if not isinstance(b, int) or b > 0:
                        act.wait_ge(xr_stored, 16 * b)
                    act.activation(xr_o, ps[0:TN, 6, 0:C], ACT.Copy).then_inc(xr_ready, 1)
                store_counts(6 * it + 2, 2)
                if front:
                    act.wait_ge(var_ready, it + 1)
                    act.activation(std, var, ACT.Sqrt).then_inc(std_ready, 1)
                store_counts(6 * it + 3, 0)
                if front:
                    act.wait_ge(xt_done, it + 1)
                    act.activation(xnT.rearrange("p k n -> p (k n)"), ps[:, 4, 0:KC * TN], ACT.Copy).then_inc(xT_ready, 1)
                store_counts(6 * it + 4, 1)
                store_counts(6 * it + 5, 2)

            act.wait_ge(fine_ready, 1)
            act.wait_ge(cnt_out, 16)
            act.wait_ge(fold_stored, 32)
            build_pass(0, True, False)
            with act.Fori(1, T) as it:
                build_pass(it, True, True)
            build_pass(T, False, True)
            act.wait_ge(built, BANKS)
            act.activation(adj[:, :, N - D5:N], ps[:, 0, 0:KEYS].rearrange("p (s d) -> p s d", s=T), ACT.Copy).then_inc(stored, 1)

            def message(k, ch, n):
                act.wait_ge(agg_done[k][0], ch + 1)
                act.activation(msgT[:, 0, 0:n], ps[:, 0, 0:n], ACT.Copy).then_inc(msg_ready[k][0], 1)

            def norms(k, ch, tiles):
                for j in range(tiles):
                    act.wait_ge(o_ready[k], CT * ch + min(tiles, j // 2 * 2 + 2))
                    last = act.activation(ps[0:TN, 2 + j // 2, (j % 2) * C:(j % 2 + 1) * C], o_t[:, j, :], ACT.Square,
                                          accum_out=ss[:, j:j + 1])
                    last.then_inc(sq_done[k], 1)
                act.wait_ge(sq_done[k], CT * ch + tiles)
                act.activation(nrm[:, 0:tiles], ss[:, 0:tiles], ACT.Sqrt).then_inc(nrm_ready[k], 1)

            def h_turned(n, j):
                act.wait_ge(ht_done, n + 1)
                if not isinstance(n, int) or n >= 2:
                    act.wait_ge(proj2_done, n - 1)
                act.activation(hT[:, j % 2].rearrange("p k n -> p (k n)"), ps[:, 4 + j % 2, 0:KC * TN], ACT.Copy).then_inc(hT_ready, 1)

            def h_projected(n, j, stores):
                act.wait_ge(proj2_done, n + 1)
                if not isinstance(n, int) or n >= 2:
                    act.wait_ge(xp_stored[j % 2], 16 * stores)
                act.activation(xp_o[:, j % 2, 0:C], ps[0:TN, 6 + j % 2, 0:C], ACT.Relu).then_inc(hi2_ready, 1)
                if not isinstance(n, int) or n >= 2:
                    act.wait_ge(xr2_stored[j % 2], 16 * stores)
                act.activation(xr_o2[:, j % 2, :], ps[0:TN, 6 + j % 2, C:2 * C], ACT.Copy).then_inc(xr2_ready, 1)

            def next_inputs(ch, tiles):
                for j in range(min(2, tiles)):
                    h_turned(CT * ch + j, j)
                for j in range(tiles):
                    h_projected(CT * ch + j, j, 2 * ch + j // 2)
                    if j + 2 < tiles:
                        h_turned(CT * ch + j + 2, j + 2)

            message(0, 0, CN)
            norms(0, 0, CT)
            message(0, 1, CN)
            next_inputs(0, CT)
            with act.Fori(2, CH) as ch:
                norms(0, ch - 1, CT)
                message(0, ch, CN)
                next_inputs(ch - 1, CT)
            norms(0, CH - 1, CT)
            message(0, CH, TN)
            next_inputs(CH - 1, CT)
            norms(0, CH, 1)
            next_inputs(CH, 1)

            message(1, 0, CN)
            with act.Fori(1, CH) as ch:
                norms(1, ch - 1, CT)
                message(1, ch, CN)
            norms(1, CH - 1, CT)
            message(1, CH, TN)
            norms(1, CH, 1)

            act.wait_ge(var2_ready, 1)
            act.activation(std2, var2, ACT.Sqrt).then_inc(std2_ready, 1)

            def x_turned(t, j):
                act.wait_ge(f_xt_done, t + 1)
                if not isinstance(t, int) or t >= R:
                    act.wait_ge(lg_done, t - R + 1)
                act.activation(f_xT[:, j].rearrange("p k n -> p (k n)"), ps[:, 5, 0:KC * TN], ACT.Copy).then_inc(f_xT_ready, 1)

            def exps(t, j):
                act.wait_ge(sub_ready, t + 1)
                act.activation(f_e[:, j, :], f_e[:, j, :], ACT.Exp).then_inc(exp_ready, 1)

            def w_turned(t):
                act.wait_ge(wT_done, t + 1)
                act.activation(w_tr[:, :, bass.ds(TN * t, TN)], ps[:, 6, 0:PAIRS * TN].rearrange("p (k n) -> p k n", k=PAIRS),
                               ACT.Copy).then_inc(wT_ready, 1)

            def slice_pass(p, j, front=True, back=True):
                if front:
                    x_turned(p, j)
                if back:
                    w_turned(p - 2)
                if front:
                    exps(p, j)

            slice_pass(0, 0, back=False)
            slice_pass(1, 1, back=False)
            slice_pass(2, 2)
            slice_pass(3, 3)
            with act.Fori(1, CH) as i:
                for j in range(R):
                    slice_pass(R * i + j, j)
            for p in range(CH * R, T + 2):
                slice_pass(p, p % R, front=p < T)

            act.wait_ge(mid_pe, 1)
            act.activation(sT[:, 0, :], ps[:, 4, :], ACT.Copy).then_inc(mid_act, 1)
            act.wait_ge(mid_pe, 3)
            act.activation(qT, ps[0:D, 4, :], ACT.Copy).then_inc(mid_act, 1)
            act.wait_ge(mid_pe, 5)
            act.activation(v_sb, ps[0:G, 6, :], ACT.Copy).then_inc(mid_act, 1)
            act.wait_ge(mid_dve, 5)
            act.activation(a_e.rearrange("p h g -> p (h g)"), a_e.rearrange("p h g -> p (h g)"), ACT.Exp, scale=SCALE).then_inc(mid_act, 1)

        @block.vector
        def _(dve):
            c = Chain(dve, dve_steps)
            dve.wait_ge(consts, 2)
            dve.wait_ge(rows_in, 16)
            c.link(dve.tensor_copy(rowmax, rows[:, ROW - 1:ROW]))
            dve.tensor_scalar(step, thr, rowmax, None, ALU.is_gt).then_inc(step_ready, 1)
            dve.wait_ge(r0_done, 1)
            c.link(dve.tensor_scalar(r0, ps[0:TN, 7, 0:1], float(TN - 1), None, ALU.min))
            dve.tensor_copy(r0_i, r0).then_inc(r0_ready, 1)
            dve.wait_ge(fold_in, 16 * 5)
            c.link(dve.tensor_scalar(rtemp, temp, 0.1, 5.0, ALU.max, ALU.min))
            c.link(dve.reciprocal(rtemp, rtemp))
            dve.tensor_copy(rtemp_row, rtemp.unsqueeze(2).to_broadcast([1, H, G])).then_inc(rt_row, 1)
            dve.wait_ge(row_in, 16)
            c.link(dve.tensor_copy(picked_f, picked))
            c.link(dve.tensor_scalar(junk[:, 0:ROW], picked_f, own[:, 0:1], None, ALU.is_lt, ALU.add, accum_out=below))
            c.link(dve.scalar_tensor_tensor(out=start, in0=r0, scalar=float(ROW), in1=below, op0=ALU.mult, op1=ALU.add))
            c.link(dve.tensor_scalar(start_c, start, float(E - COARSE), None, ALU.min))
            dve.tensor_copy(start_i, start_c).then_inc(start_ready, 1)
            dve.wait_ge(fold_done, 1)
            dve.wait_ge(rt_done, 1)
            dve.tensor_copy(rtemp_all, ps[:, 7, :]).then_inc(rt_ready, 1)
            dve.wait_ge(rt_ready, 1)
            for kc in range(KC):
                last = dve.tensor_tensor(wxs_o[:, kc, :], ps[:, 4 + kc, :], rtemp_all, ALU.mult)
            last.then_inc(fold_ready, 1)
            c.link(dve.tensor_tensor(bxs_t, ps[0:1, 6, :].rearrange("p (h g) -> p h g", h=H),
                                     bsl.unsqueeze(1).to_broadcast([1, H, G]), ALU.add))
            dve.tensor_tensor(bxs_o, bxs_t, rtemp_row, ALU.mult).then_inc(fold_ready, 1)
            dve.wait_ge(coarse_in, 16)
            c.link(dve.tensor_copy(coarse_f, coarse))
            for i in range(5):
                c.link(dve.tensor_scalar(junk, coarse_f, base5[:, i:i + 1], None, ALU.is_lt, ALU.add,
                                         accum_out=below5[:, i:i + 1]))
            c.link(dve.tensor_scalar(start5, below5, start_c, float(E - WIN), ALU.add, ALU.min))
            dve.tensor_copy(start5_i[:, :, 0], start5).then_inc(fine_ready, 1)
            for i in range(5):
                dve.wait_ge(win_in[i], 32)
                c.link(dve.tensor_scalar(hi_i[:, i], win_s[:, i], 1.0 / TN, -0.496, ALU.mult, ALU.add))
                c.link(dve.tensor_copy(win_f[:, i], win_d[:, i]))
                c.link(dve.tensor_scalar(dl[:, i], win_f[:, i], base5[:, i:i + 1], None, ALU.subtract))
                c.link(dve.tensor_scalar(ge0[:, i], dl[:, i], 0.0, None, ALU.is_ge))
                c.link(dve.scalar_tensor_tensor(out=low_f[:, i], in0=hi_i[:, i], scalar=-float(TN), in1=win_s[:, i],
                                                op0=ALU.mult, op1=ALU.add))
                c.link(dve.scalar_tensor_tensor(out=valid[:, i], in0=dl[:, i], scalar=float(D5), in1=ge0[:, i],
                                                op0=ALU.is_lt, op1=ALU.mult))
                c.link(dve.scalar_tensor_tensor(out=pair_f[:, i], in0=hi_i[:, i], scalar=float(D5), in1=dl[:, i],
                                                op0=ALU.mult, op1=ALU.add))
                dve.scalar_tensor_tensor(out=key_f[:, i], in0=pair_f[:, i], scalar=1.0, in1=valid[:, i],
                                         op0=ALU.add, op1=ALU.mult).then_inc(keys_ready, 1)
            for i in range(5):
                for d in range(D5):
                    col = D5 * i + d
                    c.link(dve.tensor_scalar(junk2, win_f[:, i], own[:, col:col + 1], None, ALU.is_equal, ALU.add,
                                             accum_out=cnt[:, col:col + 1]))
            dve.tensor_reduce(cnt_row, cnt, AX_X, ALU.add).then_inc(cnt_rows_ready, 1)
            dve.wait_ge(total_done, 1)
            dve.tensor_scalar(covered[0:1, 0:1], ps[0:1, 7, 0:1], float(E), None, ALU.is_equal).then_inc(covered_ready, 1)

            def one_hots(g, slot, tile0):
                first = isinstance(g, int) and g < 3
                if not first:
                    dve.wait_ge(built, 2 * g - 4)
                pairs = slice(slot * HALF, (slot + 1) * HALF)
                low = low_t[:, bass.ds(tile0, SUB)].rearrange("p (a k) -> p a k", k=2).unsqueeze(2).to_broadcast([P, HALF, P, 2])
                key = key_t[:, bass.ds(tile0, SUB)].rearrange("p (a k) -> p a k", k=2).unsqueeze(2).to_broadcast([P, HALF, KEYS, 2])
                dve.tensor_tensor(oh_low[:, pairs], iota_low.unsqueeze(1).to_broadcast([P, HALF, P, 2]), low, ALU.is_equal)
                dve.tensor_tensor(oh_key[:, pairs], iota_key.unsqueeze(1).to_broadcast([P, HALF, KEYS, 2]), key,
                                  ALU.is_equal).then_inc(oh_ready, 1)

            def build_pass(it, front, back, par, loads):
                if front:
                    dve.wait_ge(x_loaded[par], 16 * loads)
                    c.link(dve.bn_stats(st6, x_in[:, par, :]))
                one_hots(3 * it, 0, 24 * it)
                if front:
                    c.link(dve.bn_aggr(mv, st6))
                    dve.tensor_scalar(var, mv[:, 1:2], EPS_LN, None, ALU.add).then_inc(var_ready, 1)
                one_hots(3 * it + 1, 1, 24 * it + 8)
                if front:
                    dve.wait_ge(std_ready, it + 1)
                    c.link(dve.reciprocal(rstd, std))
                    if not isinstance(it, int) or it > 0:
                        dve.wait_ge(xt_done, it)
                    dve.tensor_scalar(xn, x_in[:, par, :], mv[:, 0:1], rstd, ALU.subtract, ALU.mult).then_inc(xn_ready, 1)
                one_hots(3 * it + 2, 2, 24 * it + 16)
                if back:
                    b = it - 1
                    dve.wait_ge(hi_ready, b + 1)
                    dve.scalar_tensor_tensor(out=xp[0:TN, bass.ds(b, 1), C:2 * C].rearrange("p a c -> p (a c)"),
                                             in0=ps[0:TN, 5, 0:C], scalar=0.0,
                                             in1=xp[0:TN, bass.ds(b, 1), 0:C].rearrange("p a c -> p (a c)"),
                                             op0=ALU.max, op1=ALU.subtract).then_inc(lo_ready, 1)

            dve.wait_ge(consts, 4)
            dve.wait_ge(tables_ready, 10)
            build_pass(0, True, False, 0, 1)
            rounds = (T - 1) // 2
            with dve.Fori(0, rounds) as i:
                c.loop(i, 6)
                build_pass(2 * i + 1, True, True, 1, i + 1)
                build_pass(2 * i + 2, True, True, 0, i + 2)
            c.end(rounds)
            build_pass(T, False, True, 1, 0)
            dve.wait_ge(built, 2 * 3 * PASSES - 4)
            dve.tensor_tensor(oh_low[:, 0], iota_low, low_t[:, Q - 1:Q + 1].unsqueeze(1).to_broadcast([P, P, 2]), ALU.is_equal)
            dve.tensor_tensor(oh_key[:, 0], iota_key, key_t[:, Q - 1:Q + 1].unsqueeze(1).to_broadcast([P, KEYS, 2]),
                              ALU.is_equal).then_inc(oh_ready, 1)
            dve.wait_ge(cnt_in, 16)
            c.link(dve.tensor_scalar(rcnt[0:TN, :], rcnt[0:TN, :], 1.0, None, ALU.max))
            c.link(dve.reciprocal(rcnt[0:TN, :], rcnt[0:TN, :]))
            dve.wait_ge(stored, BANKS)
            is_covered = dve.value_load(covered[0:1, 0:1], min_val=0, max_val=1)
            with dve.If(is_covered == 1):
                dve.nop()
            with dve.Else():
                g = Chain(dve, g_steps)
                dve.wait_ge(g_tables_in, 32)
                g.link(dve.tensor_copy(g_dst, g_dst_i))
                dve.wait_ge(g_node_ready, 1)
                g.link(dve.memset(g_cnt, 0.0))
                with dve.Fori(0, E // N) as s_:
                    g.loop(s_, T + 1)
                    dve.wait_ge(g_all_in, 16 * s_ + 16)
                    dve.tensor_copy(g_all, g_all_i).then_inc(g_all_used, 1)
                    dve.wait_ge(g_all_used, s_ + 1)
                    for t in range(T):
                        g.link(dve.tensor_scalar(g_eq, g_all, g_node[:, t:t + 1], None, ALU.is_equal, ALU.add,
                                                 accum_out=g_part[:, t:t + 1]))
                    g.link(dve.tensor_tensor(g_cnt, g_cnt, g_part, ALU.add))
                g.end(E // N)
                g.link(dve.tensor_scalar(g_cnt, g_cnt, 1.0, None, ALU.max))
                g.link(dve.reciprocal(rcnt[0:TN, :], g_cnt))
                dve.wait_ge(g_iota_ready, 1)
            dve.nop()

            def general_one_hots(k, ch):
                chunk = (CH + 1) * k + ch
                rel = (CH + 2) * k + ch

                def group(i, slot):
                    kk = RG * i + slot
                    dve.wait_ge(g_rel_ready, rel + 1)
                    dve.wait_ge(g_free, ROW * chunk + kk + 1)
                    dve.tensor_scalar(g_oh[:, slot, :], g_iota, g_rel[:, bass.ds(kk, 1)], None, ALU.is_equal).then_inc(g_oh_ready, 1)

                with dve.If(is_covered == 1):
                    dve.nop()
                with dve.Else():
                    if isinstance(ch, int) and ch == 0:
                        if k:
                            dve.wait_ge(g_rel_ready, rel)
                        dve.tensor_copy(g_rel, g_dst).then_inc(g_rel_ready, 1)
                    with dve.Fori(0, ROUNDS) as i:
                        for slot in range(RG):
                            group(i, slot)
                    dve.wait_ge(g_oh_ready, ROW * chunk + ROW)
                    dve.tensor_scalar(g_rel, g_rel, -float(CN), None, ALU.add).then_inc(g_rel_ready, 1)
                dve.nop()

            def message(k, ch, n, after=None):
                general_one_hots(k, ch)
                if after is not None:
                    dve.wait_ge(after, CT * ch)
                dve.wait_ge(agg_done[k][1], ch + 1)
                dve.tensor_copy(msgT[:, 1, 0:n], ps[:, 1, 0:n]).then_inc(msg_ready[k][1], 1)

            def combine(k, ch, tiles):
                for j in range(tiles):
                    n = CT * ch + j
                    dve.wait_ge(wl_done[k], CT * ch + min(tiles, j // 2 * 2 + 2))
                    dve.wait_ge(xr_loaded[k][j], 16 * (ch + 1))
                    if not isinstance(ch, int) or ch > 0:
                        if k == 0:
                            dve.wait_ge(ht_done, n - CT + 1)
                        else:
                            dve.wait_ge(x1_stored[j], 16 * ch)
                            dve.wait_ge(stats2_ready, n - CT + 1)
                    dve.scalar_tensor_tensor(out=o_t[:, j, :], in0=ps[0:TN, 2 + j // 2, (j % 2) * C:(j % 2 + 1) * C],
                                             scalar=rcnt[0:TN, bass.ds(n, 1)], in1=xr_in[:, j, :],
                                             op0=ALU.mult, op1=ALU.add).then_inc(o_ready[k], 1)
                dve.wait_ge(nrm_ready[k], ch + 1)
                c.link(dve.tensor_scalar(nrm[:, 0:tiles], nrm[:, 0:tiles], EPS_NORM, None, ALU.max))
                c.link(dve.reciprocal(inv[:, 0:tiles], nrm[:, 0:tiles]))
                for j in range(tiles):
                    n = CT * ch + j
                    if k == 0:
                        dve.tensor_scalar(o_t[:, j, :], o_t[:, j, :], inv[:, j:j + 1], 0.0, ALU.mult, ALU.max).then_inc(h_ready, 1)
                    else:
                        dve.wait_ge(res_loaded[j], 16 * (ch + 1))
                        dve.scalar_tensor_tensor(out=o_t[:, j, :], in0=o_t[:, j, :], scalar=inv[:, j:j + 1], in1=x_res[:, j, :],
                                                 op0=ALU.mult, op1=ALU.add).then_inc(x1_ready, 1)

            def row_stats(ch, tiles):
                for j in range(tiles):
                    dve.bn_stats(stats2[0:TN, bass.ds(CT * ch + j, 1), :].rearrange("p a b -> p (a b)"),
                                 o_t[:, j, :]).then_inc(stats2_ready, 1)

            def lows(ch, tiles):
                for j in range(tiles):
                    n = CT * ch + j
                    dve.wait_ge(hi2_ready, n + 1)
                    dve.wait_ge(xr2_ready, n + 1)
                    dve.scalar_tensor_tensor(out=xp_o[:, j % 2, C:2 * C], in0=ps[0:TN, 6 + j % 2, 0:C], scalar=0.0,
                                             in1=xp_o[:, j % 2, 0:C], op0=ALU.max, op1=ALU.subtract).then_inc(lo2_ready, 1)

            message(0, 0, CN)
            combine(0, 0, CT)
            message(0, 1, CN)
            lows(0, CT)
            with dve.Fori(2, CH) as ch:
                c.loop(ch - 2, 2)
                combine(0, ch - 1, CT)
                message(0, ch, CN)
                lows(ch - 1, CT)
            c.end(CH - 2)
            combine(0, CH - 1, CT)
            message(0, CH, TN)
            lows(CH - 1, CT)
            combine(0, CH, 1)
            lows(CH, 1)

            message(1, 0, CN)
            combine(1, 0, CT)
            message(1, 1, CN, x1_ready)
            row_stats(0, CT)
            with dve.Fori(2, CH) as ch:
                c.loop(ch - 2, 2)
                combine(1, ch - 1, CT)
                message(1, ch, CN, x1_ready)
                row_stats(ch - 1, CT)
            c.end(CH - 2)
            combine(1, CH - 1, CT)
            message(1, CH, TN, x1_ready)
            row_stats(CH - 1, CT)
            combine(1, CH, 1)
            dve.wait_ge(x1_ready, T)
            row_stats(CH, 1)

            dve.wait_ge(stats2_ready, T)
            dve.wait_ge(agg_done[1][1], CH + 1)
            s2 = stats2[0:TN]
            c.link(dve.tensor_tensor(mean2, s2[:, :, 1], s2[:, :, 4], ALU.add))
            c.link(dve.tensor_tensor(half2, s2[:, :, 1], s2[:, :, 4], ALU.subtract))
            c.link(dve.tensor_tensor(var2, s2[:, :, 2], s2[:, :, 5], ALU.add))
            c.link(dve.tensor_scalar(mean2, mean2, 0.5, None, ALU.mult))
            c.link(dve.tensor_tensor(half2, half2, half2, ALU.mult))
            c.link(dve.tensor_scalar(var2, var2, 1.0 / C, EPS_LN, ALU.mult, ALU.add))
            dve.scalar_tensor_tensor(out=var2, in0=half2, scalar=0.25, in1=var2, op0=ALU.mult, op1=ALU.add).then_inc(var2_ready, 1)
            dve.wait_ge(std2_ready, 1)
            c.link(dve.reciprocal(rstd2, std2))

            def normed(t, j, first, loads):
                dve.wait_ge(f_loaded[j], 16 * loads)
                if not first:
                    dve.wait_ge(s_done, t - R + 1)
                dve.tensor_scalar(f_xn[:, j, 0:C], f_in[:, j, :], mean2[:, bass.ds(t, 1)],
                                  rstd2[:, bass.ds(t, 1)], ALU.subtract, ALU.mult).then_inc(f_xn_ready, 1)

            def softmax(t, j, first):
                bank = ps[0:TN, 4 if j % 2 == 0 else 7, :].rearrange("p (h g) -> p h g", h=H)
                e = f_e[:, j, :].rearrange("p (h g) -> p h g", h=H)
                dve.wait_ge(lg_done, t + 1)
                c.link(dve.tensor_reduce(f_mx[:, j, :], bank, AX_X, ALU.max))
                if not first:
                    dve.wait_ge(fw_ready, t - R + 1)
                dve.tensor_tensor(e, bank, f_mx[:, j, :].unsqueeze(2).to_broadcast([TN, H, G]), ALU.subtract).then_inc(sub_ready, 1)

            def sums(t, j):
                e = f_e[:, j, :].rearrange("p (h g) -> p h g", h=H)
                dve.wait_ge(exp_ready, t + 1)
                c.link(dve.tensor_reduce(f_sm[:, j, :], e, AX_X, ALU.add))
                dve.reciprocal(f_rs[:, j, :], f_sm[:, j, :]).then_inc(rs_ready, 1)

            normed(0, 0, True, 1)
            for t in range(R):
                if t + 1 < R:
                    normed(t + 1, t + 1, True, 1)
                else:
                    normed(t + 1, 0, False, 2)
                softmax(t, t, True)
                sums(t, t)
            with dve.Fori(1, CH) as i:
                c.loop(i - 1, 2 * R)
                for j in range(R):
                    normed(R * i + j + 1, (j + 1) % R, False, i + 1 + (j + 1) // R)
                    softmax(R * i + j, j, False)
                    sums(R * i + j, j)
            c.end(CH - 1)
            softmax(LAST, 0, False)
            sums(LAST, 0)

            dve.wait_ge(s_done, T)
            c.link(dve.tensor_scalar(sn_e, ps[:, 0:PAIRS, C], EPS_SLICE, None, ALU.add))
            c.link(dve.reciprocal(sn_inv, sn_e))
            for k in range(PAIRS):
                last = dve.tensor_scalar(s_sb[:, k, 0:C + 1], ps[:, k, 0:C + 1], sn_inv[:, k:k + 1], None, ALU.mult)
            last.then_inc(mid_dve, 1)
            dve.wait_ge(mid_pe, 1)
            dve.tensor_copy(sT[:, 1, :], ps[:, 5, :])
            dve.tensor_copy(nr, ps[0:1, 6, :]).then_inc(mid_dve, 1)
            dve.wait_ge(mid_pe, 2)
            dve.tensor_copy(tokT, ps[0:D, 7, :]).then_inc(mid_dve, 1)
            dve.wait_ge(mid_pe, 4)
            dve.tensor_copy(kT, ps[0:D, 5, :]).then_inc(mid_dve, 1)
            dve.wait_ge(mid_pe, 6)
            sc = ps[0:G, 7, :].rearrange("p (h g) -> p h g", h=H)
            c.link(dve.tensor_reduce(am, sc, AX_X, ALU.max))
            dve.tensor_tensor(a_e, sc, am.unsqueeze(2).to_broadcast([G, H, G]), ALU.subtract).then_inc(mid_dve, 1)
            dve.wait_ge(mid_act, 4)
            c.link(dve.tensor_reduce(a_s, a_e, AX_X, ALU.add))
            c.link(dve.reciprocal(a_r, a_s))
            dve.tensor_tensor(a_w, a_e, a_r.unsqueeze(2).to_broadcast([G, H, G]), ALU.mult).then_inc(mid_dve, 1)
            dve.wait_ge(mid_pe, 7)
            dve.tensor_copy(aT, ps[0:G, 4, :]).then_inc(mid_dve, 1)
            dve.wait_ge(mid_pe, 8)
            dve.tensor_copy(osT, ps[0:D, 5, :]).then_inc(mid_dve, 1)
            dve.wait_ge(mid_pe, 9)
            for b in range(2):
                dve.tensor_copy(t_sb[:, 2 * b:2 * b + 2, :].rearrange("p k c -> p (k c)"), ps[:, 6 + b, :]).then_inc(mid_dve, 1)

            def stage(t, par, first):
                if not first:
                    dve.wait_ge(y_done, t - 1)
                dve.tensor_copy(w_st[:, par], w_tr[:, :, bass.ds(TN * t, TN)]).then_inc(w_st_ready, 1)

            def finish(t, par, stores, loads):
                dve.wait_ge(y_done, t + 1)
                dve.wait_ge(y_loaded[par], 16 * loads)
                if not isinstance(t, int) or t >= 2:
                    dve.wait_ge(y_stored[par], 16 * stores)
                dve.tensor_tensor(y_o[:, par, :], ps[0:TN, par, 0:C], y_in[:, par, :], ALU.add).then_inc(y_ready, 1)

            dve.wait_ge(wT_ready, T)
            stage(0, 0, True)
            stage(1, 1, True)
            finish(0, 0, 0, 1)
            stage(2, 0, False)
            finish(1, 1, 0, 1)
            with dve.Fori(0, (T - 3) // 2) as i:
                stage(2 * i + 3, 1, False)
                finish(2 * i + 2, 0, i + 1, i + 2)
                stage(2 * i + 4, 0, False)
                finish(2 * i + 3, 1, i + 1, i + 2)
            finish(T - 1, 0, (T - 1) // 2, (T + 1) // 2)


def kernel(**inputs):
    import numpy as np
    import concourse.bacc as bacc
    from concourse.bass_utils import run_bass_kernel_spmd as run

    nc = bacc.Bacc("TRN2", target_bir_lowering=False, num_devices=1)
    arrays, args = {}, {}

    def give(name, a):
        a = np.ascontiguousarray(a)
        arrays[f"in_{name}"] = a
        args[name] = nc.dram_tensor(f"in_{name}", a.shape, mybir.dt.from_np(a.dtype), kind="ExternalInput").ap()

    for name in ("x", "src", "dst"):
        give(name, inputs[name])
    for name in ("W_proj1", "b_proj1", "W_l1", "b_l1", "W_r1", "W_proj2", "b_proj2", "W_l2", "b_l2", "W_r2"):
        give(name.replace("W_proj", "Wp").replace("b_proj", "bp").replace("W_l", "Wl").replace("b_l", "bl").replace("W_r", "Wr"),
             inputs["L0_gnn_" + name])
    for name in ("W_fx", "b_fx", "W_slice", "b_slice", "W_q", "W_k", "W_v", "W_out", "b_out", "temperature"):
        give(name, inputs["L0_ffn_" + name])
    wx, bx = np.asarray(inputs["L0_ffn_W_x"]), np.asarray(inputs["L0_ffn_b_x"])
    heads = inputs["L0_ffn_temperature"].shape[1]
    give("W_xT", wx.reshape(wx.shape[0], heads, -1).transpose(2, 1, 0))
    give("b_xT", bx.reshape(heads, -1).T)
    out = nc.dram_tensor("out_0", inputs["x"].shape, F32, kind="ExternalOutput").ap()
    bass_gnn_ffn_kernel(nc, out=out, **args)
    r = run(nc, [arrays], core_ids=[0])
    return r.results[0]["out_0"]
```

```python
from contextlib import ExitStack

import concourse.bass as bass
from concourse import mybir

ALU = mybir.AluOpType
ACT = mybir.ActivationFunctionType
AX_X = mybir.AxisListType.X
F32 = mybir.dt.float32
F16 = mybir.dt.float16
I32 = mybir.dt.int32
U32 = mybir.dt.uint32

P = 128
C = 256
KC = C // P


class Chain:

    def __init__(self, eng, sem):
        self.eng, self.sem, self.n, self.done = eng, sem, 0, 0

    def link(self, ins):
        ins.then_inc(self.sem, 1)
        self.n += 1
        self.eng.wait_ge(self.sem, self.done + self.n)

    def loop(self, passes, per):
        self.done = passes * per
        self.start, self.per = self.n, per

    def end(self, passes):
        assert self.n == self.start + self.per, (self.n - self.start, self.per)
        self.n, self.done = self.start + passes * self.per, 0


def bass_gnn_ffn_kernel(nc, x, src, dst, Wp1, bp1, Wl1, bl1, Wr1, Wp2, bp2, Wl2, bl2, Wr2,
                        W_fx, b_fx, W_xT, b_xT, W_slice, b_slice, W_q, W_k, W_v, W_out, b_out,
                        temperature, out):
    N = x.shape[0]
    E = src.shape[0]
    TN = 125
    T = N // TN
    D5 = 5
    Q = N // D5
    WIN = P
    COARSE = 512
    ROW = E // TN
    KEYS = T * D5
    CT = 4
    CN = CT * TN
    CH = T // CT
    H, G = temperature.shape[1], W_slice.shape[1]
    D = W_slice.shape[0]
    INNER = H * D
    EPS_LN, EPS_NORM, EPS_SLICE = 1e-5, 1e-12, 1e-5
    SCALE = D ** -0.5
    assert T * TN == N and Q * D5 == N and ROW * TN == E and CH * CT + 1 == T and TN == 5 * T
    assert C == 2 * P and H * G == 4 * P and D == 64 and G == 64

    SUB = 4
    GC = CN // D5 // SUB
    GROUPS = CH * GC + TN // D5 // SUB + 1
    assert GC * SUB * D5 == CN and (GROUPS - 1) * SUB + 1 == Q and GC == T
    OH_SLOT = [q % 3 for q in range(GC - 1)] + [1]
    OH_AGE = [4, 2, 4] + [3] * (GC - 4) + [2]
    BANK = [2 + q % 2 for q in range(GC)]
    BANK_AGE = [1, 3] + [2] * (GC - 2)
    LEAD = 10
    TURN_AT, PROJECT_AT, WL_AT = 14, 18, 23
    LAST_AT = [8, 12, 16, 21]
    EARLY = T - 6
    EARLY_GROUPS = {n: [g for g in range(LEAD) if g * (T + 2 - EARLY) // LEAD == n - EARLY] for n in range(EARLY, T + 2)}
    HG = H * G
    PAIRS = HG // P
    R = 4
    RG = 5
    ROUNDS = ROW // RG
    GT = 5
    assert ROUNDS * RG == ROW and E % N == 0 and T % GT == 0
    g_sum_dram = nc.dram_tensor("g_sum_scratch", (T, TN, 2 * C), F32, kind="Internal").ap()
    g_y_dram = nc.dram_tensor("g_y_scratch", (N, 2 * C), F16, kind="Internal").ap()
    wxs_dram = nc.dram_tensor("wxs_scratch", (P, KC, HG), F32, kind="Internal").ap()
    bxs_dram = nc.dram_tensor("bxs_scratch", (1, HG), F32, kind="Internal").ap()
    xr2_dram = nc.dram_tensor("xr2_scratch", (T, TN, C), F32, kind="Internal").ap()
    xr_dram = nc.dram_tensor("xr_scratch", (T, TN, C), F32, kind="Internal").ap()
    xp_dram = nc.dram_tensor("xp_scratch", (N, 2 * C), F16, kind="Internal").ap()
    x1_dram = nc.dram_tensor("x1_scratch", (T, TN, C), F32, kind="Internal").ap()
    cnt_dram = nc.dram_tensor("cnt_scratch", (N,), F32, kind="Internal").ap()
    x_t = x.rearrange("(t p) c -> t p c", p=TN)
    out_t = out.rearrange("(t p) c -> t p c", p=TN)
    xp_t = xp_dram.rearrange("(t p) c -> t p c", p=TN)

    with ExitStack() as ctx:
        def sb(name, shape, dt=F32):
            return ctx.enter_context(nc.sbuf_tensor(name, shape, dt))

        def sem(name):
            return ctx.enter_context(nc.semaphore(name))

        adj = sb("adj", [P, T, N + 1], F16)
        adj_words = T * (N + 1) // 2
        y = sb("y", [P, T, 2 * C], F16)
        ps = ctx.enter_context(nc.psum_tensor("ps", [P, 8, 512], F32))
        ident = sb("ident", [P, P])
        wp = sb("wp", [P, KC, C])
        wr = sb("wr", [P, KC, C])
        wl = sb("wl", [P, KC, C])
        bias_p = sb("bias_p", [P, KC])
        bias_l = sb("bias_l", [P, C])
        rcnt = sb("rcnt", [P, T])
        covered = sb("covered", [1, 2], I32)
        stats2 = sb("stats2", [P, T, 6])
        key_t = sb("key_t", [P, Q + 3], F16)
        low_t = sb("low_t", [P, Q + 3], F16)
        work_words = 4864
        work = sb("work", [P, work_words])

        class Region:

            def __init__(self, base, limit):
                self.base, self.at, self.limit = base, 0, limit

            def take(self, shape, dt=F32):
                n = 1
                for s in shape[1:]:
                    n *= s
                words = n if dt in (F32, I32) else (n + 1) // 2
                words = (words + 1) // 2 * 2
                assert self.at + words <= self.limit, (self.at + words, self.limit)
                v = self.base[:, self.at:self.at + words]
                self.at += words
                if dt != F32:
                    v = v.bitcast(dt)
                v = v[0:shape[0], 0:n]
                names = "abcd"[:len(shape) - 1]
                sizes = dict(zip(names[1:], shape[2:]))
                return v.rearrange(f"p ({' '.join(names)}) -> p {' '.join(names)}", **sizes) if len(shape) > 2 else v

        def over_adj():
            return Region(adj[:, :, :].rearrange("p a b -> p (a b)")[:, 0:2 * adj_words].bitcast(F32), adj_words)

        def over_work():
            return Region(work[:, :], work_words)

        r = over_adj()
        ones = r.take([P, P])
        rows = r.take([TN, ROW], I32)
        thr = r.take([TN, TN])
        base5 = r.take([TN, 5])
        own = r.take([TN, T])
        rowmax = r.take([TN, 1])
        step = r.take([TN, TN])
        r0 = r.take([TN, 1])
        r0_i = r.take([TN, 1], I32)
        picked = r.take([TN, ROW], I32)
        picked_f = r.take([TN, ROW])
        junk = r.take([TN, ROW])
        below = r.take([TN, 1])
        start = r.take([TN, 1])
        start_c = r.take([TN, 1])
        start_i = r.take([TN, 1], I32)
        coarse = r.take([TN, COARSE], I32)
        coarse_f = r.take([TN, COARSE])
        below5 = r.take([TN, 5])
        start5 = r.take([TN, 5])
        start5_i = r.take([TN, 5, 8], I32)
        win_d = r.take([TN, 5, WIN], I32)
        win_s = r.take([TN, 5, WIN], I32)
        hi_i = r.take([TN, 5, WIN], I32)
        low_f = r.take([TN, 5, WIN])
        win_f = r.take([TN, 5, WIN])
        dl = r.take([TN, 5, WIN])
        ge0 = r.take([TN, 5, WIN])
        valid = r.take([TN, 5, WIN])
        pair_f = r.take([TN, 5, WIN])
        key_f = r.take([TN, 5, WIN])
        junk25 = r.take([TN, T, WIN], F16)
        junk5 = r.take([TN, 5, COARSE], F16)
        cnt = r.take([TN, T])
        cnt_row = r.take([TN, 1])
        wxT = r.take([D, H, C])
        wsl = r.take([D, G])
        bxT = r.take([D, H])
        bsl = r.take([1, G])
        temp = r.take([1, H])
        rtemp = r.take([1, H])
        rtemp_row = r.take([1, H, G])
        rtemp_all = r.take([P, HG])
        wxs_o = r.take([P, KC, HG])
        bxs_t = r.take([1, H, G])
        bxs_o = r.take([1, H, G])

        r = over_work()
        o_t = r.take([TN, CT, C])
        x_in, xn = o_t[:, 0:2], o_t[:, 2:4]
        hT = r.take([P, 2, KC, TN])
        xpT = r.take([P, 2, KC, TN])
        xr_o = r.take([TN, 2, C])
        y_half = r.take([TN, 2, 2 * C], F16)
        mv = r.take([TN, 2, 2])
        st6 = r.take([TN, 6])
        std = r.take([TN, 2])
        rstd = r.take([TN, 1])
        eps = r.take([TN, 1])
        ss = r.take([TN, CT])
        nrm = r.take([TN, CT])
        inv = r.take([TN, CT])
        mark = r.at
        iota_low = r.take([P, P, 2], F16)
        iota_key = r.take([P, KEYS, 2], F16)
        oh_low = r.take([P, 3 * SUB // 2, P, 2], F16)
        oh_key = r.take([P, 3 * SUB // 2, KEYS, 2], F16)
        r.at = mark
        x_res = r.take([TN, CT, C])

        r = over_adj()
        g_src = r.take([TN, ROW + 1], I32)
        g_dst_i = r.take([TN, ROW], I32)
        g_dst = r.take([TN, ROW])
        g_rel = r.take([TN, ROW])
        g_iota = r.take([TN, GT * TN], F16)
        g_idx = r.take([TN, RG, 2], I32)
        g_rows = r.take([TN, RG, 2 * C], F16)
        g_oh = r.take([TN, RG, GT * TN], F16)
        g_sum = r.take([TN, GT, 2 * C])
        g_all_i = r.take([TN, N], I32)
        g_all = r.take([TN, N])
        g_eq = r.take([TN, N])
        g_node = r.take([TN, T])
        g_part = r.take([TN, T])
        g_cnt = r.take([TN, T])
        g_ring = y[:, :, :].rearrange("p t c -> p (t c)")[:, 0:CT * 4 * C].bitcast(F32).rearrange("p (j c) -> p j c", j=CT)

        r = over_adj()
        w_tr = r.take([P, PAIRS, N])
        f_ones_row = r.take([1, TN])
        f_in = r.take([TN, R, C])
        f_xn = r.take([TN, R, C + 8])
        f_xT = r.take([P, R, KC, TN])
        f_e = r.take([TN, R, HG])
        f_w = r.take([TN, R, HG])
        f_mx = r.take([TN, R, H])
        f_sm = r.take([TN, R, H])
        f_rs = r.take([TN, R, H])
        var2 = r.take([TN, T])
        mean2 = r.take([TN, T])
        half2 = r.take([TN, T])
        std2 = r.take([TN, T])
        rstd2 = r.take([TN, T])
        wxs = r.take([P, KC, HG])
        bxs = r.take([1, HG])
        wfx = r.take([P, KC, INNER])
        bfx = r.take([1, INNER])
        wq = r.take([D, D])
        wk = r.take([D, D])
        wv = r.take([D, D])
        wo = r.take([D, H, C])
        bo = r.take([1, C])
        sn_e = r.take([P, PAIRS])
        sn_inv = r.take([P, PAIRS])
        s_sb = r.take([P, PAIRS, C + 8])
        sT = r.take([P, KC, HG])
        nr = r.take([1, HG])
        tokT = r.take([D, HG])
        qT = r.take([D, HG])
        kT = r.take([D, HG])
        v_sb = r.take([G, HG])
        am = r.take([G, H])
        a_e = r.take([G, H, G])
        a_s = r.take([G, H])
        a_r = r.take([G, H])
        a_w = r.take([G, H, G])
        aT = r.take([G, HG])
        osT = r.take([D, HG])
        t_sb = r.take([P, PAIRS, C])
        w_st = r.take([P, 2, PAIRS, TN])
        y_in = r.take([TN, 2, C])
        y_o = r.take([TN, 2, C])
        assert PAIRS == 4

        consts, dve_consts = sem("consts"), sem("dve_consts")
        rows_in, weights_in, fold_in = sem("rows_in"), sem("weights_in"), sem("fold_in")
        step_ready, r0_done, r0_ready, row_in = sem("step_ready"), sem("r0_done"), sem("r0_ready"), sem("row_in")
        start_ready, coarse_in, fine_ready = sem("start_ready"), sem("coarse_in"), sem("fine_ready")
        win_in = [sem(f"win_in{i}") for i in range(5)]
        keys_ready, turned, tables_ready = sem("keys_ready"), sem("turned"), sem("tables_ready")
        rt_row, rt_done, rt_ready, fold_done, fold_ready, fold_stored = (sem(n) for n in (
            "rt_row", "rt_done", "rt_ready", "fold_done", "fold_ready", "fold_stored"))
        cnt_out, cnt_in, rcnt_ready = sem("cnt_out"), sem("cnt_in"), sem("rcnt_ready")
        cnt_rows_ready, total_done, covered_ready = sem("cnt_rows_ready"), sem("total_done"), sem("covered_ready")
        g_tables_in, g_y_out, g_iota_ready, g_node_ready = (sem(n) for n in ("g_tables_in", "g_y_out", "g_iota_ready", "g_node_ready"))
        g_dst_ready, g_all_in, g_all_used, g_steps = (sem(n) for n in ("g_dst_ready", "g_all_in", "g_all_used", "g_steps"))
        g_free, g_idx_ready, g_oh_ready, g_rel_ready = (sem(n) for n in ("g_free", "g_idx_ready", "g_oh_ready", "g_rel_ready"))
        g_in = [sem(f"g_in{j}") for j in range(RG)]
        g_swept, g_sum_ready, g_sum_out = sem("g_swept"), sem("g_sum_ready"), sem("g_sum_out")
        g_sum_in = [sem(f"g_sum_in{j}") for j in range(CT)]
        oh_ready, built, stored = sem("oh_ready"), sem("built"), sem("adj_stored")
        x_loaded = [sem(f"x_loaded{i}") for i in range(2)]
        mv_ready, std_ready, xn_ready, h_ready = (sem(n) for n in ("mv_ready", "std_ready", "xn_ready", "h_ready"))
        x_turned, hT_ready, xpT_done, xpT_ready, xr_done, xr_ready, y_done, hi_ready, lo_ready = (
            [sem(f"{n}{k}") for k in range(2)] for n in (
                "x_turned", "hT_ready", "xpT_done", "xpT_ready", "xr_done", "xr_ready", "y_done", "hi_ready", "lo_ready"))
        xr_stored = [[sem(f"xr_stored{k}_{j}") for j in range(2)] for k in range(2)]
        y_half_stored = [sem(f"y_half_stored{j}") for j in range(2)]
        dve_steps, act_steps, pool_steps = sem("dve_steps"), sem("act_steps"), sem("pool_steps")
        agg_done, o_ready, sq_done, nrm_ready = ([sem(f"{n}{k}") for k in range(2)] for n in (
            "agg_done", "o_ready", "sq_done", "nrm_ready"))
        xr_loaded = [[sem(f"xr_loaded{k}_{j}") for j in range(CT)] for k in range(2)]
        res_loaded = [sem(f"res_loaded{j}") for j in range(CT)]
        w2_in = sem("w2_in")
        y_in2 = [sem(f"y_in{j}") for j in range(3)]
        x1_ready, stats2_ready = sem("x1_ready"), sem("stats2_ready")
        x1_stored = [sem(f"x1_stored{j}") for j in range(CT)]
        var2_ready, std2_ready, slice_w_in, mid_w_in, f_ones = (sem(n) for n in (
            "var2_ready", "std2_ready", "slice_w_in", "mid_w_in", "f_ones"))
        f_loaded = [sem(f"f_loaded{j}") for j in range(R)]
        f_xn_ready, f_xt_done, f_xT_ready, lg_done, sub_ready, exp_ready, rs_ready, fw_ready, s_done, wT_done, wT_ready = (
            sem(n) for n in ("f_xn_ready", "f_xt_done", "f_xT_ready", "lg_done", "sub_ready", "exp_ready", "rs_ready",
                             "fw_ready", "s_done", "wT_done", "wT_ready"))
        mid_pe, mid_dve, mid_act = sem("mid_pe"), sem("mid_dve"), sem("mid_act")
        out_in = [sem(f"out_in{j}") for j in range(2)]
        out_stored = [sem(f"out_stored{j}") for j in range(2)]
        w_st_ready, out_done, out_ready = sem("w_st_ready"), sem("out_done"), sem("out_ready")

        block = ctx.enter_context(nc.Block())
        LAST = T - 1

        @block.sync
        def _(sp):
            def load_x(t, par):
                sp.dma_start(x_in[:, par, :], x_t[bass.ds(t, 1)].rearrange("a p c -> p (a c)")).then_inc(x_loaded[par], 16)

            def store_xr(n, par):
                sp.wait_ge(xr_ready[0], n + 1)
                sp.dma_start(xr_dram[bass.ds(n, 1)].rearrange("a p c -> p (a c)"), xr_o[:, par, :]).then_inc(xr_stored[0][par], 16)

            def load_layer(Wp, Wr, Wl, bp, bl, done):
                for w, d in ((wp, Wp), (wr, Wr), (wl, Wl)):
                    sp.dma_start(w[:, :, :], d.rearrange("(k p) c -> p k c", p=P)).then_inc(done, 16)
                sp.dma_start(bias_p[:, :], bp.rearrange("(k p) -> p k", p=P), allow_slow_non_contiguous=True).then_inc(done, 16)
                sp.dma_start(bias_l[:, :], bl.rearrange("(a c) -> a c", a=1).to_broadcast([P, C])).then_inc(done, 16)

            sp.dma_start(rows, dst.rearrange("(p k) -> p k", k=ROW)).then_inc(rows_in, 16)
            load_x(0, 0)
            load_x(1, 1)
            load_layer(Wp1, Wr1, Wl1, bp1, bl1, weights_in)
            sp.dma_start(temp, temperature.rearrange("a h b c -> a (h b c)")).then_inc(fold_in, 16)
            sp.dma_start(wxT, W_xT).then_inc(fold_in, 16)
            sp.dma_start(wsl, W_slice).then_inc(fold_in, 16)
            sp.dma_start(bxT, b_xT).then_inc(fold_in, 16)
            sp.dma_start(bsl, b_slice.rearrange("(a g) -> a g", a=1)).then_inc(fold_in, 16)
            sp.wait_ge(xn_ready, 1)
            load_x(2, 0)
            sp.wait_ge(xn_ready, 2)
            load_x(3, 1)
            sp.wait_ge(xn_ready, 3)
            load_x(4, 0)
            store_xr(0, 0)

            def load_and_store(i, par):
                t, m = 2 * i + 6 - par, 2 * i + 2 - par
                sp.wait_ge(xn_ready, 2 * i + 5 - par)
                load_x(t, par)
                store_xr(m, par)

            with sp.Fori(0, 2) as i:
                load_and_store(i, 1)
                load_and_store(i, 0)
            sp.wait_ge(fold_ready, 2)
            sp.dma_start(wxs_dram, wxs_o).then_inc(fold_stored, 16)
            sp.dma_start(bxs_dram, bxs_o.rearrange("a h g -> a (h g)")).then_inc(fold_stored, 16)
            with sp.Fori(2, 7) as i:
                load_and_store(i, 1)
                load_and_store(i, 0)
            sp.wait_ge(cnt_rows_ready, 1)
            sp.dma_start(cnt_dram.rearrange("(p c) -> p c", c=T), cnt).then_inc(cnt_out, 16)
            with sp.Fori(7, (T - 5) // 2) as i:
                load_and_store(i, 1)
                load_and_store(i, 0)
            for m in range(T - 4, T):
                store_xr(m, m % 2)
            sp.wait_ge(cnt_out, 16)
            sp.dma_start(rcnt[0:TN, :], cnt_dram.rearrange("(t p) -> p t", p=TN), allow_slow_non_contiguous=True).then_inc(cnt_in, 16)

            def load_xr(k, n, j, first, chunk=0):
                if not first:
                    if k == 0:
                        sp.wait_ge(x_turned[1], n - CT + 1)
                    else:
                        sp.wait_ge(x1_stored[j], 16 * chunk)
                sp.dma_start(o_t[:, j, :], (xr_dram, xr2_dram)[k][bass.ds(n, 1)].rearrange("a p c -> p (a c)")).then_inc(xr_loaded[k][j], 16)

            sp.wait_ge(x_turned[0], T)
            sp.wait_ge(xn_ready, T)
            sp.wait_ge(xr_stored[0][0], 16 * (T // 2 + 1))
            sp.wait_ge(xr_stored[0][1], 16 * (T // 2))
            for j in range(CT):
                load_xr(0, j, j, True)
            sp.wait_ge(y_done[0], T)
            sp.wait_ge(xr_done[0], T)
            sp.wait_ge(xr_ready[0], T)
            sp.wait_ge(xpT_ready[0], T)
            load_layer(Wp2, Wr2, Wl2, bp2, bl2, w2_in)
            with sp.Fori(1, CH) as ch:
                for j in range(CT):
                    load_xr(0, CT * ch + j, j, False)
            load_xr(0, LAST, 0, False)

            sp.wait_ge(agg_done[0], T)
            y_all = xp_dram.rearrange("(t p) c -> p t c", p=TN)
            for piece in range(3):
                for j in range(2):
                    sp.wait_ge(y_half_stored[j], 16 * 4 * (piece + 1))
                sp.dma_start(y[0:TN, 8 * piece:8 * piece + 8, :], y_all[:, 8 * piece:8 * piece + 8, :]).then_inc(y_in2[piece], 16)

            def load_res(n, j, first):
                if not first:
                    sp.wait_ge(x1_ready, n - CT + 1)
                sp.dma_start(x_res[:, j, :], x_t[bass.ds(n, 1)].rearrange("a p c -> p (a c)")).then_inc(res_loaded[j], 16)

            for j in range(CT):
                load_res(j, j, True)
            sp.wait_ge(xr_stored[1][1], 16 * (T // 2))
            for j in range(1, CT):
                load_xr(1, j, j, True)
            sp.wait_ge(xr_stored[1][0], 16 * (T // 2 + 1))
            sp.wait_ge(x_turned[1], T)
            load_xr(1, 0, 0, True)
            with sp.Fori(1, CH) as ch:
                for j in range(CT):
                    load_xr(1, CT * ch + j, j, False, ch)
                    load_res(CT * ch + j, j, False)
            load_xr(1, LAST, 0, False, CH)
            load_res(LAST, 0, False)

            sp.wait_ge(agg_done[1], T)
            sp.wait_ge(fold_stored, 32)
            sp.dma_start(wxs, wxs_dram).then_inc(slice_w_in, 16)
            sp.dma_start(bxs, bxs_dram).then_inc(slice_w_in, 16)

            def load_f(t, j, first):
                if not first:
                    sp.wait_ge(f_xn_ready, t - R + 1)
                sp.dma_start(f_in[:, j, :], x1_dram[bass.ds(t, 1)].rearrange("a p c -> p (a c)")).then_inc(f_loaded[j], 16)

            for j in range(CT):
                sp.wait_ge(x1_stored[j], 16 * CH)
                load_f(j, j, True)
            sp.dma_start(wfx, W_fx.rearrange("(k p) c -> p k c", p=P)).then_inc(mid_w_in, 16)
            sp.dma_start(bfx, b_fx.rearrange("(a c) -> a c", a=1)).then_inc(mid_w_in, 16)
            for w, d in ((wq, W_q), (wk, W_k), (wv, W_v)):
                sp.dma_start(w, d).then_inc(mid_w_in, 16)
            sp.dma_start(wo, W_out.rearrange("(h d) c -> d h c", d=D)).then_inc(mid_w_in, 16)
            sp.dma_start(bo, b_out.rearrange("(a c) -> a c", a=1)).then_inc(mid_w_in, 16)
            with sp.Fori(1, CH) as ch:
                for j in range(R):
                    load_f(R * ch + j, j, False)
            sp.wait_ge(x1_stored[0], 16 * (CH + 1))
            load_f(LAST, 0, False)

            def load_out(t, par, first):
                if not first:
                    sp.wait_ge(out_ready, t - 1)
                sp.dma_start(y_in[:, par, :], x1_dram[bass.ds(t, 1)].rearrange("a p c -> p (a c)")).then_inc(out_in[par], 16)

            load_out(0, 0, True)
            load_out(1, 1, True)
            load_out(2, 0, False)
            with sp.Fori(0, (T - 3) // 2) as i:
                load_out(2 * i + 3, 1, False)
                load_out(2 * i + 4, 0, False)

        @block.gpsimd
        def _(pool):
            ch_ = Chain(pool, pool_steps)
            small = dict(allow_small_or_imprecise_dtypes=True)
            ch_.link(pool.memset(ones, 1.0))
            pool.iota(thr, [[T, TN]], base=0, channel_multiplier=0, **small).then_inc(consts, 1)
            pool.iota(base5, [[D5, 5]], base=0, channel_multiplier=T, **small)
            pool.iota(own, [[1, T]], base=0, channel_multiplier=T, **small).then_inc(consts, 1)
            pool.affine_select(out=ident[:, :], in_=ones, compare_op=ALU.is_equal, fill=0.0, base=0,
                               pattern=[[-1, P]], channel_multiplier=1).then_inc(consts, 1)
            pool.iota(iota_low, [[1, P], [0, 2]], base=0, channel_multiplier=0, **small)
            pool.iota(iota_key, [[1, KEYS], [0, 2]], base=1, channel_multiplier=0, **small)
            pool.memset(key_t[:, Q:Q + 3], 0.0)
            pool.memset(eps, EPS_LN)
            pool.memset(low_t[:, Q:Q + 3], 0.0).then_inc(consts, 1)

            pool.wait_ge(r0_ready, 1)
            pool.indirect_dma_start(picked, None, dst.rearrange("(p k) -> p k", k=ROW),
                                    bass.IndirectOffsetOnAxis(ap=r0_i.bitcast(U32), axis=0)).then_inc(row_in, 16)
            dst_1, src_1 = dst.rearrange("(e a) -> e a", a=1), src.rearrange("(e a) -> e a", a=1)
            pool.wait_ge(start_ready, 1)
            pool.indirect_dma_start(coarse, None, dst_1,
                                    bass.IndirectOffsetOnAxis(ap=start_i.bitcast(U32), axis=0)).then_inc(coarse_in, 16)
            pool.wait_ge(fine_ready, 1)
            for i in range(5):
                at = bass.IndirectOffsetOnAxis(ap=start5_i[:, i, 0:1].bitcast(U32), axis=0)
                pool.indirect_dma_start(win_d[:, i, :], None, dst_1, at).then_inc(win_in[i], 16)
                pool.indirect_dma_start(win_s[:, i, :], None, src_1, at).then_inc(win_in[i], 16)

            def general_tables(k):
                pool.dma_start(g_src[:, 0:ROW], src.rearrange("(p k) -> p k", k=ROW)).then_inc(g_tables_in, 16)
                pool.dma_start(g_dst_i, dst.rearrange("(p k) -> p k", k=ROW)).then_inc(g_tables_in, 16)
                pool.iota(g_iota, [[1, GT * TN]], base=0, channel_multiplier=0, **small).then_inc(g_iota_ready, 1)
                pool.wait_ge(g_tables_in, 32 * (k + 1))
                pool.tensor_copy(g_src[:, ROW:ROW + 1], g_src[:, 0:1]).then_inc(g_idx_ready, 1)
                pool.tensor_copy(g_idx[:, 0, 0:1], g_src[:, 0:1]).then_inc(g_idx_ready, 1)

            pool.wait_ge(covered_ready, 1)
            is_covered = pool.value_load(covered[0:1, 0:1], min_val=0, max_val=1)
            with pool.If(is_covered == 1):
                pool.nop()
            with pool.Else():
                pool.wait_ge(lo_ready[0], T)
                pool.wait_ge(stored, LEAD)
                pool.wait_ge(cnt_out, 16)
                pool.wait_ge(fold_stored, 32)
                pool.wait_ge(total_done, 1)
                general_tables(0)
                pool.dma_start(g_y_dram.rearrange("(t p) c -> p t c", p=TN), y[0:TN, :, :]).then_inc(g_y_out, 16)
                pool.iota(g_node, [[TN, T]], base=0, channel_multiplier=1, **small).then_inc(g_node_ready, 1)
                pieces = dst.rearrange("(s n) -> s n", n=N)
                pool.dma_start(g_all_i, pieces[0:1].to_broadcast([TN, N])).then_inc(g_all_in, 16)
                with pool.Fori(1, E // N) as s_:
                    pool.wait_ge(g_all_used, s_)
                    pool.dma_start(g_all_i, pieces[bass.ds(s_, 1)].to_broadcast([TN, N])).then_inc(g_all_in, 16)
                pool.wait_ge(g_y_out, 16)
            pool.nop()

            def general_gathers(k):
                table = g_y_dram if k == 0 else xp_dram

                def sweep(s_):
                    chunk = (T // GT) * k + s_

                    def group(i, slot):
                        u = ROW * chunk + RG * i + slot
                        pool.wait_ge(g_free, u + 2)
                        pool.wait_ge(g_idx_ready, u + 2 * k + 2)
                        pool.tensor_copy(g_idx[:, (slot + 1) % RG, 0:1], g_src[:, bass.ds(RG * i + slot + 1, 1)]
                                         ).then_inc(g_idx_ready, 1)
                        pool.indirect_dma_start(g_rows[:, slot, :], None, table,
                                                bass.IndirectOffsetOnAxis(ap=g_idx[:, slot, 0:1].bitcast(U32), axis=0)
                                                ).then_inc(g_in[slot], 16)

                    with pool.Fori(0, ROUNDS) as i:
                        for slot in range(RG):
                            group(i, slot)
                    pool.wait_ge(g_sum_ready, chunk + 1)
                    pool.dma_start(g_sum_dram[bass.ds(GT * s_, GT)].rearrange("t p c -> p t c"), g_sum).then_inc(g_sum_out, 16)

                with pool.If(is_covered == 1):
                    pool.nop()
                with pool.Else():
                    if k:
                        pool.wait_ge(stored, GROUPS)
                        pool.wait_ge(agg_done[0], T)
                        general_tables(1)
                    with pool.Fori(0, T // GT) as s_:
                        sweep(s_)
                    pool.wait_ge(g_sum_out, 16 * (T // GT) * (k + 1))
                pool.nop()

            def general_sums_back(k, ch, tiles):
                with pool.If(is_covered == 1):
                    pool.nop()
                with pool.Else():
                    for j in range(tiles):
                        n = CT * ch + j
                        if not isinstance(ch, int) or ch > 0:
                            pool.wait_ge(agg_done[k], n - CT + 1)
                        pool.dma_start(g_ring[0:TN, j, :], g_sum_dram[bass.ds(n, 1)].rearrange("a p c -> p (a c)")
                                       ).then_inc(g_sum_in[j], 16)
                pool.nop()

            def store_2(n, par, half=True):
                pool.wait_ge(lo_ready[1], n + 1)
                pool.dma_start(xp_t[bass.ds(n, 1)].rearrange("a p c -> p (a c)"),
                               y_half[:, par, :] if half else y[0:TN, LAST, :]).then_inc(y_half_stored[par], 16)
                pool.wait_ge(xr_ready[1], n + 1)
                pool.dma_start(xr2_dram[bass.ds(n, 1)].rearrange("a p c -> p (a c)"), xr_o[:, par, :]).then_inc(xr_stored[1][par], 16)

            general_gathers(0)
            general_sums_back(0, 0, CT)
            with pool.Fori(1, CH) as ch:
                general_sums_back(0, ch, CT)
                for j in range(CT):
                    store_2(CT * (ch - 1) + j, j % 2)
            general_sums_back(0, CH, 1)
            for j in range(CT):
                store_2(CT * (CH - 1) + j, j % 2)
            store_2(LAST, 0, False)
            for j in range(2):
                pool.wait_ge(y_half_stored[j], 16 * (T // 2 + 1 - j))

            def store_x1(n, j):
                pool.wait_ge(stats2_ready, n + 1)
                pool.dma_start(x1_dram[bass.ds(n, 1)].rearrange("a p c -> p (a c)"), o_t[:, j, :]).then_inc(x1_stored[j], 16)

            general_gathers(1)
            for piece in range(3):
                pool.wait_ge(y_in2[piece], 16)
            general_sums_back(1, 0, CT)
            with pool.Fori(1, CH) as ch:
                general_sums_back(1, ch, CT)
                for j in range(CT):
                    store_x1(CT * (ch - 1) + j, j)
            general_sums_back(1, CH, 1)
            for j in range(CT):
                store_x1(CT * (CH - 1) + j, j)
            store_x1(LAST, 0)

            pool.wait_ge(agg_done[1], T)
            pool.memset(f_ones_row, 1.0)
            pool.memset(f_xn[:, :, C:C + 1], 1.0).then_inc(f_ones, 1)

            def quotient(t, j, first):
                pool.wait_ge(rs_ready, t + 1)
                if not first:
                    pool.wait_ge(wT_done, t - R + 1)
                pool.tensor_tensor(f_w[:, j, :].rearrange("p (h g) -> p h g", h=H), f_e[:, j, :].rearrange("p (h g) -> p h g", h=H),
                                   f_rs[:, j, :].unsqueeze(2).to_broadcast([TN, H, G]), ALU.mult).then_inc(fw_ready, 1)

            for j in range(R):
                quotient(j, j, True)
            with pool.Fori(1, CH) as ch:
                for j in range(R):
                    quotient(R * ch + j, j, False)
            quotient(LAST, 0, False)

            def store_out(t, par):
                pool.wait_ge(out_ready, t + 1)
                pool.dma_start(out_t[bass.ds(t, 1)].rearrange("a p c -> p (a c)"), y_o[:, par, :]).then_inc(out_stored[par], 16)

            with pool.Fori(0, T // 2) as i:
                store_out(2 * i, 0)
                store_out(2 * i + 1, 1)
            store_out(LAST, 0)
            pool.wait_ge(out_stored[0], 16 * (T // 2 + 1))
            pool.wait_ge(out_stored[1], 16 * (T // 2))

        @block.tensor
        def _(pe):
            def turn(k, n, src):
                pe.wait_ge((xn_ready, h_ready)[k], n + 1)
                if not isinstance(n, int) or n >= 1:
                    pe.wait_ge(hT_ready[k], n)
                for kc in range(KC):
                    last = pe.transpose(ps[:, 4, kc * TN:(kc + 1) * TN], src[:, kc * P:(kc + 1) * P], ident[0:TN, 0:TN])
                last.then_inc(x_turned[k], 1)

            def project(k, n, par):
                pe.wait_ge(hT_ready[k], n + 1)
                if not isinstance(n, int) or n >= 1:
                    pe.wait_ge(xpT_ready[k], n)
                for mc in range(KC):
                    for kc in range(KC):
                        last = pe.matmul(ps[:, 5, mc * TN:(mc + 1) * TN], wp[:, kc, mc * P:(mc + 1) * P], hT[:, par, kc, :],
                                         start=(kc == 0), stop=(kc == 1))
                last.then_inc(xpT_done[k], 1)
                if not isinstance(n, int) or n >= 1:
                    pe.wait_ge(xr_ready[k], n)
                for kc in range(KC):
                    last = pe.matmul(ps[0:TN, 7, 0:C], hT[:, par, kc, :], wr[:, kc, :], start=(kc == 0), stop=(kc == 1))
                last.then_inc(xr_done[k], 1)

            def times_wl(k, n, par):
                pe.wait_ge(xpT_ready[k], n + 1)
                if not isinstance(n, int) or n >= 1:
                    pe.wait_ge(lo_ready[k], n)
                for kc in range(KC):
                    last = pe.matmul(ps[0:TN, 6, 0:C], xpT[:, par, kc, :], wl[:, kc, :], start=(kc == 0), stop=(kc == 1))
                last.then_inc(y_done[k], 1)

            def front(n, par):
                if not isinstance(n, int) or n < T:
                    turn(0, n, xn[:, par, :])
                if not isinstance(n, int) or n >= 2:
                    times_wl(0, n - 2, par)
                if not isinstance(n, int) or 1 <= n <= T:
                    project(0, n - 1, 1 - par)

            def count(g, q):
                q %= GC
                bank, slot = BANK[q], OH_SLOT[q]
                pe.wait_ge(oh_ready, g + 1)
                if not isinstance(g, int) or g >= BANK_AGE[q]:
                    pe.wait_ge(stored, g - BANK_AGE[q] + 1)
                for a in range(SUB):
                    last = pe.matmul(ps[:, bank, a * KEYS:(a + 1) * KEYS], oh_low[:, slot * 2 + a // 2, :, a % 2],
                                     oh_key[:, slot * 2 + a // 2, :, a % 2], start=True, stop=True)
                last.then_inc(built, 1)

            pe.wait_ge(consts, 3)
            pe.wait_ge(step_ready, 1)
            pe.matmul(ps[0:TN, 3, 0:1], step, ones[0:TN, 0:1], start=True, stop=True).then_inc(r0_done, 1)
            front(0, 0)
            pe.wait_ge(weights_in, 16 * 5)
            for n in range(1, 5):
                front(n, n % 2)
            pe.wait_ge(fold_in, 16 * 5)
            for kc in range(KC):
                for h in range(H):
                    last = pe.matmul(ps[:, kc, h * G:(h + 1) * G], wxT[:, h, kc * P:(kc + 1) * P], wsl, start=True, stop=True)
            for h in range(H):
                last = pe.matmul(ps[0:1, 2, h * G:(h + 1) * G], bxT[:, h:h + 1], wsl, start=True, stop=True)
            last.then_inc(fold_done, 1)
            pe.wait_ge(rt_row, 1)
            pe.wait_ge(r0_ready, 1)
            pe.matmul(ps[:, 3, :], ones[0:1, :], rtemp_row.rearrange("a h g -> a (h g)"), start=True, stop=True).then_inc(rt_done, 1)
            front(5, 1)
            with pe.Fori(0, 3) as i:
                front(2 * i + 6, 0)
                front(2 * i + 7, 1)
            front(12, 0)
            pe.wait_ge(fold_ready, 2)
            pe.wait_ge(keys_ready, 1)
            for i in range(5):
                if i >= 3:
                    pe.wait_ge(tables_ready, 2 * (i - 2))
                pe.transpose(ps[:, i % 3, 0:TN], key_f[:, i, :], ident[0:TN, 0:TN])
                pe.transpose(ps[:, i % 3, P:P + TN], low_f[:, i, :], ident[0:TN, 0:TN]).then_inc(turned, 1)
                front(13 + i, (13 + i) % 2)
            front(18, 0)
            pe.wait_ge(rt_ready, 1)
            pe.wait_ge(cnt_rows_ready, 1)
            pe.matmul(ps[0:1, 3, 0:1], cnt_row, ones[0:TN, 0:1], start=True, stop=True).then_inc(total_done, 1)
            pe.wait_ge(covered_ready, 1)
            pe.wait_ge(tables_ready, 10)
            for n in range(EARLY, T + 2):
                front(n, n % 2)
                for g in EARLY_GROUPS[n]:
                    count(g, g)
            pe.wait_ge(lo_ready[0], T)
            pe.wait_ge(xr_ready[0], T)
            is_covered = pe.value_load(covered[0:1, 0:1], min_val=0, max_val=1)

            def sum_tile(k, ch, j, general, steps):
                n = CT * ch + j
                if not isinstance(n, int) or n >= 2:
                    pe.wait_ge(sq_done[k], n - 1)
                if k == 0 and not general:
                    pe.wait_ge(stored, GC * ch + -(-T * (j + 1) // SUB) if not isinstance(n, int) or n < LAST else GROUPS)
                if general:
                    pe.wait_ge(g_sum_in[j], 16 * (ch + 1 + k * (CH + (j == 0))))
                    pe.matmul(ps[0:TN, j % 2, :], ident[0:TN, 0:TN], g_ring[0:TN, j, :], start=True, stop=True).then_inc(agg_done[k], 1)
                for t in range(T):
                    if not general:
                        if k == 1 and isinstance(n, int) and n == 0:
                            if t == LAST:
                                pe.wait_ge(lo_ready[1], T)
                            elif t % 8 == 0:
                                pe.wait_ge(y_in2[t // 8], 16)
                        last = pe.matmul(ps[0:TN, j % 2, :], adj[0:TN, t, bass.ds(TN * n, TN)], y[0:TN, t, :],
                                         start=(t == 0), stop=(t == LAST))
                        if t == LAST:
                            last.then_inc(agg_done[k], 1)
                    steps(t)

            def layer_1(general):
                def chunk(ch, groups, nexts):
                    for j in range(CT):
                        def steps(t):
                            s = T * j + t
                            if s % SUB == 0 and s // SUB < groups:
                                count(GC * ch + LEAD + s // SUB, LEAD + s // SUB)
                            if nexts and t == TURN_AT:
                                turn(1, CT * (ch - 1) + j, o_t[:, j, :])
                            if nexts and t == PROJECT_AT:
                                project(1, CT * (ch - 1) + j, j % 2)
                            if nexts and t == WL_AT:
                                times_wl(1, CT * (ch - 1) + j, j % 2)
                        sum_tile(0, ch, j, general, steps)

                chunk(0, GC, False)
                pe.wait_ge(w2_in, 16 * 5)
                chunk(1, GC, True)
                with pe.Fori(2, CH - 1) as ch:
                    chunk(ch, GC, True)
                chunk(CH - 1, GROUPS - GC * (CH - 1) - LEAD, True)

                def next_step(p):
                    if p < CT:
                        turn(1, CT * (CH - 1) + p, o_t[:, p, :])
                    if 2 <= p:
                        times_wl(1, CT * (CH - 1) + p - 2, p % 2)
                    if 1 <= p <= CT:
                        project(1, CT * (CH - 1) + p - 1, (p - 1) % 2)

                def steps(t):
                    if t in LAST_AT:
                        next_step(LAST_AT.index(t))
                sum_tile(0, CH, 0, general, steps)
                for p in range(len(LAST_AT), CT + 2):
                    next_step(p)
                turn(1, LAST, o_t[:, 0, :])
                project(1, LAST, 0)
                times_wl(1, LAST, 0)

            def layer_2(general):
                def chunk(ch, tiles=CT):
                    for j in range(tiles):
                        sum_tile(1, ch, j, general, lambda t: None)

                pe.wait_ge(sq_done[0], T)
                chunk(0)
                with pe.Fori(1, CH) as ch:
                    chunk(ch)
                chunk(CH, 1)

            def general_sweeps(k):
                def sweep(s_):
                    chunk = (T // GT) * k + s_

                    def group(i, slot, first=False, final=False):
                        pe.wait_ge(g_in[slot], 16 * (ROUNDS * chunk + i + 1))
                        pe.wait_ge(g_oh_ready, ROW * chunk + RG * i + slot + 1)
                        for b in range(GT):
                            last = pe.matmul(ps[0:TN, b, :], g_oh[:, slot, b * TN:(b + 1) * TN], g_rows[:, slot, :],
                                             start=first, stop=final)
                            if first and b == 0:
                                last.then_inc(g_free, 1)
                        last.then_inc(g_swept if final else g_free, 1)

                    if not isinstance(chunk, int) or chunk > 0:
                        pe.wait_ge(g_sum_ready, chunk)
                    for slot in range(RG):
                        group(0, slot, first=slot == 0)
                    with pe.Fori(1, ROUNDS - 1) as i:
                        for slot in range(RG):
                            group(i, slot)
                    for slot in range(RG):
                        group(ROUNDS - 1, slot, final=slot == RG - 1)

                sweep(0)
                with pe.Fori(1, T // GT) as s_:
                    sweep(s_)
                pe.wait_ge(g_sum_out, 16 * (T // GT) * (k + 1))
                pe.wait_ge(g_idx_ready, (ROW * (T // GT) + 2) * (k + 1))

            with pe.If(is_covered == 1):
                layer_1(False)
                layer_2(False)
            with pe.Else():
                pe.nop().then_inc(g_free, RG - 1)
                general_sweeps(0)
                layer_1(True)
                pe.wait_ge(sq_done[0], T)
                pe.wait_ge(lo_ready[1], T)
                pe.wait_ge(xr_ready[1], T)
                general_sweeps(1)
                layer_2(True)
            pe.nop()

            def turn_f(t, j):
                pe.wait_ge(f_xn_ready, t + 1)
                if not (isinstance(t, int) and t == 0):
                    pe.wait_ge(f_xT_ready, t)
                for kc in range(KC):
                    last = pe.transpose(ps[:, 5, kc * TN:(kc + 1) * TN], f_xn[:, j, kc * P:(kc + 1) * P], ident[0:TN, 0:TN])
                last.then_inc(f_xt_done, 1)

            def logits(t, j):
                pe.wait_ge(f_xT_ready, t + 1)
                if not isinstance(t, int) or t >= 2:
                    pe.wait_ge(sub_ready, t - 1)
                to = ps[0:TN, 4 if j % 2 == 0 else 7, :]
                for kc in range(KC):
                    pe.matmul(to, f_xT[:, j, kc, :], wxs[:, kc, :], start=(kc == 0), stop=False)
                pe.matmul(to, f_ones_row, bxs, start=False, stop=True).then_inc(lg_done, 1)

            def gather_slices(t, j, first, last_):
                pe.wait_ge(fw_ready, t + 1)
                for k in range(PAIRS):
                    last = pe.matmul(ps[:, k, 0:C + 1], f_w[:, j, k * P:(k + 1) * P], f_xn[:, j, 0:C + 1], start=first, stop=last_)
                last.then_inc(s_done, 1)
                if not first:
                    pe.wait_ge(wT_ready, t)
                for k in range(PAIRS):
                    last = pe.transpose(ps[:, 6, k * TN:(k + 1) * TN], f_w[:, j, k * P:(k + 1) * P], ident[0:TN, 0:TN])
                last.then_inc(wT_done, 1)

            def slice_pass(p, j, front=True, back=True):
                if front:
                    turn_f(p, j)
                if back:
                    gather_slices(p - 2, (j - 2) % R, isinstance(p, int) and p == 2, isinstance(p, int) and p == T + 1)
                if front:
                    logits(p, j)

            pe.wait_ge(f_ones, 1)
            pe.wait_ge(slice_w_in, 32)
            pe.wait_ge(sq_done[1], T)
            slice_pass(0, 0, back=False)
            slice_pass(1, 1, back=False)
            slice_pass(2, 2)
            with pe.Fori(0, (T - 5) // R) as i:
                for j in range(R):
                    slice_pass(R * i + 3 + j, (3 + j) % R)
            for p in range(3 + (T - 5) // R * R, T + 2):
                slice_pass(p, p % R, front=p < T)

            pe.wait_ge(mid_w_in, 16 * 7)
            pe.wait_ge(mid_dve, 1)
            for kc in range(KC):
                for k in range(PAIRS):
                    pe.transpose(ps[:, 4 + kc, k * P:(k + 1) * P], s_sb[:, k, kc * P:(kc + 1) * P], ident[:, :])
            pe.wait_ge(wT_ready, T)
            for k in range(PAIRS):
                last = pe.transpose(ps[0:1, 6, k * P:(k + 1) * P], s_sb[:, k, C:C + 1], ident[:, :])
            last.then_inc(mid_pe, 1)
            pe.wait_ge(mid_dve, 2)
            pe.wait_ge(mid_act, 1)
            for h in range(H):
                hs = slice(h * D, (h + 1) * D)
                for kc in range(KC):
                    pe.matmul(ps[0:D, 7, hs], wfx[:, kc, hs], sT[:, kc, hs], start=(kc == 0), stop=False)
                last = pe.matmul(ps[0:D, 7, hs], bfx[:, hs], nr[:, hs], start=False, stop=True)
            last.then_inc(mid_pe, 1)
            pe.wait_ge(mid_dve, 3)
            pe.matmul(ps[0:D, 4, :], wq, tokT, start=True, stop=True).then_inc(mid_pe, 1)
            pe.matmul(ps[0:D, 5, :], wk, tokT, start=True, stop=True).then_inc(mid_pe, 1)
            for h in range(H):
                hs = slice(h * G, (h + 1) * G)
                last = pe.matmul(ps[0:G, 6, h * D:(h + 1) * D], tokT[:, hs], wv, start=True, stop=True)
            last.then_inc(mid_pe, 1)
            pe.wait_ge(mid_dve, 4)
            pe.wait_ge(mid_act, 2)
            for h in range(H):
                hs = slice(h * G, (h + 1) * G)
                last = pe.matmul(ps[0:G, 7, hs], qT[:, hs], kT[:, hs], start=True, stop=True)
            last.then_inc(mid_pe, 1)
            pe.wait_ge(mid_dve, 6)
            for h in range(H):
                last = pe.transpose(ps[0:G, 4, h * G:(h + 1) * G], a_w[:, h, :], ident[0:G, 0:G])
            last.then_inc(mid_pe, 1)
            pe.wait_ge(mid_act, 3)
            pe.wait_ge(mid_dve, 7)
            for h in range(H):
                last = pe.matmul(ps[0:D, 5, h * G:(h + 1) * G], v_sb[:, h * D:(h + 1) * D], aT[:, h * G:(h + 1) * G],
                                 start=True, stop=True)
            last.then_inc(mid_pe, 1)
            pe.wait_ge(mid_dve, 8)
            for h in range(H):
                k = h // 2
                to = ps[(h % 2) * G:(h % 2 + 1) * G, 6 + k // 2, (k % 2) * C:(k % 2 + 1) * C]
                last = pe.matmul(to, osT[:, h * G:(h + 1) * G], wo[:, h, :], start=True, stop=h > 0)
                if h == 0:
                    pe.matmul(to, f_ones_row[:, 0:G], bo, start=False, stop=True)
            last.then_inc(mid_pe, 1)

            def outputs(t, par, first):
                pe.wait_ge(w_st_ready, t + 1)
                if not first:
                    pe.wait_ge(out_ready, t - 1)
                to = ps[0:TN, par, 0:C]
                for k in range(PAIRS):
                    last = pe.matmul(to, w_st[:, par, k, :], t_sb[:, k, :], start=(k == 0), stop=(k == PAIRS - 1))
                last.then_inc(out_done, 1)

            pe.wait_ge(mid_dve, 10)
            outputs(0, 0, True)
            outputs(1, 1, True)
            outputs(2, 0, False)
            with pe.Fori(0, (T - 3) // 2) as i:
                outputs(2 * i + 3, 1, False)
                outputs(2 * i + 4, 0, False)

        @block.scalar
        def _(act):
            def std_of(n, par):
                act.wait_ge(mv_ready, n + 1)
                act.activation(std[:, par:par + 1], mv[:, par, 1:2], ACT.Sqrt, bias=eps).then_inc(std_ready, 1)

            def turned_x(k, n, par):
                act.wait_ge(x_turned[k], n + 1)
                if not isinstance(n, int) or n >= 2:
                    act.wait_ge(xr_done[k], n - 1)
                act.activation(hT[:, par].rearrange("p k n -> p (k n)"), ps[:, 4, 0:KC * TN], ACT.Copy).then_inc(hT_ready[k], 1)

            def projected(k, n, par):
                act.wait_ge(xpT_done[k], n + 1)
                if not isinstance(n, int) or n >= 2:
                    act.wait_ge(y_done[k], n - 1)
                for mc in range(KC):
                    last = act.activation(xpT[:, par, mc, :], ps[:, 5, mc * TN:(mc + 1) * TN], ACT.Relu, bias=bias_p[:, mc:mc + 1])
                last.then_inc(xpT_ready[k], 1)

            def high(k, n, to):
                act.wait_ge(y_done[k], n + 1)
                act.activation(to, ps[0:TN, 6, 0:C], ACT.Copy).then_inc(hi_ready[k], 1)

            def table(i, at, to):
                act.wait_ge(turned, i + 1)
                act.activation(to[:, 0:Q].rearrange("e (p i) -> e i p", i=5)[:, i, :], ps[:, i % 3, at:at + TN],
                               ACT.Copy).then_inc(tables_ready, 1)

            def front(n, par):
                if not isinstance(n, int) or n < T:
                    turned_x(0, n, par)
                if not isinstance(n, int) or n >= 2:
                    high(0, n - 2, y[0:TN, bass.ds(n - 2, 1), 0:C].rearrange("p a c -> p (a c)"))
                if not isinstance(n, int) or 1 <= n <= T:
                    projected(0, n - 1, 1 - par)
                if not isinstance(n, int) or n + 2 < T:
                    std_of(n + 2, par)

            def store_counts(g, q):
                act.wait_ge(built, g + 1)
                if isinstance(g, int) and g == GROUPS - 1:
                    act.activation(adj[:, :, N - D5:N], ps[:, BANK[q % GC], 0:KEYS].rearrange("p (s d) -> p s d", s=T),
                                   ACT.Copy).then_inc(stored, 1)
                    return
                act.activation(adj[:, :, bass.ds(g * SUB * D5, SUB * D5)].rearrange("p s (q d) -> p q s d", q=SUB),
                               ps[:, BANK[q % GC], 0:SUB * KEYS].rearrange("p (q s d) -> p q s d", q=SUB, s=T),
                               ACT.Copy).then_inc(stored, 1)

            act.wait_ge(consts, 4)
            act.wait_ge(weights_in, 16 * 5)
            std_of(0, 0)
            std_of(1, 1)
            for n in range(3):
                front(n, n % 2)
            with act.Fori(0, 5) as i:
                front(2 * i + 3, 1)
                front(2 * i + 4, 0)
            for i in range(5):
                table(i, 0, key_t)
                front(13 + i, (13 + i) % 2)
                table(i, P, low_t)
            front(18, 0)
            act.wait_ge(cnt_out, 16)
            act.wait_ge(fold_stored, 32)
            act.wait_ge(total_done, 1)
            act.wait_ge(rt_ready, 1)
            for n in range(EARLY, T + 2):
                front(n, n % 2)
                for g in EARLY_GROUPS[n]:
                    store_counts(g, g)

            def squares(k, n, j):
                act.wait_ge(o_ready[k], n + 1)
                act.activation(ps[0:TN, j % 2, 0:C], o_t[:, j, :], ACT.Square, accum_out=ss[:, j:j + 1]).then_inc(sq_done[k], 1)

            def norms(k, ch, tiles):
                act.wait_ge(sq_done[k], CT * ch + tiles)
                act.activation(nrm[:, 0:tiles], ss[:, 0:tiles], ACT.Sqrt).then_inc(nrm_ready[k], 1)

            def half_high(n, par, stores):
                if not isinstance(n, int) or n >= 2:
                    act.wait_ge(y_half_stored[par], 16 * stores)
                high(1, n, y_half[:, par, 0:C])

            def chunk(ch, groups, nexts):
                for j in range(CT):
                    for t in range(T):
                        s = T * j + t
                        if s % SUB == 0 and s // SUB < groups:
                            store_counts(GC * ch + LEAD + s // SUB, LEAD + s // SUB)
                        if t == 7 and j > 0:
                            squares(0, CT * ch + j - 1, j - 1)
                        if t == 7 and j == 0 and nexts:
                            squares(0, CT * ch - 1, CT - 1)
                            norms(0, ch - 1, CT)
                        if nexts and t == TURN_AT:
                            turned_x(1, CT * (ch - 1) + j, j % 2)
                        if nexts and t == PROJECT_AT:
                            projected(1, CT * (ch - 1) + j, j % 2)
                        if nexts and t == WL_AT:
                            half_high(CT * (ch - 1) + j, j % 2, 2 * (ch - 1) + j // 2)

            chunk(0, GC, False)
            act.wait_ge(xr_done[0], T)
            act.wait_ge(w2_in, 16 * 5)
            chunk(1, GC, True)
            with act.Fori(2, CH - 1) as ch:
                chunk(ch, GC, True)
            chunk(CH - 1, GROUPS - GC * (CH - 1) - LEAD, True)
            squares(0, CT * CH - 1, CT - 1)
            norms(0, CH - 1, CT)
            for p in range(CT + 2):
                n = CT * (CH - 1) + p
                if p < CT:
                    turned_x(1, n, p % 2)
                if 2 <= p:
                    half_high(n - 2, p % 2, (n - 2) // 2)
                if 1 <= p <= CT:
                    projected(1, n - 1, (p - 1) % 2)
                if p == 3:
                    squares(0, LAST, 0)
                    norms(0, CH, 1)
            turned_x(1, LAST, 0)
            projected(1, LAST, 0)
            act.wait_ge(agg_done[0], T)
            high(1, LAST, y[0:TN, LAST, 0:C])

            def chunk_2(ch, first=False):
                for j in range(CT):
                    if j > 0:
                        squares(1, CT * ch + j - 1, j - 1)
                    elif not first:
                        squares(1, CT * ch - 1, CT - 1)
                        norms(1, ch - 1, CT)

            chunk_2(0, True)
            with act.Fori(1, CH) as ch:
                chunk_2(ch)
            squares(1, CT * CH - 1, CT - 1)
            norms(1, CH - 1, CT)
            squares(1, LAST, 0)
            norms(1, CH, 1)

            act.wait_ge(var2_ready, 1)
            act.activation(std2, var2, ACT.Sqrt).then_inc(std2_ready, 1)

            def f_turned(t, j):
                act.wait_ge(f_xt_done, t + 1)
                if not isinstance(t, int) or t >= R:
                    act.wait_ge(lg_done, t - R + 1)
                act.activation(f_xT[:, j].rearrange("p k n -> p (k n)"), ps[:, 5, 0:KC * TN], ACT.Copy).then_inc(f_xT_ready, 1)

            def exps(t, j):
                act.wait_ge(sub_ready, t + 1)
                act.activation(f_e[:, j, :], f_e[:, j, :], ACT.Exp).then_inc(exp_ready, 1)

            def w_turned(t):
                act.wait_ge(wT_done, t + 1)
                act.activation(w_tr[:, :, bass.ds(TN * t, TN)], ps[:, 6, 0:PAIRS * TN].rearrange("p (k n) -> p k n", k=PAIRS),
                               ACT.Copy).then_inc(wT_ready, 1)

            def slice_pass(p, j, front=True, back=True):
                if front:
                    f_turned(p, j)
                if back:
                    w_turned(p - 2)
                if front:
                    exps(p, j)

            slice_pass(0, 0, back=False)
            slice_pass(1, 1, back=False)
            slice_pass(2, 2)
            slice_pass(3, 3)
            with act.Fori(1, CH) as i:
                for j in range(R):
                    slice_pass(R * i + j, j)
            for p in range(CH * R, T + 2):
                slice_pass(p, p % R, front=p < T)

            act.wait_ge(mid_pe, 1)
            act.activation(sT[:, 0, :], ps[:, 4, :], ACT.Copy).then_inc(mid_act, 1)
            act.wait_ge(mid_pe, 3)
            act.activation(qT, ps[0:D, 4, :], ACT.Copy).then_inc(mid_act, 1)
            act.wait_ge(mid_pe, 5)
            act.activation(v_sb, ps[0:G, 6, :], ACT.Copy).then_inc(mid_act, 1)
            act.wait_ge(mid_dve, 5)
            act.activation(a_e.rearrange("p h g -> p (h g)"), a_e.rearrange("p h g -> p (h g)"), ACT.Exp, scale=SCALE).then_inc(mid_act, 1)

        @block.vector
        def _(dve):
            c = Chain(dve, dve_steps)

            def later(n, m):
                return not isinstance(n, int) or n >= m

            def row_stats_x(n, par, loads):
                dve.wait_ge(x_loaded[par], 16 * loads)
                if later(n, 2):
                    dve.wait_ge(xn_ready, n - 1)
                if later(n, 1):
                    dve.wait_ge(mv_ready, n)
                c.link(dve.bn_stats(st6, x_in[:, par, :]))

            def row_moments(n, par):
                dve.bn_aggr(mv[:, par, :], st6).then_inc(mv_ready, 1)

            def norm_x(n, par):
                dve.wait_ge(std_ready, n + 1)
                if later(n, 1):
                    dve.wait_ge(xn_ready, n)
                c.link(dve.reciprocal(rstd, std[:, par:par + 1]))
                if later(n, 2):
                    dve.wait_ge(x_turned[0], n - 1)
                dve.tensor_scalar(xn[:, par, :], x_in[:, par, :], mv[:, par, 0:1], rstd, ALU.subtract, ALU.mult).then_inc(xn_ready, 1)

            def low(k, n, half):
                dve.wait_ge(hi_ready[k], n + 1)
                dve.tensor_tensor(half[:, C:2 * C], ps[0:TN, 6, 0:C], half[:, 0:C], ALU.subtract).then_inc(lo_ready[k], 1)

            def add_bias(k, n, par, stores):
                dve.wait_ge(xr_done[k], n + 1)
                if later(n, 2):
                    dve.wait_ge(xr_stored[k][par], 16 * stores)
                dve.tensor_tensor(xr_o[:, par, :], ps[0:TN, 7, 0:C], bias_l[0:TN, :], ALU.add).then_inc(xr_ready[k], 1)

            def front(n, par, loads):
                if not isinstance(n, int) or n + 1 < T:
                    norm_x(n + 1, 1 - par)
                if not isinstance(n, int) or n + 2 < T:
                    row_stats_x(n + 2, par, loads)
                if later(n, 2):
                    low(0, n - 2, y[0:TN, bass.ds(n - 2, 1), :].rearrange("p a c -> p (a c)"))
                if not isinstance(n, int) or n + 2 < T:
                    row_moments(n + 2, par)
                if not isinstance(n, int) or 1 <= n <= T:
                    add_bias(0, n - 1, 1 - par, loads - 3 + par)

            def one_hots(g, q):
                q %= GC
                if later(g, OH_AGE[q]):
                    dve.wait_ge(built, g - OH_AGE[q] + 1)
                pairs = slice(OH_SLOT[q] * 2, OH_SLOT[q] * 2 + 2)
                tile0 = g * SUB
                to = [P, 2, P, 2], [P, 2, KEYS, 2]
                one = [tab[:, bass.ds(tile0, SUB)].rearrange("p (a k) -> p a k", k=2).unsqueeze(2).to_broadcast(shape)
                       for tab, shape in zip((low_t, key_t), to)]
                dve.tensor_tensor(oh_low[:, pairs], iota_low.unsqueeze(1).to_broadcast(to[0]), one[0], ALU.is_equal)
                dve.tensor_tensor(oh_key[:, pairs], iota_key.unsqueeze(1).to_broadcast(to[1]), one[1], ALU.is_equal).then_inc(oh_ready, 1)

            dve.wait_ge(consts, 2)
            dve.wait_ge(rows_in, 16)
            c.link(dve.tensor_copy(rowmax, rows[:, ROW - 1:ROW]))
            dve.tensor_scalar(step, thr, rowmax, None, ALU.is_gt).then_inc(step_ready, 1)
            row_stats_x(0, 0, 1)
            row_moments(0, 0)
            dve.wait_ge(r0_done, 1)
            c.link(dve.tensor_scalar(r0, ps[0:TN, 3, 0:1], float(TN - 1), None, ALU.min))
            dve.tensor_copy(r0_i, r0).then_inc(r0_ready, 1)
            norm_x(0, 0)
            row_stats_x(1, 1, 1)
            row_moments(1, 1)
            dve.wait_ge(weights_in, 16 * 5)
            front(0, 0, 2)
            front(1, 1, 2)
            dve.wait_ge(row_in, 16)
            c.link(dve.tensor_copy(picked_f, picked))
            c.link(dve.tensor_scalar(junk[:, 0:ROW], picked_f, own[:, 0:1], None, ALU.is_lt, ALU.add, accum_out=below))
            c.link(dve.scalar_tensor_tensor(out=start, in0=r0, scalar=float(ROW), in1=below, op0=ALU.mult, op1=ALU.add))
            c.link(dve.tensor_scalar(start_c, start, float(E - COARSE), None, ALU.min))
            dve.tensor_copy(start_i, start_c).then_inc(start_ready, 1)
            front(2, 0, 3)
            front(3, 1, 3)
            dve.wait_ge(fold_in, 16 * 5)
            c.link(dve.tensor_scalar(rtemp, temp, 0.1, 5.0, ALU.max, ALU.min))
            c.link(dve.reciprocal(rtemp, rtemp))
            dve.tensor_copy(rtemp_row, rtemp.unsqueeze(2).to_broadcast([1, H, G])).then_inc(rt_row, 1)
            dve.wait_ge(coarse_in, 16)
            c.link(dve.tensor_copy(coarse_f, coarse))
            for i in range(2):
                last = dve.tensor_scalar(junk5[:, i], coarse_f, base5[:, i:i + 1], None, ALU.is_lt, ALU.add,
                                         accum_out=below5[:, i:i + 1])
            front(4, 0, 4)
            for i in range(2, 5):
                last = dve.tensor_scalar(junk5[:, i], coarse_f, base5[:, i:i + 1], None, ALU.is_lt, ALU.add,
                                         accum_out=below5[:, i:i + 1])
            c.link(last)
            c.link(dve.tensor_scalar(start5, below5, start_c, float(E - WIN), ALU.add, ALU.min))
            dve.tensor_copy(start5_i[:, :, 0], start5).then_inc(fine_ready, 1)
            front(5, 1, 4)
            dve.wait_ge(fold_done, 1)
            dve.wait_ge(rt_done, 1)
            dve.tensor_copy(rtemp_all, ps[:, 3, :]).then_inc(rt_ready, 1)
            dve.wait_ge(rt_ready, 1)
            for kc in range(KC):
                last = dve.tensor_tensor(wxs_o[:, kc, :], ps[:, kc, :], rtemp_all, ALU.mult)
            last.then_inc(fold_ready, 1)
            c.link(dve.tensor_tensor(bxs_t, ps[0:1, 2, :].rearrange("p (h g) -> p h g", h=H),
                                     bsl.unsqueeze(1).to_broadcast([1, H, G]), ALU.add))
            dve.tensor_tensor(bxs_o, bxs_t, rtemp_row, ALU.mult).then_inc(fold_ready, 1)
            with dve.Fori(0, 2) as i:
                c.loop(i, 4)
                front(2 * i + 6, 0, i + 5)
                front(2 * i + 7, 1, i + 5)
            c.end(2)
            for i in range(5):
                dve.wait_ge(win_in[i], 32)
            dve.tensor_scalar(hi_i, win_s, 1.0 / TN, -0.496, ALU.mult, ALU.add)
            c.link(dve.tensor_copy(win_f, win_d))
            dve.scalar_tensor_tensor(out=low_f, in0=hi_i, scalar=-float(TN), in1=win_s, op0=ALU.mult, op1=ALU.add)
            c.link(dve.tensor_tensor(dl, win_f, base5.unsqueeze(2).to_broadcast([TN, 5, WIN]), ALU.subtract))
            front(10, 0, 7)
            dve.tensor_scalar(ge0, dl, 0.0, None, ALU.is_ge)
            c.link(dve.scalar_tensor_tensor(out=pair_f, in0=hi_i, scalar=float(D5), in1=dl, op0=ALU.mult, op1=ALU.add))
            c.link(dve.scalar_tensor_tensor(out=valid, in0=dl, scalar=float(D5), in1=ge0, op0=ALU.is_lt, op1=ALU.mult))
            dve.scalar_tensor_tensor(out=key_f, in0=pair_f, scalar=1.0, in1=valid, op0=ALU.add, op1=ALU.mult).then_inc(keys_ready, 1)
            for i in range(5):
                front(11 + i, (11 + i) % 2, (13 + i) // 2 + 1)
                for d in range(D5):
                    col = D5 * i + d
                    last = dve.tensor_scalar(junk25[:, col, :], win_f[:, i], own[:, col:col + 1], None, ALU.is_equal, ALU.add,
                                             accum_out=cnt[:, col:col + 1])
            c.link(last)
            dve.tensor_reduce(cnt_row, cnt, AX_X, ALU.add).then_inc(cnt_rows_ready, 1)
            for n in range(16, EARLY):
                front(n, n % 2, (n + 2) // 2 + 1)
            dve.wait_ge(total_done, 1)
            dve.tensor_scalar(covered[0:1, 0:1], ps[0:1, 3, 0:1], float(E), None, ALU.is_equal).then_inc(covered_ready, 1)
            dve.wait_ge(consts, 4)
            dve.wait_ge(tables_ready, 10)
            for n in range(EARLY, T + 2):
                for g in EARLY_GROUPS[n]:
                    one_hots(g, g)
                front(n, n % 2, (n + 2) // 2 + 1)
            dve.wait_ge(cnt_in, 16)
            c.link(dve.tensor_scalar(rcnt[0:TN, :], rcnt[0:TN, :], 1.0, None, ALU.max))
            dve.reciprocal(rcnt[0:TN, :], rcnt[0:TN, :]).then_inc(rcnt_ready, 1)
            dve.wait_ge(rcnt_ready, 1)
            is_covered = dve.value_load(covered[0:1, 0:1], min_val=0, max_val=1)

            def general_one_hots(k):
                def sweep(s_):
                    chunk, rel = (T // GT) * k + s_, (T // GT + 1) * k + s_

                    def group(i, slot):
                        kk = RG * i + slot
                        dve.wait_ge(g_rel_ready, rel + 1)
                        dve.wait_ge(g_free, ROW * chunk + kk + 1)
                        dve.tensor_scalar(g_oh[:, slot, :], g_iota, g_rel[:, bass.ds(kk, 1)], None, ALU.is_equal).then_inc(g_oh_ready, 1)

                    with dve.Fori(0, ROUNDS) as i:
                        for slot in range(RG):
                            group(i, slot)
                    dve.wait_ge(g_oh_ready, ROW * chunk + ROW)
                    dve.tensor_scalar(g_rel, g_rel, -float(GT * TN), None, ALU.add).then_inc(g_rel_ready, 1)
                    dve.wait_ge(g_swept, chunk + 1)
                    if not isinstance(chunk, int) or chunk > 0:
                        dve.wait_ge(g_sum_out, 16 * chunk)
                    dve.tensor_copy(g_sum, ps[0:TN, 0:GT, :]).then_inc(g_sum_ready, 1)

                if k:
                    dve.wait_ge(g_rel_ready, T // GT + 1)
                    dve.wait_ge(stored, GROUPS)
                    dve.wait_ge(g_tables_in, 64)
                    dve.tensor_copy(g_dst, g_dst_i).then_inc(g_dst_ready, 1)
                    dve.wait_ge(g_dst_ready, 1)
                    dve.wait_ge(g_iota_ready, 2)
                dve.tensor_copy(g_rel, g_dst).then_inc(g_rel_ready, 1)
                sweep(0)
                with dve.Fori(1, T // GT) as s_:
                    sweep(s_)

            with dve.If(is_covered == 1):
                dve.nop()
            with dve.Else():
                g = Chain(dve, g_steps)
                dve.wait_ge(g_tables_in, 32)
                g.link(dve.tensor_copy(g_dst, g_dst_i))
                dve.wait_ge(g_node_ready, 1)
                g.link(dve.memset(g_cnt, 0.0))
                with dve.Fori(0, E // N) as s_:
                    g.loop(s_, T + 1)
                    dve.wait_ge(g_all_in, 16 * s_ + 16)
                    dve.tensor_copy(g_all, g_all_i).then_inc(g_all_used, 1)
                    dve.wait_ge(g_all_used, s_ + 1)
                    for t in range(T):
                        g.link(dve.tensor_scalar(g_eq, g_all, g_node[:, t:t + 1], None, ALU.is_equal, ALU.add,
                                                 accum_out=g_part[:, t:t + 1]))
                    g.link(dve.tensor_tensor(g_cnt, g_cnt, g_part, ALU.add))
                g.end(E // N)
                g.link(dve.tensor_scalar(g_cnt, g_cnt, 1.0, None, ALU.max))
                g.link(dve.reciprocal(rcnt[0:TN, :], g_cnt))
                dve.wait_ge(g_iota_ready, 1)
                general_one_hots(0)
            dve.nop()

            def combine(k, ch, j, n):
                dve.wait_ge(agg_done[k], n + 1)
                dve.wait_ge(xr_loaded[k][j], 16 * (ch + 1))
                for half in range(KC):
                    last = dve.scalar_tensor_tensor(out=o_t[:, j, :], in0=ps[0:TN, j % 2, half * C:(half + 1) * C],
                                                    scalar=rcnt[0:TN, bass.ds(n, 1)], in1=o_t[:, j, :],
                                                    op0=ALU.mult, op1=ALU.add)
                    if half == 0:
                        c.link(last)
                last.then_inc(o_ready[k], 1)

            def finish(k, ch, tiles):
                dve.wait_ge(nrm_ready[k], ch + 1)
                c.link(dve.tensor_scalar(nrm[:, 0:tiles], nrm[:, 0:tiles], EPS_NORM, None, ALU.max))
                c.link(dve.reciprocal(inv[:, 0:tiles], nrm[:, 0:tiles]))
                for j in range(tiles):
                    if k == 0:
                        dve.tensor_scalar(o_t[:, j, :], o_t[:, j, :], inv[:, j:j + 1], 0.0, ALU.mult, ALU.max).then_inc(h_ready, 1)
                    else:
                        dve.wait_ge(res_loaded[j], 16 * (ch + 1))
                        dve.scalar_tensor_tensor(out=o_t[:, j, :], in0=o_t[:, j, :], scalar=inv[:, j:j + 1], in1=x_res[:, j, :],
                                                 op0=ALU.mult, op1=ALU.add).then_inc(x1_ready, 1)
                        if j > 0:
                            row_stats(ch, j - 1)
                if k == 1:
                    row_stats(ch, tiles - 1)

            def row_stats(ch, j):
                dve.wait_ge(x1_ready, CT * ch + j + 1)
                dve.bn_stats(stats2[0:TN, bass.ds(CT * ch + j, 1), :].rearrange("p a b -> p (a b)"),
                             o_t[:, j, :]).then_inc(stats2_ready, 1)

            def chunk(ch, groups, nexts):
                for j in range(CT):
                    for t in range(T):
                        s = T * j + t
                        if s % SUB == 0 and s // SUB < groups:
                            one_hots(GC * ch + LEAD + s // SUB, LEAD + s // SUB)
                        before = CT * (ch - 1) + j - 1
                        if nexts and t == 3 and (j > 0 or later(ch, 2)):
                            add_bias(1, before, (j - 1) % 2, 2 * (ch - 1) + (j - 1) // 2)
                        if nexts and t == 9 and (j > 0 or later(ch, 2)):
                            low(1, before, y_half[:, (j - 1) % 2, :])
                        if t == 11 and j > 0:
                            combine(0, ch, j - 1, CT * ch + j - 1)
                        if t == 11 and j == 0 and nexts:
                            combine(0, ch - 1, CT - 1, CT * ch - 1)
                        if t == 17 and j == 0 and nexts:
                            finish(0, ch - 1, CT)

            chunk(0, GC, False)
            dve.wait_ge(xr_stored[0][0], 16 * (T // 2 + 1))
            dve.wait_ge(xr_stored[0][1], 16 * (T // 2))
            dve.wait_ge(w2_in, 16 * 5)
            chunk(1, GC, True)
            with dve.Fori(2, CH - 1) as ch:
                c.loop(ch - 2, CT + 2)
                chunk(ch, GC, True)
            c.end(CH - 3)
            chunk(CH - 1, GROUPS - GC * (CH - 1) - LEAD, True)
            combine(0, CH - 1, CT - 1, CT * CH - 1)
            add_bias(1, CT * (CH - 1) - 1, 1, CT * (CH - 1) // 2 - 1)
            low(1, CT * (CH - 1) - 1, y_half[:, 1, :])
            finish(0, CH - 1, CT)
            for p in range(1, CT + 2):
                n = CT * (CH - 1) + p
                if 2 <= p:
                    low(1, n - 2, y_half[:, p % 2, :])
                if p <= CT:
                    add_bias(1, n - 1, (p - 1) % 2, (n - 1) // 2)
                if p == 3:
                    combine(0, CH, 0, LAST)
            finish(0, CH, 1)
            add_bias(1, LAST, 0, LAST // 2)
            low(1, LAST, y[0:TN, LAST, :])

            with dve.If(is_covered == 1):
                dve.nop()
            with dve.Else():
                general_one_hots(1)
            dve.nop()

            def chunk_2(ch, first=False):
                for j in range(CT):
                    if j > 0:
                        combine(1, ch, j - 1, CT * ch + j - 1)
                    elif not first:
                        combine(1, ch - 1, CT - 1, CT * ch - 1)
                        finish(1, ch - 1, CT)

            chunk_2(0, True)
            with dve.Fori(1, CH) as ch:
                c.loop(ch - 1, CT + 2)
                chunk_2(ch)
            c.end(CH - 1)
            combine(1, CH - 1, CT - 1, CT * CH - 1)
            finish(1, CH - 1, CT)
            combine(1, CH, 0, LAST)
            finish(1, CH, 1)

            dve.wait_ge(stats2_ready, T)
            dve.wait_ge(agg_done[1], T)
            s2 = stats2[0:TN]
            c.link(dve.tensor_tensor(mean2, s2[:, :, 1], s2[:, :, 4], ALU.add))
            c.link(dve.tensor_tensor(half2, s2[:, :, 1], s2[:, :, 4], ALU.subtract))
            c.link(dve.tensor_tensor(var2, s2[:, :, 2], s2[:, :, 5], ALU.add))
            c.link(dve.tensor_scalar(mean2, mean2, 0.5, None, ALU.mult))
            c.link(dve.tensor_tensor(half2, half2, half2, ALU.mult))
            c.link(dve.tensor_scalar(var2, var2, 1.0 / C, EPS_LN, ALU.mult, ALU.add))
            dve.scalar_tensor_tensor(out=var2, in0=half2, scalar=0.25, in1=var2, op0=ALU.mult, op1=ALU.add).then_inc(var2_ready, 1)
            dve.wait_ge(std2_ready, 1)
            c.link(dve.reciprocal(rstd2, std2))

            def normed(t, j, first, loads):
                dve.wait_ge(f_loaded[j], 16 * loads)
                if not first:
                    dve.wait_ge(s_done, t - R + 1)
                dve.tensor_scalar(f_xn[:, j, 0:C], f_in[:, j, :], mean2[:, bass.ds(t, 1)],
                                  rstd2[:, bass.ds(t, 1)], ALU.subtract, ALU.mult).then_inc(f_xn_ready, 1)

            def softmax(t, j, first):
                bank = ps[0:TN, 4 if j % 2 == 0 else 7, :].rearrange("p (h g) -> p h g", h=H)
                e = f_e[:, j, :].rearrange("p (h g) -> p h g", h=H)
                dve.wait_ge(lg_done, t + 1)
                c.link(dve.tensor_reduce(f_mx[:, j, :], bank, AX_X, ALU.max))
                if not first:
                    dve.wait_ge(fw_ready, t - R + 1)
                dve.tensor_tensor(e, bank, f_mx[:, j, :].unsqueeze(2).to_broadcast([TN, H, G]), ALU.subtract).then_inc(sub_ready, 1)

            def sums(t, j):
                e = f_e[:, j, :].rearrange("p (h g) -> p h g", h=H)
                dve.wait_ge(exp_ready, t + 1)
                c.link(dve.tensor_reduce(f_sm[:, j, :], e, AX_X, ALU.add))
                dve.reciprocal(f_rs[:, j, :], f_sm[:, j, :]).then_inc(rs_ready, 1)

            normed(0, 0, True, 1)
            for t in range(R):
                if t + 1 < R:
                    normed(t + 1, t + 1, True, 1)
                else:
                    normed(t + 1, 0, False, 2)
                softmax(t, t, True)
                sums(t, t)
            with dve.Fori(1, CH) as i:
                c.loop(i - 1, 2 * R)
                for j in range(R):
                    normed(R * i + j + 1, (j + 1) % R, False, i + 1 + (j + 1) // R)
                    softmax(R * i + j, j, False)
                    sums(R * i + j, j)
            c.end(CH - 1)
            softmax(LAST, 0, False)
            sums(LAST, 0)

            dve.wait_ge(s_done, T)
            c.link(dve.tensor_scalar(sn_e, ps[:, 0:PAIRS, C], EPS_SLICE, None, ALU.add))
            c.link(dve.reciprocal(sn_inv, sn_e))
            for k in range(PAIRS):
                last = dve.tensor_scalar(s_sb[:, k, 0:C + 1], ps[:, k, 0:C + 1], sn_inv[:, k:k + 1], None, ALU.mult)
            last.then_inc(mid_dve, 1)
            dve.wait_ge(mid_pe, 1)
            dve.tensor_copy(sT[:, 1, :], ps[:, 5, :])
            dve.tensor_copy(nr, ps[0:1, 6, :]).then_inc(mid_dve, 1)
            dve.wait_ge(mid_pe, 2)
            dve.tensor_copy(tokT, ps[0:D, 7, :]).then_inc(mid_dve, 1)
            dve.wait_ge(mid_pe, 4)
            dve.tensor_copy(kT, ps[0:D, 5, :]).then_inc(mid_dve, 1)
            dve.wait_ge(mid_pe, 6)
            sc = ps[0:G, 7, :].rearrange("p (h g) -> p h g", h=H)
            c.link(dve.tensor_reduce(am, sc, AX_X, ALU.max))
            dve.tensor_tensor(a_e, sc, am.unsqueeze(2).to_broadcast([G, H, G]), ALU.subtract).then_inc(mid_dve, 1)
            dve.wait_ge(mid_act, 4)
            c.link(dve.tensor_reduce(a_s, a_e, AX_X, ALU.add))
            c.link(dve.reciprocal(a_r, a_s))
            dve.tensor_tensor(a_w, a_e, a_r.unsqueeze(2).to_broadcast([G, H, G]), ALU.mult).then_inc(mid_dve, 1)
            dve.wait_ge(mid_pe, 7)
            dve.tensor_copy(aT, ps[0:G, 4, :]).then_inc(mid_dve, 1)
            dve.wait_ge(mid_pe, 8)
            dve.tensor_copy(osT, ps[0:D, 5, :]).then_inc(mid_dve, 1)
            dve.wait_ge(mid_pe, 9)
            for b in range(2):
                dve.tensor_copy(t_sb[:, 2 * b:2 * b + 2, :].rearrange("p k c -> p (k c)"), ps[:, 6 + b, :]).then_inc(mid_dve, 1)

            def stage(t, par, first):
                if not first:
                    dve.wait_ge(out_done, t - 1)
                dve.tensor_copy(w_st[:, par], w_tr[:, :, bass.ds(TN * t, TN)]).then_inc(w_st_ready, 1)

            def finish(t, par, stores, loads):
                dve.wait_ge(out_done, t + 1)
                dve.wait_ge(out_in[par], 16 * loads)
                if not isinstance(t, int) or t >= 2:
                    dve.wait_ge(out_stored[par], 16 * stores)
                dve.tensor_tensor(y_o[:, par, :], ps[0:TN, par, 0:C], y_in[:, par, :], ALU.add).then_inc(out_ready, 1)

            dve.wait_ge(wT_ready, T)
            stage(0, 0, True)
            stage(1, 1, True)
            finish(0, 0, 0, 1)
            stage(2, 0, False)
            finish(1, 1, 0, 1)
            with dve.Fori(0, (T - 3) // 2) as i:
                stage(2 * i + 3, 1, False)
                finish(2 * i + 2, 0, i + 1, i + 2)
                stage(2 * i + 4, 0, False)
                finish(2 * i + 3, 1, i + 1, i + 2)
            finish(T - 1, 0, (T - 1) // 2, (T + 1) // 2)


def kernel(**inputs):
    import numpy as np
    import concourse.bacc as bacc
    from concourse.bass_utils import run_bass_kernel_spmd as run

    nc = bacc.Bacc("TRN2", target_bir_lowering=False, num_devices=1)
    arrays, args = {}, {}

    def give(name, a):
        a = np.ascontiguousarray(a)
        arrays[f"in_{name}"] = a
        args[name] = nc.dram_tensor(f"in_{name}", a.shape, mybir.dt.from_np(a.dtype), kind="ExternalInput").ap()

    for name in ("x", "src", "dst"):
        give(name, inputs[name])
    for name in ("W_proj1", "b_proj1", "W_l1", "b_l1", "W_r1", "W_proj2", "b_proj2", "W_l2", "b_l2", "W_r2"):
        give(name.replace("W_proj", "Wp").replace("b_proj", "bp").replace("W_l", "Wl").replace("b_l", "bl").replace("W_r", "Wr"),
             inputs["L0_gnn_" + name])
    for name in ("W_fx", "b_fx", "W_slice", "b_slice", "W_q", "W_k", "W_v", "W_out", "b_out", "temperature"):
        give(name, inputs["L0_ffn_" + name])
    wx, bx = np.asarray(inputs["L0_ffn_W_x"]), np.asarray(inputs["L0_ffn_b_x"])
    heads = inputs["L0_ffn_temperature"].shape[1]
    give("W_xT", wx.reshape(wx.shape[0], heads, -1).transpose(2, 1, 0))
    give("b_xT", bx.reshape(heads, -1).T)
    out = nc.dram_tensor("out_0", inputs["x"].shape, F32, kind="ExternalOutput").ap()
    bass_gnn_ffn_kernel(nc, out=out, **args)
    r = run(nc, [arrays], core_ids=[0])
    return r.results[0]["out_0"]
```

```python
from contextlib import ExitStack

import concourse.bass as bass
from concourse import mybir

ALU = mybir.AluOpType
ACT = mybir.ActivationFunctionType
AX_X = mybir.AxisListType.X
F32 = mybir.dt.float32
F16 = mybir.dt.float16
BF16 = mybir.dt.bfloat16
I32 = mybir.dt.int32
U32 = mybir.dt.uint32

P = 128
C = 256
KC = C // P


class Chain:

    def __init__(self, eng, sem):
        self.eng, self.sem, self.n, self.done = eng, sem, 0, 0

    def link(self, ins):
        ins.then_inc(self.sem, 1)
        self.n += 1
        self.eng.wait_ge(self.sem, self.done + self.n)

    def loop(self, passes, per):
        self.done = passes * per
        self.start, self.per = self.n, per

    def end(self, passes):
        assert self.n == self.start + self.per, (self.n - self.start, self.per)
        self.n, self.done = self.start + passes * self.per, 0


def bass_gnn_ffn_kernel(nc, x, src, dst, Wp1, bp1, Wl1, bl1, Wr1, Wp2, bp2, Wl2, bl2, Wr2,
                        W_fx, b_fx, W_xT, b_xT, W_slice, b_slice, W_q, W_k, W_v, W_out, b_out,
                        temperature, out):
    N = x.shape[0]
    E = src.shape[0]
    TN = 125
    T = N // TN
    D5 = 5
    Q = N // D5
    WIN = P
    COARSE = 512
    ROW = E // TN
    KEYS = T * D5
    CT = 4
    CN = CT * TN
    CH = T // CT
    H, G = temperature.shape[1], W_slice.shape[1]
    D = W_slice.shape[0]
    INNER = H * D
    EPS_LN, EPS_NORM, EPS_SLICE = 1e-5, 1e-12, 1e-5
    SCALE = D ** -0.5
    assert T * TN == N and Q * D5 == N and ROW * TN == E and CH * CT + 1 == T and TN == 5 * T
    assert C == 2 * P and H * G == 4 * P and D == 64 and G == 64

    SUB = 4
    GC = CN // D5 // SUB
    GROUPS = CH * GC + TN // D5 // SUB + 1
    assert GC * SUB * D5 == CN and (GROUPS - 1) * SUB + 1 == Q and GC == T
    OH_SLOT = [q % 3 for q in range(GC - 1)] + [1]
    OH_AGE = [4, 2, 4] + [3] * (GC - 4) + [2]
    BANK = [2 + q % 2 for q in range(GC)]
    BANK_AGE = [1, 3] + [2] * (GC - 2)
    LEAD = 12
    TURN_AT, PROJECT_AT, WL_AT = 14, 18, 23
    LAST_AT = [8, 12, 16, 21]
    EARLY = T - 6
    EARLY_GROUPS = {n: [g for g in range(LEAD) if g * (T + 2 - EARLY) // LEAD == n - EARLY] for n in range(EARLY, T + 2)}
    HG = H * G
    PAIRS = HG // P
    R = 4
    W_SCALE = 256.0
    RG = 5
    ROUNDS = ROW // RG
    GT = 5
    assert ROUNDS * RG == ROW and E % N == 0 and T % GT == 0
    g_sum_dram = nc.dram_tensor("g_sum_scratch", (T, TN, 2 * C), F32, kind="Internal").ap()
    g_y_dram = nc.dram_tensor("g_y_scratch", (N, 2 * C), F16, kind="Internal").ap()
    wxs_dram = nc.dram_tensor("wxs_scratch", (P, KC, HG), F32, kind="Internal").ap()
    bxs_dram = nc.dram_tensor("bxs_scratch", (3, HG), BF16, kind="Internal").ap()
    xr2_dram = nc.dram_tensor("xr2_scratch", (T, TN, C), F32, kind="Internal").ap()
    xr_dram = nc.dram_tensor("xr_scratch", (T, TN, C), F32, kind="Internal").ap()
    y2_dram = nc.dram_tensor("y2_scratch", (N, 2 * C), F16, kind="Internal").ap()
    x1_dram = nc.dram_tensor("x1_scratch", (T, TN, C), F32, kind="Internal").ap()
    cnt_dram = nc.dram_tensor("cnt_scratch", (N,), F32, kind="Internal").ap()
    x_t = x.rearrange("(t p) c -> t p c", p=TN)
    out_t = out.rearrange("(t p) c -> t p c", p=TN)
    y2_t = y2_dram.rearrange("(t p) c -> t p c", p=TN)

    with ExitStack() as ctx:
        def sb(name, shape, dt=F32):
            return ctx.enter_context(nc.sbuf_tensor(name, shape, dt))

        def sem(name):
            return ctx.enter_context(nc.semaphore(name))

        adj = sb("adj", [P, T, N + 1], F16)
        adj_words = T * (N + 1) // 2
        y = sb("y", [P, T, 2 * C], F16)
        ps = ctx.enter_context(nc.psum_tensor("ps", [P, 8, 512], F32))
        ident = sb("ident", [P, P])
        wp = sb("wp", [P, KC, C])
        wr = sb("wr", [P, KC, C])
        wl = sb("wl", [P, KC, C])
        bias_p = sb("bias_p", [P, KC])
        bias_l = sb("bias_l", [P, C])
        rcnt = sb("rcnt", [P, T])
        covered = sb("covered", [1, 2], I32)
        stats2 = sb("stats2", [P, T, 6])
        key_t = sb("key_t", [P, Q + 3], F16)
        low_t = sb("low_t", [P, Q + 3], F16)
        work_words = 4864
        work = sb("work", [P, work_words])

        class Region:

            def __init__(self, base, limit):
                self.base, self.at, self.limit = base, 0, limit

            def take(self, shape, dt=F32):
                n = 1
                for s in shape[1:]:
                    n *= s
                words = n if dt in (F32, I32) else (n + 1) // 2
                words = (words + 1) // 2 * 2
                assert self.at + words <= self.limit, (self.at + words, self.limit)
                v = self.base[:, self.at:self.at + words]
                self.at += words
                if dt != F32:
                    v = v.bitcast(dt)
                v = v[0:shape[0], 0:n]
                names = "abcd"[:len(shape) - 1]
                sizes = dict(zip(names[1:], shape[2:]))
                return v.rearrange(f"p ({' '.join(names)}) -> p {' '.join(names)}", **sizes) if len(shape) > 2 else v

        def over_adj():
            return Region(adj[:, :, :].rearrange("p a b -> p (a b)")[:, 0:2 * adj_words].bitcast(F32), adj_words)

        def over_work():
            return Region(work[:, :], work_words)

        r = over_adj()
        ones = r.take([P, P])
        rows = r.take([TN, ROW], I32)
        thr = r.take([TN, TN])
        base5 = r.take([TN, 5])
        own = r.take([TN, T])
        rowmax = r.take([TN, 1])
        step = r.take([TN, TN])
        r0 = r.take([TN, 1])
        r0_i = r.take([TN, 1], I32)
        picked = r.take([TN, ROW], I32)
        picked_f = r.take([TN, ROW])
        junk = r.take([TN, ROW])
        below = r.take([TN, 1])
        start = r.take([TN, 1])
        start_c = r.take([TN, 1])
        start_i = r.take([TN, 1], I32)
        coarse = r.take([TN, COARSE], I32)
        coarse_f = r.take([TN, COARSE])
        below5 = r.take([TN, 5])
        start5 = r.take([TN, 5])
        start5_i = r.take([TN, 5, 8], I32)
        win_d = r.take([TN, 5, WIN], I32)
        win_s = r.take([TN, 5, WIN], I32)
        hi_i = r.take([TN, 5, WIN], I32)
        low_f = r.take([TN, 5, WIN])
        win_f = r.take([TN, 5, WIN])
        dl = r.take([TN, 5, WIN])
        ge0 = r.take([TN, 5, WIN])
        valid = r.take([TN, 5, WIN])
        pair_f = r.take([TN, 5, WIN])
        key_f = r.take([TN, 5, WIN])
        junk25 = r.take([TN, T, WIN], F16)
        junk5 = r.take([TN, 5, COARSE], F16)
        cnt = r.take([TN, T])
        cnt_row = r.take([TN, 1])
        wxT = r.take([D, H, C])
        wsl = r.take([D, G])
        bxT = r.take([D, H])
        bsl = r.take([1, G])
        temp = r.take([1, H])
        rtemp = r.take([1, H])
        rtemp_row = r.take([1, H, G])
        rtemp_all = r.take([P, HG])
        wxs_o = r.take([P, KC, HG])
        bxs_t = r.take([1, H, G])
        bxs_o = r.take([1, H, G])
        bxs_rest = r.take([1, 2, HG])
        bxs_parts = r.take([1, 3, HG], BF16)

        r = over_work()
        o_t = r.take([TN, CT, C])
        x_in, xn = o_t[:, 0:2], o_t[:, 2:4]
        hT = r.take([P, 2, KC, TN])
        xpT = r.take([P, 2, KC, TN])
        xr_o = r.take([TN, 2, C])
        y_half = r.take([TN, 2, 2 * C], F16)
        mv = r.take([TN, 2, 2])
        st6 = r.take([TN, 6])
        std = r.take([TN, 2])
        rstd = r.take([TN, 1])
        eps = r.take([TN, 1])
        ss = r.take([TN, CT])
        nrm = r.take([TN, CT])
        inv = r.take([TN, CT])
        last_o, last_res = xr_o[:, 0, :], xr_o[:, 1, :]
        mark = r.at
        iota_low = r.take([P, P, 2], F16)
        iota_key = r.take([P, KEYS, 2], F16)
        oh_low = r.take([P, 3 * SUB // 2, P, 2], F16)
        oh_key = r.take([P, 3 * SUB // 2, KEYS, 2], F16)
        r.at = mark
        x_res = r.take([TN, CT, C])
        mean2 = r.take([TN, T])
        half2 = r.take([TN, T])
        var2 = r.take([TN, T])
        std2 = r.take([TN, T])
        rstd2 = r.take([TN, T])

        r = over_adj()
        g_src = r.take([TN, ROW + 1], I32)
        g_dst_i = r.take([TN, ROW], I32)
        g_dst = r.take([TN, ROW])
        g_rel = r.take([TN, ROW])
        g_iota = r.take([TN, GT * TN], F16)
        g_idx = r.take([TN, RG, 2], I32)
        g_rows = r.take([TN, RG, 2 * C], F16)
        g_oh = r.take([TN, RG, GT * TN], F16)
        g_sum = r.take([TN, GT, 2 * C])
        g_all_i = r.take([TN, N], I32)
        g_all = r.take([TN, N])
        g_eq = r.take([TN, N])
        g_node = r.take([TN, T])
        g_part = r.take([TN, T])
        g_cnt = r.take([TN, T])
        g_ring = y[:, :, :].rearrange("p t c -> p (t c)")[:, 0:CT * 4 * C].bitcast(F32).rearrange("p (j c) -> p j c", j=CT)

        r = over_adj()
        w_tr = r.take([P, 2 * PAIRS, N], F16)
        ident16 = r.take([P, P], F16)
        f_ones_row = r.take([1, TN])
        f_in = r.take([TN, R, C])
        f_xn = r.take([TN, R, C + 8])
        f_xh = r.take([TN, R, C + 8], F16)
        f_xl = r.take([TN, R, C], F16)
        f_wh = r.take([TN, R, HG], F16)
        f_wl = r.take([TN, R, HG], F16)
        f_xT = r.take([P, R, KC, TN])
        f_e = r.take([TN, R, HG])
        f_w = r.take([TN, R, HG])
        f_mx = r.take([TN, R, H])
        f_sm = r.take([TN, R, H])
        f_ss = r.take([TN, R, H])
        f_rs = r.take([TN, R, H])
        wxs = r.take([P, KC, HG])
        bxs = r.take([3, HG], BF16)
        f_ones3 = r.take([3, TN], BF16)
        wfx = r.take([P, KC, INNER])
        bfx = r.take([1, INNER])
        wq = r.take([D, D])
        wk = r.take([D, D])
        wv = r.take([D, D])
        wo = r.take([D, H, C])
        bo = r.take([1, C])
        sn_e = r.take([P, PAIRS])
        sn_inv = r.take([P, PAIRS])
        s_sb = r.take([P, PAIRS, C + 8])
        sT = r.take([P, KC, HG])
        nr = r.take([1, HG])
        tokT = r.take([D, HG])
        qT = r.take([D, HG])
        kT = r.take([D, HG])
        v_sb = r.take([G, HG])
        am = r.take([G, H])
        a_e = r.take([G, H, G])
        a_s = r.take([G, H])
        a_r = r.take([G, H])
        a_w = r.take([G, H, G])
        aT = r.take([G, HG])
        osT = r.take([D, HG])
        t_half = r.take([P, 2, PAIRS, C], F16)
        y_in = r.take([TN, R, C])
        y_o = r.take([TN, R, C])
        assert PAIRS == 4

        consts = sem("consts")
        rows_in, weights_in, fold_in = sem("rows_in"), sem("weights_in"), sem("fold_in")
        step_ready, r0_done, r0_ready, row_in = sem("step_ready"), sem("r0_done"), sem("r0_ready"), sem("row_in")
        start_ready, coarse_in, fine_ready = sem("start_ready"), sem("coarse_in"), sem("fine_ready")
        win_in = [sem(f"win_in{i}") for i in range(5)]
        keys_ready, turned, tables_ready = sem("keys_ready"), sem("turned"), sem("tables_ready")
        rt_row, rt_done, rt_ready, fold_done, fold_ready, fold_stored = (sem(n) for n in (
            "rt_row", "rt_done", "rt_ready", "fold_done", "fold_ready", "fold_stored"))
        cnt_out, cnt_in, rcnt_ready, bias_stored = sem("cnt_out"), sem("cnt_in"), sem("rcnt_ready"), sem("bias_stored")
        cnt_rows_ready, total_done, covered_ready = sem("cnt_rows_ready"), sem("total_done"), sem("covered_ready")
        g_tables_in, g_y_out, g_iota_ready, g_node_ready = (sem(n) for n in ("g_tables_in", "g_y_out", "g_iota_ready", "g_node_ready"))
        g_dst_ready, g_all_in, g_all_used, g_steps = (sem(n) for n in ("g_dst_ready", "g_all_in", "g_all_used", "g_steps"))
        g_free, g_idx_ready, g_oh_ready, g_rel_ready = (sem(n) for n in ("g_free", "g_idx_ready", "g_oh_ready", "g_rel_ready"))
        g_in = [sem(f"g_in{j}") for j in range(RG)]
        g_swept, g_sum_ready, g_sum_out = sem("g_swept"), sem("g_sum_ready"), sem("g_sum_out")
        g_sum_in = [sem(f"g_sum_in{j}") for j in range(CT)]
        oh_ready, built, stored = sem("oh_ready"), sem("built"), sem("adj_stored")
        x_loaded = [sem(f"x_loaded{i}") for i in range(2)]
        mv_ready, std_ready, xn_ready, h_ready = (sem(n) for n in ("mv_ready", "std_ready", "xn_ready", "h_ready"))
        x_turned, hT_ready, xpT_done, xpT_ready, xr_done, xr_ready, y_done, hi_ready, lo_ready = (
            [sem(f"{n}{k}") for k in range(2)] for n in (
                "x_turned", "hT_ready", "xpT_done", "xpT_ready", "xr_done", "xr_ready", "y_done", "hi_ready", "lo_ready"))
        xr_stored = [[sem(f"xr_stored{k}_{j}") for j in range(2)] for k in range(2)]
        y_half_stored = [sem(f"y_half_stored{j}") for j in range(2)]
        dve_steps, pool_steps = sem("dve_steps"), sem("pool_steps")
        agg_done, o_ready, sq_done, nrm_ready = ([sem(f"{n}{k}") for k in range(2)] for n in (
            "agg_done", "o_ready", "sq_done", "nrm_ready"))
        xr_loaded = [[sem(f"xr_loaded{k}_{j}") for j in range(CT)] for k in range(2)]
        res_loaded = [sem(f"res_loaded{j}") for j in range(CT)]
        last_in = sem("last_in")
        w2_in = sem("w2_in")
        y_in2 = [sem(f"y_in{j}") for j in range(3)]
        x1_ready, stats2_ready = sem("x1_ready"), sem("stats2_ready")
        x1_stored = [sem(f"x1_stored{j}") for j in range(CT)]
        var2_ready, std2_ready, slice_w_in, mid_w_in, f_ones = (sem(n) for n in (
            "var2_ready", "std2_ready", "slice_w_in", "mid_w_in", "f_ones"))
        f_loaded = [sem(f"f_loaded{j}") for j in range(R)]
        f_xn_ready, f_xt_done, f_xT_ready, lg_done, sub_ready, exp_ready, rs_ready, fw_ready, s_done, wT_done, wT_ready = (
            sem(n) for n in ("f_xn_ready", "f_xt_done", "f_xT_ready", "lg_done", "sub_ready", "exp_ready", "rs_ready",
                             "fw_ready", "s_done", "wT_done", "wT_ready"))
        mid_pe, mid_dve, mid_act = sem("mid_pe"), sem("mid_dve"), sem("mid_act")
        out_stored = [sem(f"out_stored{j}") for j in range(R)]
        out_done, out_ready = sem("out_done"), sem("out_ready")
        xh_ready, xl_ready, wh_ready, wl_ready = (sem(n) for n in ("xh_ready", "xl_ready", "wh_ready", "wl_ready"))

        block = ctx.enter_context(nc.Block())
        LAST = T - 1

        def is_last(n):
            return isinstance(n, int) and n == LAST
        wt16 = ps[:, 6, :].bitcast(F16).rearrange("p (i n) -> p i n", n=P)

        @block.sync
        def _(sp):
            def load_x(t, par):
                sp.dma_start(x_in[:, par, :], x_t[bass.ds(t, 1)].rearrange("a p c -> p (a c)")).then_inc(x_loaded[par], 16)

            def store_xr(n, par):
                sp.wait_ge(xr_ready[0], n + 1)
                sp.dma_start(xr_dram[bass.ds(n, 1)].rearrange("a p c -> p (a c)"), xr_o[:, par, :]).then_inc(xr_stored[0][par], 16)

            def load_layer(Wp, Wr, Wl, bp, bl, done):
                for w, d in ((wp, Wp), (wr, Wr), (wl, Wl)):
                    sp.dma_start(w[:, :, :], d.rearrange("(k p) c -> p k c", p=P)).then_inc(done, 16)
                sp.dma_start(bias_p[:, :], bp.rearrange("(k p) -> p k", p=P), allow_slow_non_contiguous=True).then_inc(done, 16)
                sp.dma_start(bias_l[:, :], bl.rearrange("(a c) -> a c", a=1).to_broadcast([P, C])).then_inc(done, 16)

            load_x(0, 0)
            sp.dma_start(rows, dst.rearrange("(p k) -> p k", k=ROW)).then_inc(rows_in, 16)
            load_x(1, 1)
            load_layer(Wp1, Wr1, Wl1, bp1, bl1, weights_in)
            sp.dma_start(temp, temperature.rearrange("a h b c -> a (h b c)")).then_inc(fold_in, 16)
            sp.dma_start(wxT, W_xT).then_inc(fold_in, 16)
            sp.dma_start(wsl, W_slice).then_inc(fold_in, 16)
            sp.dma_start(bxT, b_xT).then_inc(fold_in, 16)
            sp.dma_start(bsl, b_slice.rearrange("(a g) -> a g", a=1)).then_inc(fold_in, 16)
            sp.wait_ge(xn_ready, 1)
            load_x(2, 0)
            sp.wait_ge(xn_ready, 2)
            load_x(3, 1)
            sp.wait_ge(xn_ready, 3)
            load_x(4, 0)
            store_xr(0, 0)

            def load_and_store(i, par):
                t, m = 2 * i + 6 - par, 2 * i + 2 - par
                sp.wait_ge(xn_ready, 2 * i + 5 - par)
                load_x(t, par)
                store_xr(m, par)

            with sp.Fori(0, (T - 5) // 2) as i:
                load_and_store(i, 1)
                load_and_store(i, 0)
            for m in range(T - 4, T):
                store_xr(m, m % 2)

            def load_xr(k, n, j, first, chunk=0):
                if not first:
                    if k == 0:
                        sp.wait_ge(x_turned[1], n - CT + 1)
                    else:
                        sp.wait_ge(x1_stored[j], 16 * chunk)
                sp.dma_start(o_t[:, j, :], (xr_dram, xr2_dram)[k][bass.ds(n, 1)].rearrange("a p c -> p (a c)")).then_inc(xr_loaded[k][j], 16)

            sp.wait_ge(x_turned[0], T)
            sp.wait_ge(xn_ready, T)
            sp.wait_ge(xr_stored[0][0], 16 * (T // 2 + 1))
            sp.wait_ge(xr_stored[0][1], 16 * (T // 2))
            for j in range(CT):
                load_xr(0, j, j, True)
            sp.wait_ge(y_done[0], T)
            sp.wait_ge(xr_done[0], T)
            sp.wait_ge(xr_ready[0], T)
            sp.wait_ge(xpT_ready[0], T)
            load_layer(Wp2, Wr2, Wl2, bp2, bl2, w2_in)
            with sp.Fori(1, CH) as ch:
                for j in range(CT):
                    load_xr(0, CT * ch + j, j, False)
            load_xr(0, LAST, 0, False)

            sp.wait_ge(agg_done[0], T)
            y_all = y2_dram.rearrange("(t p) c -> p t c", p=TN)
            for piece in range(3):
                for j in range(2):
                    sp.wait_ge(y_half_stored[j], 16 * 4 * (piece + 1))
                sp.dma_start(y[0:TN, 8 * piece:8 * piece + 8, :], y_all[:, 8 * piece:8 * piece + 8, :]).then_inc(y_in2[piece], 16)

            def load_res(n, j, first):
                if not first:
                    sp.wait_ge(x1_ready, n - CT + 1)
                sp.dma_start(x_res[:, j, :], x_t[bass.ds(n, 1)].rearrange("a p c -> p (a c)")).then_inc(res_loaded[j], 16)

            for j in range(CT):
                load_res(j, j, True)
            sp.wait_ge(xr_stored[1][1], 16 * (T // 2))
            for j in range(1, CT):
                load_xr(1, j, j, True)
            sp.wait_ge(xr_stored[1][0], 16 * (T // 2 + 1))
            sp.wait_ge(x_turned[1], T)
            load_xr(1, 0, 0, True)
            sp.dma_start(last_o, xr2_dram[LAST]).then_inc(last_in, 16)
            sp.dma_start(last_res, x_t[LAST]).then_inc(last_in, 16)
            with sp.Fori(1, CH) as ch:
                for j in range(CT):
                    load_xr(1, CT * ch + j, j, False, ch)
                    load_res(CT * ch + j, j, False)

            sp.wait_ge(agg_done[1], T)
            sp.wait_ge(fold_stored, 16)
            sp.wait_ge(bias_stored, 16)
            sp.dma_start(wxs, wxs_dram).then_inc(slice_w_in, 16)
            sp.dma_start(bxs, bxs_dram).then_inc(slice_w_in, 16)

            def load_f(t, j, first):
                if not first:
                    sp.wait_ge(f_xn_ready, t - R + 1)
                sp.dma_start(f_in[:, j, :], x1_dram[bass.ds(t, 1)].rearrange("a p c -> p (a c)")).then_inc(f_loaded[j], 16)

            for j in range(CT):
                sp.wait_ge(x1_stored[j], 16)
                load_f(j, j, True)
            sp.dma_start(wfx, W_fx.rearrange("(k p) c -> p k c", p=P)).then_inc(mid_w_in, 16)
            sp.dma_start(bfx, b_fx.rearrange("(a c) -> a c", a=1)).then_inc(mid_w_in, 16)
            for w, d in ((wq, W_q), (wk, W_k), (wv, W_v)):
                sp.dma_start(w, d).then_inc(mid_w_in, 16)
            sp.dma_start(wo, W_out.rearrange("(h d) c -> d h c", d=D)).then_inc(mid_w_in, 16)
            sp.dma_start(bo, b_out.rearrange("(a c) -> a c", a=1)).then_inc(mid_w_in, 16)
            for j in range(CT):
                sp.wait_ge(x1_stored[j], 16 * CH)
            with sp.Fori(1, CH) as ch:
                for j in range(R):
                    load_f(R * ch + j, j, False)
            sp.wait_ge(x1_stored[0], 16 * (CH + 1))
            load_f(LAST, 0, False)

            sp.wait_ge(f_xn_ready, T)
            def load_out(t, j):
                if not isinstance(t, int) or t >= R:
                    sp.wait_ge(out_ready, t - R + 1)
                sp.dma_start(y_in[:, j, :], x1_dram[bass.ds(t, 1)].rearrange("a p c -> p (a c)")).then_inc(f_loaded[j], 16)

            for j in range(R):
                load_out(j, j)
            with sp.Fori(1, CH) as i:
                for j in range(R):
                    load_out(R * i + j, j)
            load_out(LAST, 0)

        @block.gpsimd
        def _(pool):
            ch_ = Chain(pool, pool_steps)
            small = dict(allow_small_or_imprecise_dtypes=True)
            pool.memset(eps, EPS_LN).then_inc(consts, 1)
            pool.iota(thr, [[T, TN]], base=0, channel_multiplier=0, **small).then_inc(consts, 1)
            ch_.link(pool.memset(ones, 1.0))
            pool.affine_select(out=ident[:, :], in_=ones, compare_op=ALU.is_equal, fill=0.0, base=0,
                               pattern=[[-1, P]], channel_multiplier=1).then_inc(consts, 1)
            pool.iota(base5, [[D5, 5]], base=0, channel_multiplier=T, **small)
            pool.iota(own, [[1, T]], base=0, channel_multiplier=T, **small).then_inc(consts, 1)
            pool.iota(iota_low, [[1, P], [0, 2]], base=0, channel_multiplier=0, **small)
            pool.iota(iota_key, [[1, KEYS], [0, 2]], base=1, channel_multiplier=0, **small)
            pool.memset(key_t[:, Q:Q + 3], 0.0)
            pool.memset(low_t[:, Q:Q + 3], 0.0).then_inc(consts, 1)

            pool.wait_ge(r0_ready, 1)
            pool.indirect_dma_start(picked, None, dst.rearrange("(p k) -> p k", k=ROW),
                                    bass.IndirectOffsetOnAxis(ap=r0_i.bitcast(U32), axis=0)).then_inc(row_in, 16)
            dst_1, src_1 = dst.rearrange("(e a) -> e a", a=1), src.rearrange("(e a) -> e a", a=1)
            pool.wait_ge(start_ready, 1)
            pool.indirect_dma_start(coarse, None, dst_1,
                                    bass.IndirectOffsetOnAxis(ap=start_i.bitcast(U32), axis=0)).then_inc(coarse_in, 16)
            pool.wait_ge(fine_ready, 1)
            for i in range(5):
                at = bass.IndirectOffsetOnAxis(ap=start5_i[:, i, 0:1].bitcast(U32), axis=0)
                pool.indirect_dma_start(win_d[:, i, :], None, dst_1, at).then_inc(win_in[i], 16)
                pool.indirect_dma_start(win_s[:, i, :], None, src_1, at).then_inc(win_in[i], 16)

            pool.wait_ge(fold_ready, 2)
            rest = bxs_o.rearrange("a h g -> a (h g)")
            for part in range(3):
                ch_.link(pool.tensor_copy(bxs_parts[:, part, :], rest))
                if part < 2:
                    ch_.link(pool.tensor_tensor(bxs_rest[:, part, :], rest, bxs_parts[:, part, :], ALU.subtract))
                    rest = bxs_rest[:, part, :]
            pool.dma_start(bxs_dram.rearrange("(a k) c -> a k c", a=1), bxs_parts).then_inc(bias_stored, 16)
            pool.dma_start(wxs_dram, wxs_o).then_inc(fold_stored, 16)
            pool.wait_ge(cnt_rows_ready, 1)
            pool.dma_start(cnt_dram.rearrange("(p c) -> p c", c=T), cnt).then_inc(cnt_out, 16)
            pool.wait_ge(cnt_out, 16)
            pool.dma_start(rcnt[0:TN, :], cnt_dram.rearrange("(t p) -> p t", p=TN), allow_slow_non_contiguous=True).then_inc(cnt_in, 16)


            def general_tables(k):
                pool.dma_start(g_src[:, 0:ROW], src.rearrange("(p k) -> p k", k=ROW)).then_inc(g_tables_in, 16)
                pool.dma_start(g_dst_i, dst.rearrange("(p k) -> p k", k=ROW)).then_inc(g_tables_in, 16)
                pool.iota(g_iota, [[1, GT * TN]], base=0, channel_multiplier=0, **small).then_inc(g_iota_ready, 1)
                pool.wait_ge(g_tables_in, 32 * (k + 1))
                pool.tensor_copy(g_src[:, ROW:ROW + 1], g_src[:, 0:1]).then_inc(g_idx_ready, 1)
                pool.tensor_copy(g_idx[:, 0, 0:1], g_src[:, 0:1]).then_inc(g_idx_ready, 1)

            pool.wait_ge(covered_ready, 1)
            is_covered = pool.value_load(covered[0:1, 0:1], min_val=0, max_val=1)
            with pool.If(is_covered == 1):
                pool.nop()
            with pool.Else():
                pool.wait_ge(lo_ready[0], T)
                pool.wait_ge(stored, LEAD)
                pool.wait_ge(cnt_out, 16)
                pool.wait_ge(fold_stored, 16)
                pool.wait_ge(bias_stored, 16)
                pool.wait_ge(total_done, 1)
                general_tables(0)
                pool.dma_start(g_y_dram.rearrange("(t p) c -> p t c", p=TN), y[0:TN, :, :]).then_inc(g_y_out, 16)
                pool.iota(g_node, [[TN, T]], base=0, channel_multiplier=1, **small).then_inc(g_node_ready, 1)
                pieces = dst.rearrange("(s n) -> s n", n=N)
                pool.dma_start(g_all_i, pieces[0:1].to_broadcast([TN, N])).then_inc(g_all_in, 16)
                with pool.Fori(1, E // N) as s_:
                    pool.wait_ge(g_all_used, s_)
                    pool.dma_start(g_all_i, pieces[bass.ds(s_, 1)].to_broadcast([TN, N])).then_inc(g_all_in, 16)
                pool.wait_ge(g_y_out, 16)
            pool.nop()

            def general_gathers(k):
                table = g_y_dram if k == 0 else y2_dram

                def sweep(s_):
                    chunk = (T // GT) * k + s_

                    def group(i, slot):
                        u = ROW * chunk + RG * i + slot
                        pool.wait_ge(g_free, u + 2)
                        pool.wait_ge(g_idx_ready, u + 2 * k + 2)
                        pool.tensor_copy(g_idx[:, (slot + 1) % RG, 0:1], g_src[:, bass.ds(RG * i + slot + 1, 1)]
                                         ).then_inc(g_idx_ready, 1)
                        pool.indirect_dma_start(g_rows[:, slot, :], None, table,
                                                bass.IndirectOffsetOnAxis(ap=g_idx[:, slot, 0:1].bitcast(U32), axis=0)
                                                ).then_inc(g_in[slot], 16)

                    with pool.Fori(0, ROUNDS) as i:
                        for slot in range(RG):
                            group(i, slot)
                    pool.wait_ge(g_sum_ready, chunk + 1)
                    pool.dma_start(g_sum_dram[bass.ds(GT * s_, GT)].rearrange("t p c -> p t c"), g_sum).then_inc(g_sum_out, 16)

                with pool.If(is_covered == 1):
                    pool.nop()
                with pool.Else():
                    if k:
                        pool.wait_ge(stored, GROUPS)
                        pool.wait_ge(agg_done[0], T)
                        general_tables(1)
                    with pool.Fori(0, T // GT) as s_:
                        sweep(s_)
                    pool.wait_ge(g_sum_out, 16 * (T // GT) * (k + 1))
                pool.nop()

            def general_sums_back(k, ch, tiles):
                with pool.If(is_covered == 1):
                    pool.nop()
                with pool.Else():
                    for j in range(tiles):
                        n = CT * ch + j
                        if not isinstance(ch, int) or ch > 0:
                            pool.wait_ge(agg_done[k], n - CT + 1)
                        pool.dma_start(g_ring[0:TN, j, :], g_sum_dram[bass.ds(n, 1)].rearrange("a p c -> p (a c)")
                                       ).then_inc(g_sum_in[j], 16)
                pool.nop()

            def store_2(n, par, half=True):
                pool.wait_ge(lo_ready[1], n + 1)
                pool.dma_start(y2_t[bass.ds(n, 1)].rearrange("a p c -> p (a c)"),
                               y_half[:, par, :] if half else y[0:TN, LAST, :]).then_inc(y_half_stored[par], 16)
                pool.wait_ge(xr_ready[1], n + 1)
                pool.dma_start(xr2_dram[bass.ds(n, 1)].rearrange("a p c -> p (a c)"), xr_o[:, par, :]).then_inc(xr_stored[1][par], 16)

            general_gathers(0)
            general_sums_back(0, 0, CT)
            with pool.Fori(1, CH) as ch:
                general_sums_back(0, ch, CT)
                for j in range(CT):
                    store_2(CT * (ch - 1) + j, j % 2)
            general_sums_back(0, CH, 1)
            for j in range(CT):
                store_2(CT * (CH - 1) + j, j % 2)
            store_2(LAST, 0, False)
            for j in range(2):
                pool.wait_ge(y_half_stored[j], 16 * (T // 2 + 1 - j))

            def store_x1(n, j):
                pool.wait_ge(stats2_ready, n + 1)
                pool.dma_start(x1_dram[bass.ds(n, 1)].rearrange("a p c -> p (a c)"), last_o if is_last(n) else o_t[:, j, :]
                               ).then_inc(x1_stored[j], 16)

            general_gathers(1)
            for piece in range(3):
                pool.wait_ge(y_in2[piece], 16)
            general_sums_back(1, 0, CT)
            with pool.Fori(1, CH) as ch:
                general_sums_back(1, ch, CT)
                for j in range(CT):
                    store_x1(CT * (ch - 1) + j, j)
            general_sums_back(1, CH, 1)
            pool.wait_ge(agg_done[1], T)
            pool.memset(f_ones3, 1.0)
            pool.tensor_copy(ident16, ident[:, :])
            pool.memset(f_ones_row, 1.0)
            pool.memset(f_xn[:, :, C:C + 1], 1.0).then_inc(f_ones, 1)
            for j in range(CT):
                store_x1(CT * (CH - 1) + j, j)
            store_x1(LAST, 0)


            def row_lows(t, j):
                pool.wait_ge(xh_ready, t + 1)
                if not isinstance(t, int) or t >= R:
                    pool.wait_ge(s_done, t - R + 1)
                pool.tensor_tensor(f_xl[:, j, :], f_xn[:, j, 0:C], f_xh[:, j, 0:C], ALU.subtract).then_inc(xl_ready, 1)

            def quotient(t, j):
                pool.wait_ge(rs_ready, t + 1)
                if not isinstance(t, int) or t >= R:
                    pool.wait_ge(wl_ready, t - R + 1)
                pool.tensor_tensor(f_w[:, j, :].rearrange("p (h g) -> p h g", h=H), f_e[:, j, :].rearrange("p (h g) -> p h g", h=H),
                                   f_rs[:, j, :].unsqueeze(2).to_broadcast([TN, H, G]), ALU.mult).then_inc(fw_ready, 1)

            def weight_lows(t, j):
                pool.wait_ge(wh_ready, t + 1)
                if not isinstance(t, int) or t >= R:
                    pool.wait_ge(wT_done, t - R + 1)
                pool.tensor_tensor(f_wl[:, j, :], f_w[:, j, :], f_wh[:, j, :], ALU.subtract).then_inc(wl_ready, 1)

            def halves(q, j):
                if not isinstance(q, int) or q < T:
                    row_lows(q, j)
                if not isinstance(q, int) or q >= 2:
                    weight_lows(q - 2, (j - 2) % R)
                if not isinstance(q, int) or 1 <= q <= T:
                    quotient(q - 1, (j - 1) % R)

            for q in range(2 * R):
                halves(q, q % R)
            with pool.Fori(2, CH) as i:
                for j in range(R):
                    halves(R * i + j, j)
            for q in range(R * CH, T + 2):
                halves(q, q % R)

            def store_out(t, j):
                pool.wait_ge(out_ready, t + 1)
                pool.dma_start(out_t[bass.ds(t, 1)].rearrange("a p c -> p (a c)"), y_o[:, j, :]).then_inc(out_stored[j], 16)

            for j in range(R):
                store_out(j, j)
            with pool.Fori(1, CH) as i:
                for j in range(R):
                    store_out(R * i + j, j)
            store_out(LAST, 0)
            for j in range(R):
                pool.wait_ge(out_stored[j], 16 * (CH + (j == 0)))

        @block.tensor
        def _(pe):
            def turn(k, n, src):
                pe.wait_ge((xn_ready, h_ready)[k], n + 1)
                if not isinstance(n, int) or n >= 1:
                    pe.wait_ge(hT_ready[k], n)
                for kc in range(KC):
                    last = pe.transpose(ps[:, 4, kc * TN:(kc + 1) * TN], src[:, kc * P:(kc + 1) * P], ident[0:TN, 0:TN])
                last.then_inc(x_turned[k], 1)

            def project(k, n, par):
                pe.wait_ge(hT_ready[k], n + 1)
                if not isinstance(n, int) or n >= 1:
                    pe.wait_ge(xpT_ready[k], n)
                for mc in range(KC):
                    for kc in range(KC):
                        last = pe.matmul(ps[:, 5, mc * TN:(mc + 1) * TN], wp[:, kc, mc * P:(mc + 1) * P], hT[:, par, kc, :],
                                         start=(kc == 0), stop=(kc == 1))
                last.then_inc(xpT_done[k], 1)
                if not isinstance(n, int) or n >= 1:
                    pe.wait_ge(xr_ready[k], n)
                for kc in range(KC):
                    last = pe.matmul(ps[0:TN, 7, 0:C], hT[:, par, kc, :], wr[:, kc, :], start=(kc == 0), stop=(kc == 1))
                last.then_inc(xr_done[k], 1)

            def times_wl(k, n, par):
                pe.wait_ge(xpT_ready[k], n + 1)
                if not isinstance(n, int) or n >= 1:
                    pe.wait_ge(lo_ready[k], n)
                for kc in range(KC):
                    last = pe.matmul(ps[0:TN, 6, 0:C], xpT[:, par, kc, :], wl[:, kc, :], start=(kc == 0), stop=(kc == 1))
                last.then_inc(y_done[k], 1)

            def front(n, par):
                if not isinstance(n, int) or n < T:
                    turn(0, n, xn[:, par, :])
                if not isinstance(n, int) or n >= 2:
                    times_wl(0, n - 2, par)
                if not isinstance(n, int) or 1 <= n <= T:
                    project(0, n - 1, 1 - par)

            def count(g, q):
                q %= GC
                bank, slot = BANK[q], OH_SLOT[q]
                pe.wait_ge(oh_ready, g + 1)
                if not isinstance(g, int) or g >= BANK_AGE[q]:
                    pe.wait_ge(stored, g - BANK_AGE[q] + 1)
                for a in range(SUB):
                    last = pe.matmul(ps[:, bank, a * KEYS:(a + 1) * KEYS], oh_low[:, slot * 2 + a // 2, :, a % 2],
                                     oh_key[:, slot * 2 + a // 2, :, a % 2], start=True, stop=True)
                last.then_inc(built, 1)

            pe.wait_ge(consts, 3)
            pe.wait_ge(step_ready, 1)
            pe.matmul(ps[0:TN, 3, 0:1], step, ones[0:TN, 0:1], start=True, stop=True).then_inc(r0_done, 1)
            front(0, 0)
            pe.wait_ge(weights_in, 16 * 5)
            for n in range(1, 5):
                front(n, n % 2)
            pe.wait_ge(fold_in, 16 * 5)
            for kc in range(KC):
                for h in range(H):
                    last = pe.matmul(ps[:, kc, h * G:(h + 1) * G], wxT[:, h, kc * P:(kc + 1) * P], wsl, start=True, stop=True)
            for h in range(H):
                last = pe.matmul(ps[0:1, 2, h * G:(h + 1) * G], bxT[:, h:h + 1], wsl, start=True, stop=True)
            last.then_inc(fold_done, 1)
            pe.wait_ge(rt_row, 1)
            pe.wait_ge(r0_ready, 1)
            pe.matmul(ps[:, 3, :], ones[0:1, :], rtemp_row.rearrange("a h g -> a (h g)"), start=True, stop=True).then_inc(rt_done, 1)
            front(5, 1)
            with pe.Fori(0, 3) as i:
                front(2 * i + 6, 0)
                front(2 * i + 7, 1)
            front(12, 0)
            pe.wait_ge(fold_ready, 2)
            pe.wait_ge(keys_ready, 1)
            for i in range(5):
                if i >= 3:
                    pe.wait_ge(tables_ready, 2 * (i - 2))
                pe.transpose(ps[:, i % 3, 0:TN], key_f[:, i, :], ident[0:TN, 0:TN])
                pe.transpose(ps[:, i % 3, P:P + TN], low_f[:, i, :], ident[0:TN, 0:TN]).then_inc(turned, 1)
                front(13 + i, (13 + i) % 2)
            front(18, 0)
            pe.wait_ge(rt_ready, 1)
            pe.wait_ge(cnt_rows_ready, 1)
            pe.matmul(ps[0:1, 3, 0:1], cnt_row, ones[0:TN, 0:1], start=True, stop=True).then_inc(total_done, 1)
            pe.wait_ge(covered_ready, 1)
            pe.wait_ge(tables_ready, 10)
            for n in range(EARLY, T + 2):
                front(n, n % 2)
                for g in EARLY_GROUPS[n]:
                    count(g, g)
            pe.wait_ge(lo_ready[0], T)
            pe.wait_ge(xr_ready[0], T)
            is_covered = pe.value_load(covered[0:1, 0:1], min_val=0, max_val=1)

            def sum_tile(k, ch, j, general, steps):
                n = CT * ch + j
                if not isinstance(n, int) or n >= 2:
                    pe.wait_ge(sq_done[k], n - 1)
                if k == 0 and not general:
                    pe.wait_ge(stored, GC * ch + -(-T * (j + 1) // SUB) if not isinstance(n, int) or n < LAST else GROUPS)
                if general:
                    pe.wait_ge(g_sum_in[j], 16 * (ch + 1 + k * (CH + (j == 0))))
                    pe.matmul(ps[0:TN, j % 2, :], ident[0:TN, 0:TN], g_ring[0:TN, j, :], start=True, stop=True).then_inc(agg_done[k], 1)
                for t in range(T):
                    if not general:
                        if k == 1 and isinstance(n, int) and n == 0:
                            if t == LAST:
                                pe.wait_ge(lo_ready[1], T)
                            elif t % 8 == 0:
                                pe.wait_ge(y_in2[t // 8], 16)
                        last = pe.matmul(ps[0:TN, j % 2, :], adj[0:TN, t, bass.ds(TN * n, TN)], y[0:TN, t, :],
                                         start=(t == 0), stop=(t == LAST))
                        if t == LAST:
                            last.then_inc(agg_done[k], 1)
                    steps(t)

            def layer_1(general):
                def chunk(ch, groups, nexts):
                    for j in range(CT):
                        def steps(t):
                            s = T * j + t
                            if s % SUB == 0 and s // SUB < groups:
                                count(GC * ch + LEAD + s // SUB, LEAD + s // SUB)
                            if nexts and t == TURN_AT:
                                turn(1, CT * (ch - 1) + j, o_t[:, j, :])
                            if nexts and t == PROJECT_AT:
                                project(1, CT * (ch - 1) + j, j % 2)
                            if nexts and t == WL_AT:
                                times_wl(1, CT * (ch - 1) + j, j % 2)
                        sum_tile(0, ch, j, general, steps)

                chunk(0, GC, False)
                pe.wait_ge(w2_in, 16 * 5)
                chunk(1, GC, True)
                with pe.Fori(2, CH - 1) as ch:
                    chunk(ch, GC, True)
                chunk(CH - 1, GROUPS - GC * (CH - 1) - LEAD, True)

                def next_step(p):
                    if p < CT:
                        turn(1, CT * (CH - 1) + p, o_t[:, p, :])
                    if 2 <= p:
                        times_wl(1, CT * (CH - 1) + p - 2, p % 2)
                    if 1 <= p <= CT:
                        project(1, CT * (CH - 1) + p - 1, (p - 1) % 2)

                def steps(t):
                    if t in LAST_AT:
                        next_step(LAST_AT.index(t))
                sum_tile(0, CH, 0, general, steps)
                for p in range(len(LAST_AT), CT + 2):
                    next_step(p)
                turn(1, LAST, o_t[:, 0, :])
                project(1, LAST, 0)
                times_wl(1, LAST, 0)

            def layer_2(general):
                def chunk(ch, tiles=CT):
                    for j in range(tiles):
                        sum_tile(1, ch, j, general, lambda t: None)

                pe.wait_ge(sq_done[0], T)
                chunk(0)
                with pe.Fori(1, CH) as ch:
                    chunk(ch)
                chunk(CH, 1)

            def general_sweeps(k):
                def sweep(s_):
                    chunk = (T // GT) * k + s_

                    def group(i, slot, first=False, final=False):
                        pe.wait_ge(g_in[slot], 16 * (ROUNDS * chunk + i + 1))
                        pe.wait_ge(g_oh_ready, ROW * chunk + RG * i + slot + 1)
                        for b in range(GT):
                            last = pe.matmul(ps[0:TN, b, :], g_oh[:, slot, b * TN:(b + 1) * TN], g_rows[:, slot, :],
                                             start=first, stop=final)
                            if first and b == 0:
                                last.then_inc(g_free, 1)
                        last.then_inc(g_swept if final else g_free, 1)

                    if not isinstance(chunk, int) or chunk > 0:
                        pe.wait_ge(g_sum_ready, chunk)
                    for slot in range(RG):
                        group(0, slot, first=slot == 0)
                    with pe.Fori(1, ROUNDS - 1) as i:
                        for slot in range(RG):
                            group(i, slot)
                    for slot in range(RG):
                        group(ROUNDS - 1, slot, final=slot == RG - 1)

                sweep(0)
                with pe.Fori(1, T // GT) as s_:
                    sweep(s_)
                pe.wait_ge(g_sum_out, 16 * (T // GT) * (k + 1))
                pe.wait_ge(g_idx_ready, (ROW * (T // GT) + 2) * (k + 1))

            with pe.If(is_covered == 1):
                layer_1(False)
                layer_2(False)
            with pe.Else():
                pe.nop().then_inc(g_free, RG - 1)
                general_sweeps(0)
                layer_1(True)
                pe.wait_ge(sq_done[0], T)
                pe.wait_ge(lo_ready[1], T)
                pe.wait_ge(xr_ready[1], T)
                general_sweeps(1)
                layer_2(True)
            pe.nop()

            def turn_f(t, j):
                pe.wait_ge(f_xn_ready, t + 1)
                if not (isinstance(t, int) and t == 0):
                    pe.wait_ge(f_xT_ready, t)
                for kc in range(KC):
                    last = pe.transpose(ps[:, 5, kc * TN:(kc + 1) * TN], f_xn[:, j, kc * P:(kc + 1) * P], ident[0:TN, 0:TN])
                last.then_inc(f_xt_done, 1)

            def logits(t, j):
                pe.wait_ge(f_xT_ready, t + 1)
                if not isinstance(t, int) or t >= 2:
                    pe.wait_ge(sub_ready, t - 1)
                to = ps[0:TN, 4 if j % 2 == 0 else 7, :]
                for kc in range(KC):
                    pe.matmul(to, f_xT[:, j, kc, :], wxs[:, kc, :], start=(kc == 0), stop=False)
                pe.matmul(to, f_ones3, bxs, start=False, stop=True).then_inc(lg_done, 1)

            def gather_slices(t, j, first, last_):
                pe.wait_ge(wl_ready, t + 1)
                pe.wait_ge(xl_ready, t + 1)
                for k in range(PAIRS):
                    high, low = f_wh[:, j, k * P:(k + 1) * P], f_wl[:, j, k * P:(k + 1) * P]
                    pe.matmul(ps[:, k, 0:C + 1], high, f_xh[:, j, 0:C + 1], start=first, stop=False)
                    pe.matmul(ps[:, k, 0:C], high, f_xl[:, j, :], start=False, stop=False)
                    last = pe.matmul(ps[:, k, 0:C + 1], low, f_xh[:, j, 0:C + 1], start=False, stop=last_)
                last.then_inc(s_done, 1)
                if not first:
                    pe.wait_ge(wT_ready, t)
                for half, w in enumerate((f_wh, f_wl)):
                    for k in range(PAIRS):
                        last = pe.transpose(wt16[:, half * PAIRS + k, 0:TN], w[:, j, k * P:(k + 1) * P], ident16[0:TN, 0:TN])
                last.then_inc(wT_done, 1)

            def slice_pass(p, j, front=True, back=True):
                if front:
                    turn_f(p, j)
                if back:
                    gather_slices(p - 3, (j - 3) % R, isinstance(p, int) and p == 3, isinstance(p, int) and p == T + 2)
                if front:
                    logits(p, j)

            pe.wait_ge(f_ones, 1)
            pe.wait_ge(slice_w_in, 32)
            for p in range(3):
                slice_pass(p, p, back=False)
            pe.wait_ge(sq_done[1], T)
            slice_pass(3, 3)
            with pe.Fori(1, CH) as i:
                for j in range(R):
                    slice_pass(R * i + j, j)
            for p in range(R * CH, T + 3):
                slice_pass(p, p % R, front=p < T)

            pe.wait_ge(mid_w_in, 16 * 7)
            pe.wait_ge(mid_dve, 1)
            for kc in range(KC):
                for k in range(PAIRS):
                    pe.transpose(ps[:, 4 + kc, k * P:(k + 1) * P], s_sb[:, k, kc * P:(kc + 1) * P], ident[:, :])
            pe.wait_ge(wT_ready, T)
            for k in range(PAIRS):
                last = pe.transpose(ps[0:1, 6, k * P:(k + 1) * P], s_sb[:, k, C:C + 1], ident[:, :])
            last.then_inc(mid_pe, 1)
            pe.wait_ge(mid_dve, 2)
            pe.wait_ge(mid_act, 1)
            for h in range(H):
                hs = slice(h * D, (h + 1) * D)
                for kc in range(KC):
                    pe.matmul(ps[0:D, 7, hs], wfx[:, kc, hs], sT[:, kc, hs], start=(kc == 0), stop=False)
                last = pe.matmul(ps[0:D, 7, hs], bfx[:, hs], nr[:, hs], start=False, stop=True)
            last.then_inc(mid_pe, 1)
            pe.wait_ge(mid_dve, 3)
            pe.matmul(ps[0:D, 4, :], wq, tokT, start=True, stop=True).then_inc(mid_pe, 1)
            pe.matmul(ps[0:D, 5, :], wk, tokT, start=True, stop=True).then_inc(mid_pe, 1)
            for h in range(H):
                hs = slice(h * G, (h + 1) * G)
                last = pe.matmul(ps[0:G, 6, h * D:(h + 1) * D], tokT[:, hs], wv, start=True, stop=True)
            last.then_inc(mid_pe, 1)
            pe.wait_ge(mid_dve, 4)
            pe.wait_ge(mid_act, 2)
            for h in range(H):
                hs = slice(h * G, (h + 1) * G)
                last = pe.matmul(ps[0:G, 7, hs], qT[:, hs], kT[:, hs], start=True, stop=True)
            last.then_inc(mid_pe, 1)
            pe.wait_ge(mid_dve, 6)
            for h in range(H):
                last = pe.transpose(ps[0:G, 4, h * G:(h + 1) * G], a_w[:, h, :], ident[0:G, 0:G])
            last.then_inc(mid_pe, 1)
            pe.wait_ge(mid_act, 3)
            pe.wait_ge(mid_dve, 7)
            for h in range(H):
                last = pe.matmul(ps[0:D, 5, h * G:(h + 1) * G], v_sb[:, h * D:(h + 1) * D], aT[:, h * G:(h + 1) * G],
                                 start=True, stop=True)
            last.then_inc(mid_pe, 1)
            pe.wait_ge(mid_dve, 8)
            for h in range(H):
                k = h // 2
                to = ps[(h % 2) * G:(h % 2 + 1) * G, 6 + k // 2, (k % 2) * C:(k % 2 + 1) * C]
                last = pe.matmul(to, osT[:, h * G:(h + 1) * G], wo[:, h, :], start=True, stop=h > 0)
                if h == 0:
                    pe.matmul(to, f_ones_row[:, 0:G], bo, start=False, stop=True)
            last.then_inc(mid_pe, 1)

            def outputs(t, j):
                if not isinstance(t, int) or t >= R:
                    pe.wait_ge(out_ready, t - R + 1)
                terms = [(a, b, k) for k in range(PAIRS) for a, b in ((0, 0), (0, 1), (1, 0))]
                for a, b, k in terms:
                    last = pe.matmul(ps[0:TN, j, 0:C], w_tr[:, a * PAIRS + k, bass.ds(TN * t, TN)], t_half[:, b, k, :],
                                     start=(a, b, k) == terms[0], stop=(a, b, k) == terms[-1])
                last.then_inc(out_done, 1)

            pe.wait_ge(mid_dve, 10)
            pe.wait_ge(wT_ready, T)
            for j in range(R):
                outputs(j, j)
            with pe.Fori(1, CH) as i:
                for j in range(R):
                    outputs(R * i + j, j)
            outputs(LAST, 0)

        @block.scalar
        def _(act):
            def std_of(n, par):
                act.wait_ge(mv_ready, n + 1)
                act.activation(std[:, par:par + 1], mv[:, par, 1:2], ACT.Sqrt, bias=eps).then_inc(std_ready, 1)

            def turned_x(k, n, par):
                act.wait_ge(x_turned[k], n + 1)
                if not isinstance(n, int) or n >= 2:
                    act.wait_ge(xr_done[k], n - 1)
                act.activation(hT[:, par].rearrange("p k n -> p (k n)"), ps[:, 4, 0:KC * TN], ACT.Copy).then_inc(hT_ready[k], 1)

            def projected(k, n, par):
                act.wait_ge(xpT_done[k], n + 1)
                if not isinstance(n, int) or n >= 2:
                    act.wait_ge(y_done[k], n - 1)
                for mc in range(KC):
                    last = act.activation(xpT[:, par, mc, :], ps[:, 5, mc * TN:(mc + 1) * TN], ACT.Relu, bias=bias_p[:, mc:mc + 1])
                last.then_inc(xpT_ready[k], 1)

            def high(k, n, to):
                act.wait_ge(y_done[k], n + 1)
                act.activation(to, ps[0:TN, 6, 0:C], ACT.Copy).then_inc(hi_ready[k], 1)

            def table(i, at, to):
                act.wait_ge(turned, i + 1)
                act.activation(to[:, 0:Q].rearrange("e (p i) -> e i p", i=5)[:, i, :], ps[:, i % 3, at:at + TN],
                               ACT.Copy).then_inc(tables_ready, 1)

            def front(n, par):
                if not isinstance(n, int) or n < T:
                    turned_x(0, n, par)
                if not isinstance(n, int) or n >= 2:
                    high(0, n - 2, y[0:TN, bass.ds(n - 2, 1), 0:C].rearrange("p a c -> p (a c)"))
                if not isinstance(n, int) or 1 <= n <= T:
                    projected(0, n - 1, 1 - par)
                if not isinstance(n, int) or n + 2 < T:
                    std_of(n + 2, par)

            def store_counts(g, q):
                act.wait_ge(built, g + 1)
                if isinstance(g, int) and g == GROUPS - 1:
                    act.activation(adj[:, :, N - D5:N], ps[:, BANK[q % GC], 0:KEYS].rearrange("p (s d) -> p s d", s=T),
                                   ACT.Copy).then_inc(stored, 1)
                    return
                act.activation(adj[:, :, bass.ds(g * SUB * D5, SUB * D5)].rearrange("p s (q d) -> p q s d", q=SUB),
                               ps[:, BANK[q % GC], 0:SUB * KEYS].rearrange("p (q s d) -> p q s d", q=SUB, s=T),
                               ACT.Copy).then_inc(stored, 1)

            act.wait_ge(consts, 1)
            std_of(0, 0)
            std_of(1, 1)
            act.wait_ge(weights_in, 16 * 5)
            for n in range(3):
                front(n, n % 2)
            with act.Fori(0, 5) as i:
                front(2 * i + 3, 1)
                front(2 * i + 4, 0)
            for i in range(5):
                table(i, 0, key_t)
                front(13 + i, (13 + i) % 2)
                table(i, P, low_t)
            front(18, 0)
            act.wait_ge(cnt_out, 16)
            act.wait_ge(fold_stored, 16)
            act.wait_ge(bias_stored, 16)
            act.wait_ge(total_done, 1)
            act.wait_ge(rt_ready, 1)
            for n in range(EARLY, T + 2):
                front(n, n % 2)
                for g in EARLY_GROUPS[n]:
                    store_counts(g, g)

            def squares(k, n, j):
                act.wait_ge(o_ready[k], n + 1)
                act.activation(ps[0:TN, j % 2, 0:C], last_o if k == 1 and is_last(n) else o_t[:, j, :], ACT.Square,
                               accum_out=ss[:, j:j + 1]).then_inc(sq_done[k], 1)

            def norms(k, ch, tiles):
                act.wait_ge(sq_done[k], CT * ch + tiles)
                act.activation(nrm[:, 0:tiles], ss[:, 0:tiles], ACT.Sqrt).then_inc(nrm_ready[k], 1)

            def half_high(n, par, stores):
                if not isinstance(n, int) or n >= 2:
                    act.wait_ge(y_half_stored[par], 16 * stores)
                high(1, n, y_half[:, par, 0:C])

            def chunk(ch, groups, nexts):
                for j in range(CT):
                    for t in range(T):
                        s = T * j + t
                        if s % SUB == 0 and s // SUB < groups:
                            store_counts(GC * ch + LEAD + s // SUB, LEAD + s // SUB)
                        if t == 7 and j > 0:
                            squares(0, CT * ch + j - 1, j - 1)
                        if t == 7 and j == 0 and nexts:
                            squares(0, CT * ch - 1, CT - 1)
                            norms(0, ch - 1, CT)
                        if nexts and t == TURN_AT:
                            turned_x(1, CT * (ch - 1) + j, j % 2)
                        if nexts and t == PROJECT_AT:
                            projected(1, CT * (ch - 1) + j, j % 2)
                        if nexts and t == WL_AT:
                            half_high(CT * (ch - 1) + j, j % 2, 2 * (ch - 1) + j // 2)

            chunk(0, GC, False)
            act.wait_ge(xr_done[0], T)
            act.wait_ge(w2_in, 16 * 5)
            chunk(1, GC, True)
            with act.Fori(2, CH - 1) as ch:
                chunk(ch, GC, True)
            chunk(CH - 1, GROUPS - GC * (CH - 1) - LEAD, True)
            squares(0, CT * CH - 1, CT - 1)
            norms(0, CH - 1, CT)
            for p in range(CT + 2):
                n = CT * (CH - 1) + p
                if p < CT:
                    turned_x(1, n, p % 2)
                if 2 <= p:
                    half_high(n - 2, p % 2, (n - 2) // 2)
                if 1 <= p <= CT:
                    projected(1, n - 1, (p - 1) % 2)
                if p == 3:
                    squares(0, LAST, 0)
                    norms(0, CH, 1)
            turned_x(1, LAST, 0)
            projected(1, LAST, 0)
            act.wait_ge(agg_done[0], T)
            high(1, LAST, y[0:TN, LAST, 0:C])

            def stds(t0, t1, done):
                act.wait_ge(var2_ready, done)
                act.activation(std2[:, t0:t1], var2[:, t0:t1], ACT.Sqrt).then_inc(std2_ready, 1)

            def chunk_2(ch, first=False):
                for j in range(CT):
                    if j > 0:
                        squares(1, CT * ch + j - 1, j - 1)
                    elif not first:
                        squares(1, CT * ch - 1, CT - 1)
                        norms(1, ch - 1, CT)

            chunk_2(0, True)
            with act.Fori(1, CH) as ch:
                chunk_2(ch)
            stds(0, CT * (CH - 1), 1)
            squares(1, CT * CH - 1, CT - 1)
            norms(1, CH - 1, CT)
            squares(1, LAST, 0)
            norms(1, CH, 1)

            def f_turned(t, j):
                act.wait_ge(f_xt_done, t + 1)
                if not isinstance(t, int) or t >= R:
                    act.wait_ge(lg_done, t - R + 1)
                act.activation(f_xT[:, j].rearrange("p k n -> p (k n)"), ps[:, 5, 0:KC * TN], ACT.Copy).then_inc(f_xT_ready, 1)

            def exps(t, j):
                act.wait_ge(sub_ready, t + 1)
                act.activation(f_e[:, j, :], f_e[:, j, :], ACT.Exp).then_inc(exp_ready, 1)

            def row_highs(t, j):
                act.wait_ge(f_xn_ready, t + 1)
                if not isinstance(t, int) or t >= R:
                    act.wait_ge(s_done, t - R + 1)
                act.activation(f_xh[:, j, 0:C + 1], f_xn[:, j, 0:C + 1], ACT.Copy).then_inc(xh_ready, 1)

            def weight_highs(t, j):
                act.wait_ge(fw_ready, t + 1)
                if not isinstance(t, int) or t >= R:
                    act.wait_ge(wT_done, t - R + 1)
                act.activation(f_wh[:, j, :], f_w[:, j, :], ACT.Copy).then_inc(wh_ready, 1)

            def w_turned(t):
                act.wait_ge(wT_done, t + 1)
                act.activation(w_tr[:, :, bass.ds(TN * t, TN)], wt16[:, :, 0:TN], ACT.Copy).then_inc(wT_ready, 1)

            def slice_pass(p, j):
                if not isinstance(p, int) or p < T:
                    f_turned(p, j)
                    row_highs(p, j)
                if not isinstance(p, int) or 2 <= p <= T + 1:
                    weight_highs(p - 2, (j - 2) % R)
                if not isinstance(p, int) or 1 <= p <= T:
                    exps(p - 1, (j - 1) % R)
                if not isinstance(p, int) or p >= 3:
                    w_turned(p - 3)

            act.wait_ge(f_ones, 1)
            slice_pass(0, 0)
            stds(CT * (CH - 1), T, 2)
            for p in range(1, 2 * R):
                slice_pass(p, p % R)
            with act.Fori(2, CH) as i:
                for j in range(R):
                    slice_pass(R * i + j, j)
            for p in range(CH * R, T + 3):
                slice_pass(p, p % R)

            act.wait_ge(mid_pe, 1)
            act.activation(sT[:, 0, :], ps[:, 4, :], ACT.Copy).then_inc(mid_act, 1)
            act.wait_ge(mid_pe, 3)
            act.activation(qT, ps[0:D, 4, :], ACT.Copy).then_inc(mid_act, 1)
            act.wait_ge(mid_pe, 5)
            act.activation(v_sb, ps[0:G, 6, :], ACT.Copy).then_inc(mid_act, 1)
            act.wait_ge(mid_dve, 5)
            act.activation(a_e.rearrange("p h g -> p (h g)"), a_e.rearrange("p h g -> p (h g)"), ACT.Exp, scale=SCALE).then_inc(mid_act, 1)
            act.wait_ge(mid_pe, 9)
            act.activation(t_half[:, 0, 2:4, :].rearrange("p k c -> p (k c)"), ps[:, 7, :], ACT.Copy).then_inc(mid_act, 1)

        @block.vector
        def _(dve):
            c = Chain(dve, dve_steps)

            def later(n, m):
                return not isinstance(n, int) or n >= m

            def row_stats_x(n, par, loads):
                dve.wait_ge(x_loaded[par], 16 * loads)
                if later(n, 2):
                    dve.wait_ge(xn_ready, n - 1)
                if later(n, 1):
                    dve.wait_ge(mv_ready, n)
                c.link(dve.bn_stats(st6, x_in[:, par, :]))

            def row_moments(n, par):
                dve.bn_aggr(mv[:, par, :], st6).then_inc(mv_ready, 1)

            def norm_x(n, par):
                dve.wait_ge(std_ready, n + 1)
                if later(n, 1):
                    dve.wait_ge(xn_ready, n)
                c.link(dve.reciprocal(rstd, std[:, par:par + 1]))
                if later(n, 2):
                    dve.wait_ge(x_turned[0], n - 1)
                dve.tensor_scalar(xn[:, par, :], x_in[:, par, :], mv[:, par, 0:1], rstd, ALU.subtract, ALU.mult).then_inc(xn_ready, 1)

            def low(k, n, half):
                dve.wait_ge(hi_ready[k], n + 1)
                dve.tensor_tensor(half[:, C:2 * C], ps[0:TN, 6, 0:C], half[:, 0:C], ALU.subtract).then_inc(lo_ready[k], 1)

            def add_bias(k, n, par, stores):
                dve.wait_ge(xr_done[k], n + 1)
                if later(n, 2):
                    dve.wait_ge(xr_stored[k][par], 16 * stores)
                dve.tensor_tensor(xr_o[:, par, :], ps[0:TN, 7, 0:C], bias_l[0:TN, :], ALU.add).then_inc(xr_ready[k], 1)

            def front(n, par, loads):
                if not isinstance(n, int) or n + 1 < T:
                    norm_x(n + 1, 1 - par)
                if not isinstance(n, int) or n + 2 < T:
                    row_stats_x(n + 2, par, loads)
                if later(n, 2):
                    low(0, n - 2, y[0:TN, bass.ds(n - 2, 1), :].rearrange("p a c -> p (a c)"))
                if not isinstance(n, int) or n + 2 < T:
                    row_moments(n + 2, par)
                if not isinstance(n, int) or 1 <= n <= T:
                    add_bias(0, n - 1, 1 - par, loads - 3 + par)

            def one_hots(g, q):
                q %= GC
                if later(g, OH_AGE[q]):
                    dve.wait_ge(built, g - OH_AGE[q] + 1)
                pairs = slice(OH_SLOT[q] * 2, OH_SLOT[q] * 2 + 2)
                tile0 = g * SUB
                to = [P, 2, P, 2], [P, 2, KEYS, 2]
                one = [tab[:, bass.ds(tile0, SUB)].rearrange("p (a k) -> p a k", k=2).unsqueeze(2).to_broadcast(shape)
                       for tab, shape in zip((low_t, key_t), to)]
                dve.tensor_tensor(oh_low[:, pairs], iota_low.unsqueeze(1).to_broadcast(to[0]), one[0], ALU.is_equal)
                dve.tensor_tensor(oh_key[:, pairs], iota_key.unsqueeze(1).to_broadcast(to[1]), one[1], ALU.is_equal).then_inc(oh_ready, 1)

            row_stats_x(0, 0, 1)
            row_moments(0, 0)
            dve.wait_ge(consts, 2)
            dve.wait_ge(rows_in, 16)
            c.link(dve.tensor_copy(rowmax, rows[:, ROW - 1:ROW]))
            dve.tensor_scalar(step, thr, rowmax, None, ALU.is_gt).then_inc(step_ready, 1)
            norm_x(0, 0)
            dve.wait_ge(r0_done, 1)
            c.link(dve.tensor_scalar(r0, ps[0:TN, 3, 0:1], float(TN - 1), None, ALU.min))
            dve.tensor_copy(r0_i, r0).then_inc(r0_ready, 1)
            row_stats_x(1, 1, 1)
            row_moments(1, 1)
            front(0, 0, 2)
            dve.wait_ge(weights_in, 16 * 5)
            front(1, 1, 2)
            dve.wait_ge(consts, 4)
            dve.wait_ge(row_in, 16)
            c.link(dve.tensor_copy(picked_f, picked))
            c.link(dve.tensor_scalar(junk[:, 0:ROW], picked_f, own[:, 0:1], None, ALU.is_lt, ALU.add, accum_out=below))
            c.link(dve.scalar_tensor_tensor(out=start, in0=r0, scalar=float(ROW), in1=below, op0=ALU.mult, op1=ALU.add))
            c.link(dve.tensor_scalar(start_c, start, float(E - COARSE), None, ALU.min))
            dve.tensor_copy(start_i, start_c).then_inc(start_ready, 1)
            front(2, 0, 3)
            front(3, 1, 3)
            dve.wait_ge(fold_in, 16 * 5)
            c.link(dve.tensor_scalar(rtemp, temp, 0.1, 5.0, ALU.max, ALU.min))
            c.link(dve.reciprocal(rtemp, rtemp))
            dve.tensor_copy(rtemp_row, rtemp.unsqueeze(2).to_broadcast([1, H, G])).then_inc(rt_row, 1)
            dve.wait_ge(coarse_in, 16)
            c.link(dve.tensor_copy(coarse_f, coarse))
            for i in range(2):
                last = dve.tensor_scalar(junk5[:, i], coarse_f, base5[:, i:i + 1], None, ALU.is_lt, ALU.add,
                                         accum_out=below5[:, i:i + 1])
            front(4, 0, 4)
            for i in range(2, 5):
                last = dve.tensor_scalar(junk5[:, i], coarse_f, base5[:, i:i + 1], None, ALU.is_lt, ALU.add,
                                         accum_out=below5[:, i:i + 1])
            c.link(last)
            c.link(dve.tensor_scalar(start5, below5, start_c, float(E - WIN), ALU.add, ALU.min))
            dve.tensor_copy(start5_i[:, :, 0], start5).then_inc(fine_ready, 1)
            front(5, 1, 4)
            dve.wait_ge(fold_done, 1)
            dve.wait_ge(rt_done, 1)
            dve.tensor_copy(rtemp_all, ps[:, 3, :]).then_inc(rt_ready, 1)
            dve.wait_ge(rt_ready, 1)
            for kc in range(KC):
                last = dve.tensor_tensor(wxs_o[:, kc, :], ps[:, kc, :], rtemp_all, ALU.mult)
            last.then_inc(fold_ready, 1)
            c.link(dve.tensor_tensor(bxs_t, ps[0:1, 2, :].rearrange("p (h g) -> p h g", h=H),
                                     bsl.unsqueeze(1).to_broadcast([1, H, G]), ALU.add))
            dve.tensor_tensor(bxs_o, bxs_t, rtemp_row, ALU.mult).then_inc(fold_ready, 1)
            with dve.Fori(0, 2) as i:
                c.loop(i, 4)
                front(2 * i + 6, 0, i + 5)
                front(2 * i + 7, 1, i + 5)
            c.end(2)
            for i in range(5):
                dve.wait_ge(win_in[i], 32)
            dve.tensor_scalar(hi_i, win_s, 1.0 / TN, -0.496, ALU.mult, ALU.add)
            c.link(dve.tensor_copy(win_f, win_d))
            dve.scalar_tensor_tensor(out=low_f, in0=hi_i, scalar=-float(TN), in1=win_s, op0=ALU.mult, op1=ALU.add)
            c.link(dve.tensor_tensor(dl, win_f, base5.unsqueeze(2).to_broadcast([TN, 5, WIN]), ALU.subtract))
            front(10, 0, 7)
            dve.tensor_scalar(ge0, dl, 0.0, None, ALU.is_ge)
            c.link(dve.scalar_tensor_tensor(out=pair_f, in0=hi_i, scalar=float(D5), in1=dl, op0=ALU.mult, op1=ALU.add))
            c.link(dve.scalar_tensor_tensor(out=valid, in0=dl, scalar=float(D5), in1=ge0, op0=ALU.is_lt, op1=ALU.mult))
            dve.scalar_tensor_tensor(out=key_f, in0=pair_f, scalar=1.0, in1=valid, op0=ALU.add, op1=ALU.mult).then_inc(keys_ready, 1)
            for i in range(5):
                front(11 + i, (11 + i) % 2, (13 + i) // 2 + 1)
                for d in range(D5):
                    col = D5 * i + d
                    last = dve.tensor_scalar(junk25[:, col, :], win_f[:, i], own[:, col:col + 1], None, ALU.is_equal, ALU.add,
                                             accum_out=cnt[:, col:col + 1])
            c.link(last)
            dve.tensor_reduce(cnt_row, cnt, AX_X, ALU.add).then_inc(cnt_rows_ready, 1)
            for n in range(16, EARLY):
                front(n, n % 2, (n + 2) // 2 + 1)
            dve.wait_ge(total_done, 1)
            dve.tensor_scalar(covered[0:1, 0:1], ps[0:1, 3, 0:1], float(E), None, ALU.is_equal).then_inc(covered_ready, 1)
            dve.wait_ge(consts, 5)
            dve.wait_ge(tables_ready, 10)
            for n in range(EARLY, T + 2):
                for g in EARLY_GROUPS[n]:
                    one_hots(g, g)
                front(n, n % 2, (n + 2) // 2 + 1)
                if n == EARLY + 4:
                    dve.wait_ge(cnt_in, 16)
                    c.link(dve.tensor_scalar(rcnt[0:TN, :], rcnt[0:TN, :], 1.0, None, ALU.max))
                    dve.reciprocal(rcnt[0:TN, :], rcnt[0:TN, :]).then_inc(rcnt_ready, 1)
                    dve.wait_ge(rcnt_ready, 1)
                    is_covered = dve.value_load(covered[0:1, 0:1], min_val=0, max_val=1)

            def general_one_hots(k):
                def sweep(s_):
                    chunk, rel = (T // GT) * k + s_, (T // GT + 1) * k + s_

                    def group(i, slot):
                        kk = RG * i + slot
                        dve.wait_ge(g_rel_ready, rel + 1)
                        dve.wait_ge(g_free, ROW * chunk + kk + 1)
                        dve.tensor_scalar(g_oh[:, slot, :], g_iota, g_rel[:, bass.ds(kk, 1)], None, ALU.is_equal).then_inc(g_oh_ready, 1)

                    with dve.Fori(0, ROUNDS) as i:
                        for slot in range(RG):
                            group(i, slot)
                    dve.wait_ge(g_oh_ready, ROW * chunk + ROW)
                    dve.tensor_scalar(g_rel, g_rel, -float(GT * TN), None, ALU.add).then_inc(g_rel_ready, 1)
                    dve.wait_ge(g_swept, chunk + 1)
                    if not isinstance(chunk, int) or chunk > 0:
                        dve.wait_ge(g_sum_out, 16 * chunk)
                    dve.tensor_copy(g_sum, ps[0:TN, 0:GT, :]).then_inc(g_sum_ready, 1)

                if k:
                    dve.wait_ge(g_rel_ready, T // GT + 1)
                    dve.wait_ge(stored, GROUPS)
                    dve.wait_ge(g_tables_in, 64)
                    dve.tensor_copy(g_dst, g_dst_i).then_inc(g_dst_ready, 1)
                    dve.wait_ge(g_dst_ready, 1)
                    dve.wait_ge(g_iota_ready, 2)
                dve.tensor_copy(g_rel, g_dst).then_inc(g_rel_ready, 1)
                sweep(0)
                with dve.Fori(1, T // GT) as s_:
                    sweep(s_)

            with dve.If(is_covered == 1):
                dve.nop()
            with dve.Else():
                g = Chain(dve, g_steps)
                dve.wait_ge(g_tables_in, 32)
                g.link(dve.tensor_copy(g_dst, g_dst_i))
                dve.wait_ge(g_node_ready, 1)
                g.link(dve.memset(g_cnt, 0.0))
                with dve.Fori(0, E // N) as s_:
                    g.loop(s_, T + 1)
                    dve.wait_ge(g_all_in, 16 * s_ + 16)
                    dve.tensor_copy(g_all, g_all_i).then_inc(g_all_used, 1)
                    dve.wait_ge(g_all_used, s_ + 1)
                    for t in range(T):
                        g.link(dve.tensor_scalar(g_eq, g_all, g_node[:, t:t + 1], None, ALU.is_equal, ALU.add,
                                                 accum_out=g_part[:, t:t + 1]))
                    g.link(dve.tensor_tensor(g_cnt, g_cnt, g_part, ALU.add))
                g.end(E // N)
                g.link(dve.tensor_scalar(g_cnt, g_cnt, 1.0, None, ALU.max))
                g.link(dve.reciprocal(rcnt[0:TN, :], g_cnt))
                dve.wait_ge(g_iota_ready, 1)
                general_one_hots(0)
            dve.nop()

            def combine(k, ch, j, n):
                dve.wait_ge(agg_done[k], n + 1)
                o = o_t[:, j, :]
                if k == 1 and is_last(n):
                    o = last_o
                    dve.wait_ge(last_in, 32)
                else:
                    dve.wait_ge(xr_loaded[k][j], 16 * (ch + 1))
                for half in range(KC):
                    last = dve.scalar_tensor_tensor(out=o, in0=ps[0:TN, j % 2, half * C:(half + 1) * C],
                                                    scalar=rcnt[0:TN, bass.ds(n, 1)], in1=o,
                                                    op0=ALU.mult, op1=ALU.add)
                    if half == 0:
                        c.link(last)
                last.then_inc(o_ready[k], 1)

            def finish(k, ch, tiles):
                dve.wait_ge(nrm_ready[k], ch + 1)
                c.link(dve.tensor_scalar(nrm[:, 0:tiles], nrm[:, 0:tiles], EPS_NORM, None, ALU.max))
                c.link(dve.reciprocal(inv[:, 0:tiles], nrm[:, 0:tiles]))
                if k == 1 and tiles == 1:
                    dve.scalar_tensor_tensor(out=last_o, in0=last_o, scalar=inv[:, 0:1], in1=last_res,
                                             op0=ALU.mult, op1=ALU.add).then_inc(x1_ready, 1)
                    dve.wait_ge(x1_ready, T)
                    dve.bn_stats(stats2[0:TN, LAST, :], last_o).then_inc(stats2_ready, 1)
                    return
                for j in range(tiles):
                    if k == 0:
                        dve.tensor_scalar(o_t[:, j, :], o_t[:, j, :], inv[:, j:j + 1], 0.0, ALU.mult, ALU.max).then_inc(h_ready, 1)
                    else:
                        dve.wait_ge(res_loaded[j], 16 * (ch + 1))
                        dve.scalar_tensor_tensor(out=o_t[:, j, :], in0=o_t[:, j, :], scalar=inv[:, j:j + 1], in1=x_res[:, j, :],
                                                 op0=ALU.mult, op1=ALU.add).then_inc(x1_ready, 1)
                        if j > 0:
                            row_stats(ch, j - 1)
                if k == 1:
                    row_stats(ch, tiles - 1)

            def row_stats(ch, j):
                dve.wait_ge(x1_ready, CT * ch + j + 1)
                dve.bn_stats(stats2[0:TN, bass.ds(CT * ch + j, 1), :].rearrange("p a b -> p (a b)"),
                             o_t[:, j, :]).then_inc(stats2_ready, 1)

            def chunk(ch, groups, nexts):
                for j in range(CT):
                    for t in range(T):
                        s = T * j + t
                        if s % SUB == 0 and s // SUB < groups:
                            one_hots(GC * ch + LEAD + s // SUB, LEAD + s // SUB)
                        before = CT * (ch - 1) + j - 1
                        if nexts and t == 3 and (j > 0 or later(ch, 2)):
                            add_bias(1, before, (j - 1) % 2, 2 * (ch - 1) + (j - 1) // 2)
                        if nexts and t == 9 and (j > 0 or later(ch, 2)):
                            low(1, before, y_half[:, (j - 1) % 2, :])
                        if t == 11 and j > 0:
                            combine(0, ch, j - 1, CT * ch + j - 1)
                        if t == 11 and j == 0 and nexts:
                            combine(0, ch - 1, CT - 1, CT * ch - 1)
                        if t == 17 and j == 0 and nexts:
                            finish(0, ch - 1, CT)

            chunk(0, GC, False)
            dve.wait_ge(xr_stored[0][0], 16 * (T // 2 + 1))
            dve.wait_ge(xr_stored[0][1], 16 * (T // 2))
            dve.wait_ge(w2_in, 16 * 5)
            chunk(1, GC, True)
            with dve.Fori(2, CH - 1) as ch:
                c.loop(ch - 2, CT + 2)
                chunk(ch, GC, True)
            c.end(CH - 3)
            chunk(CH - 1, GROUPS - GC * (CH - 1) - LEAD, True)
            combine(0, CH - 1, CT - 1, CT * CH - 1)
            add_bias(1, CT * (CH - 1) - 1, 1, CT * (CH - 1) // 2 - 1)
            low(1, CT * (CH - 1) - 1, y_half[:, 1, :])
            finish(0, CH - 1, CT)
            for p in range(1, CT + 2):
                n = CT * (CH - 1) + p
                if p == CT:
                    finish(0, CH, 1)
                if 2 <= p:
                    low(1, n - 2, y_half[:, p % 2, :])
                if p <= CT:
                    add_bias(1, n - 1, (p - 1) % 2, (n - 1) // 2)
                if p == 3:
                    combine(0, CH, 0, LAST)
            add_bias(1, LAST, 0, LAST // 2)
            low(1, LAST, y[0:TN, LAST, :])

            def moments(t0, t1):
                dve.wait_ge(stats2_ready, t1)
                s2 = stats2[0:TN, t0:t1]
                mean, half, var = mean2[:, t0:t1], half2[:, t0:t1], var2[:, t0:t1]
                c.link(dve.tensor_tensor(mean, s2[:, :, 1], s2[:, :, 4], ALU.add))
                c.link(dve.tensor_tensor(half, s2[:, :, 1], s2[:, :, 4], ALU.subtract))
                c.link(dve.tensor_tensor(var, s2[:, :, 2], s2[:, :, 5], ALU.add))
                c.link(dve.tensor_scalar(mean, mean, 0.5, None, ALU.mult))
                c.link(dve.tensor_tensor(half, half, half, ALU.mult))
                c.link(dve.tensor_scalar(var, var, 1.0 / C, EPS_LN, ALU.mult, ALU.add))
                dve.scalar_tensor_tensor(out=var, in0=half, scalar=0.25, in1=var, op0=ALU.mult, op1=ALU.add).then_inc(var2_ready, 1)

            def inverses(t0, t1, done):
                dve.wait_ge(std2_ready, done)
                c.link(dve.reciprocal(rstd2[:, t0:t1], std2[:, t0:t1]))

            with dve.If(is_covered == 1):
                dve.nop()
            with dve.Else():
                general_one_hots(1)
            dve.nop()

            def chunk_2(ch, first=False):
                for j in range(CT):
                    if j > 0:
                        combine(1, ch, j - 1, CT * ch + j - 1)
                    elif not first:
                        combine(1, ch - 1, CT - 1, CT * ch - 1)
                        finish(1, ch - 1, CT)

            chunk_2(0, True)
            with dve.Fori(1, CH) as ch:
                c.loop(ch - 1, CT + 2)
                chunk_2(ch)
            c.end(CH - 1)
            moments(0, CT * (CH - 1))
            combine(1, CH - 1, CT - 1, CT * CH - 1)
            inverses(0, CT * (CH - 1), 1)
            finish(1, CH - 1, CT)
            combine(1, CH, 0, LAST)
            finish(1, CH, 1)

            def normed(t, j, first, loads):
                dve.wait_ge(f_loaded[j], 16 * loads)
                if not first:
                    dve.wait_ge(xl_ready, t - R + 1)
                    dve.wait_ge(f_xt_done, t - R + 1)
                dve.tensor_scalar(f_xn[:, j, 0:C], f_in[:, j, :], mean2[:, bass.ds(t, 1)],
                                  rstd2[:, bass.ds(t, 1)], ALU.subtract, ALU.mult).then_inc(f_xn_ready, 1)

            def softmax(t, j, first):
                bank = ps[0:TN, 4 if j % 2 == 0 else 7, :].rearrange("p (h g) -> p h g", h=H)
                e = f_e[:, j, :].rearrange("p (h g) -> p h g", h=H)
                dve.wait_ge(lg_done, t + 1)
                c.link(dve.tensor_reduce(f_mx[:, j, :], bank, AX_X, ALU.max))
                if not first:
                    dve.wait_ge(fw_ready, t - R + 1)
                dve.tensor_tensor(e, bank, f_mx[:, j, :].unsqueeze(2).to_broadcast([TN, H, G]), ALU.subtract).then_inc(sub_ready, 1)

            def sums(t, j):
                e = f_e[:, j, :].rearrange("p (h g) -> p h g", h=H)
                dve.wait_ge(exp_ready, t + 1)
                c.link(dve.tensor_reduce(f_sm[:, j, :], e, AX_X, ALU.add))
                c.link(dve.tensor_scalar(f_ss[:, j, :], f_sm[:, j, :], 1.0 / W_SCALE, None, ALU.mult))
                dve.reciprocal(f_rs[:, j, :], f_ss[:, j, :]).then_inc(rs_ready, 1)

            normed(0, 0, True, 1)
            normed(1, 1, True, 1)
            moments(CT * (CH - 1), T)
            inverses(CT * (CH - 1), T, 2)

            def tile(t, j, ch):
                softmax(t, j, isinstance(t, int) and t < R)
                if not isinstance(t, int) or t + 2 < T:
                    normed(t + 2, (j + 2) % R, isinstance(t, int) and t + 2 < R, ch + 1 + (j + 2) // R)
                sums(t, j)

            for t in range(R):
                tile(t, t, 0)
            with dve.Fori(1, CH - 1) as i:
                c.loop(i - 1, 3 * R)
                for j in range(R):
                    tile(R * i + j, j, i)
            c.end(CH - 2)
            for t in range(R * (CH - 1), T):
                tile(t, t % R, t // R)

            dve.wait_ge(s_done, T)
            c.link(dve.tensor_scalar(sn_e, ps[:, 0:PAIRS, C], EPS_SLICE * W_SCALE, None, ALU.add))
            c.link(dve.reciprocal(sn_inv, sn_e))
            for k in range(PAIRS):
                last = dve.tensor_scalar(s_sb[:, k, 0:C + 1], ps[:, k, 0:C + 1], sn_inv[:, k:k + 1], None, ALU.mult)
            last.then_inc(mid_dve, 1)
            dve.wait_ge(mid_pe, 1)
            dve.tensor_copy(sT[:, 1, :], ps[:, 5, :])
            dve.tensor_copy(nr, ps[0:1, 6, :]).then_inc(mid_dve, 1)
            dve.wait_ge(mid_pe, 2)
            dve.tensor_copy(tokT, ps[0:D, 7, :]).then_inc(mid_dve, 1)
            dve.wait_ge(mid_pe, 4)
            dve.tensor_copy(kT, ps[0:D, 5, :]).then_inc(mid_dve, 1)
            dve.wait_ge(mid_pe, 6)
            sc = ps[0:G, 7, :].rearrange("p (h g) -> p h g", h=H)
            c.link(dve.tensor_reduce(am, sc, AX_X, ALU.max))
            dve.tensor_tensor(a_e, sc, am.unsqueeze(2).to_broadcast([G, H, G]), ALU.subtract).then_inc(mid_dve, 1)
            dve.wait_ge(mid_act, 4)
            c.link(dve.tensor_reduce(a_s, a_e, AX_X, ALU.add))
            c.link(dve.reciprocal(a_r, a_s))
            dve.tensor_tensor(a_w, a_e, a_r.unsqueeze(2).to_broadcast([G, H, G]), ALU.mult).then_inc(mid_dve, 1)
            dve.wait_ge(mid_pe, 7)
            dve.tensor_copy(aT, ps[0:G, 4, :]).then_inc(mid_dve, 1)
            dve.wait_ge(mid_pe, 8)
            dve.tensor_copy(osT, ps[0:D, 5, :]).then_inc(mid_dve, 1)
            dve.wait_ge(mid_pe, 9)
            for b in range(2):
                high, low = (t_half[:, half, 2 * b:2 * b + 2, :].rearrange("p k c -> p (k c)") for half in range(2))
                if b == 0:
                    c.link(dve.tensor_copy(high, ps[:, 6 + b, :]))
                else:
                    dve.wait_ge(mid_act, 5)
                dve.tensor_tensor(low, ps[:, 6 + b, :], high, ALU.subtract).then_inc(mid_dve, 1)

            def finish(t, j, ch):
                dve.wait_ge(out_done, t + 1)
                dve.wait_ge(f_loaded[j], 16 * (CH + (j == 0) + ch + 1))
                if not isinstance(t, int) or t >= R:
                    dve.wait_ge(out_stored[j], 16 * ch)
                dve.scalar_tensor_tensor(out=y_o[:, j, :], in0=ps[0:TN, j, 0:C], scalar=1.0 / W_SCALE, in1=y_in[:, j, :],
                                         op0=ALU.mult, op1=ALU.add).then_inc(out_ready, 1)

            for j in range(R):
                finish(j, j, 0)
            with dve.Fori(1, CH) as i:
                for j in range(R):
                    finish(R * i + j, j, i)
            finish(LAST, 0, CH)


def kernel(**inputs):
    import numpy as np
    import concourse.bacc as bacc
    from concourse.bass_utils import run_bass_kernel_spmd as run

    nc = bacc.Bacc("TRN2", target_bir_lowering=False, num_devices=1)
    arrays, args = {}, {}

    def give(name, a):
        a = np.ascontiguousarray(a)
        arrays[f"in_{name}"] = a
        args[name] = nc.dram_tensor(f"in_{name}", a.shape, mybir.dt.from_np(a.dtype), kind="ExternalInput").ap()

    for name in ("x", "src", "dst"):
        give(name, inputs[name])
    for name in ("W_proj1", "b_proj1", "W_l1", "b_l1", "W_r1", "W_proj2", "b_proj2", "W_l2", "b_l2", "W_r2"):
        give(name.replace("W_proj", "Wp").replace("b_proj", "bp").replace("W_l", "Wl").replace("b_l", "bl").replace("W_r", "Wr"),
             inputs["L0_gnn_" + name])
    for name in ("W_fx", "b_fx", "W_slice", "b_slice", "W_q", "W_k", "W_v", "W_out", "b_out", "temperature"):
        give(name, inputs["L0_ffn_" + name])
    wx, bx = np.asarray(inputs["L0_ffn_W_x"]), np.asarray(inputs["L0_ffn_b_x"])
    heads = inputs["L0_ffn_temperature"].shape[1]
    give("W_xT", wx.reshape(wx.shape[0], heads, -1).transpose(2, 1, 0))
    give("b_xT", bx.reshape(heads, -1).T)
    out = nc.dram_tensor("out_0", inputs["x"].shape, F32, kind="ExternalOutput").ap()
    bass_gnn_ffn_kernel(nc, out=out, **args)
    r = run(nc, [arrays], core_ids=[0])
    return r.results[0]["out_0"]
```
